# Optimizing a Trainium2 kernel written in Bass

```python
import numpy as np
import jax
import jax.numpy as jnp

def _softmax(x, axis=-1):
    return jax.nn.softmax(x, axis=axis)

def _gelu(x):
    return jax.nn.gelu(x, approximate=True)

def _silu(x):
    return jax.nn.silu(x)

def _sigmoid(x):
    return jax.nn.sigmoid(x)

def _layernorm(x, axis=-1, eps=1e-05):
    m = jnp.mean(x, axis=axis, keepdims=True)
    v = jnp.var(x, axis=axis, keepdims=True)
    return (x - m) / jnp.sqrt(v + eps)

def _scatter_add(tgt, idx, src, axis=0):
    return tgt.at[idx].add(src)

def _segment_sum(src, seg, n):
    return jax.ops.segment_sum(src, seg, n)
kernel_name = 'mk_sandwich_d1_jaxref_r8_c62636'

def setup_inputs(seed: int=0):
    np.random.seed(seed)
    _w = jnp.asarray

    def _L0_attn_setup():
        import jax, jax.numpy as jnp
        import numpy as np
        EMBED_DIM = 128
        NUM_HEADS = 16
        HEAD_DIM = EMBED_DIM // NUM_HEADS
        SEQ_LEN = 128
        BATCH = 4
        MAX_REL_POS = 2

        def _rel_index(length_q, length_k):
            q = jnp.arange(length_q)[:, None]
            k = jnp.arange(length_k)[None, :]
            return jnp.clip(k - q, -MAX_REL_POS, MAX_REL_POS) + MAX_REL_POS
        key = jax.random.key(seed)
        ks = jax.random.split(key, 12)
        s = 1.0 / np.sqrt(EMBED_DIM)
        x = jax.random.normal(ks[0], (BATCH, SEQ_LEN, EMBED_DIM), dtype=jnp.float32)
        W_q = jax.random.normal(ks[1], (EMBED_DIM, EMBED_DIM), dtype=jnp.float32) * s
        b_q = jnp.zeros((EMBED_DIM,), dtype=jnp.float32)
        W_k = jax.random.normal(ks[2], (EMBED_DIM, EMBED_DIM), dtype=jnp.float32) * s
        b_k = jnp.zeros((EMBED_DIM,), dtype=jnp.float32)
        W_v = jax.random.normal(ks[3], (EMBED_DIM, EMBED_DIM), dtype=jnp.float32) * s
        b_v = jnp.zeros((EMBED_DIM,), dtype=jnp.float32)
        W_o = jax.random.normal(ks[4], (EMBED_DIM, EMBED_DIM), dtype=jnp.float32) * s
        b_o = jnp.zeros((EMBED_DIM,), dtype=jnp.float32)
        lim = float(np.sqrt(6.0 / (2 * MAX_REL_POS + 1 + HEAD_DIM)))
        rel_k_table = jax.random.uniform(ks[5], (2 * MAX_REL_POS + 1, HEAD_DIM), jnp.float32, -lim, lim)
        rel_v_table = jax.random.uniform(ks[6], (2 * MAX_REL_POS + 1, HEAD_DIM), jnp.float32, -lim, lim)
        return {'x': x, 'W_q': W_q, 'b_q': b_q, 'W_k': W_k, 'b_k': b_k, 'W_v': W_v, 'b_v': b_v, 'W_o': W_o, 'b_o': b_o, 'rel_k_table': rel_k_table, 'rel_v_table': rel_v_table}
    _L0_attn_in = _L0_attn_setup()

    def _L0_ffn_setup():
        import jax, jax.numpy as jnp
        import numpy as np
        D_MODEL = 128
        H_SHARED = 256
        H_ROUTED = 128
        N_EXPERTS = 8
        TOP_K = 2
        key = jax.random.key(seed)
        ks = jax.random.split(key, 8)
        B, T = (2, 256)
        sc_d = 1.0 / np.sqrt(D_MODEL)
        sc_hs = 1.0 / np.sqrt(H_SHARED)
        sc_hr = 1.0 / np.sqrt(H_ROUTED)
        return {'x': jax.random.normal(ks[0], (B, T, D_MODEL), dtype=jnp.float32), 'router_w': jax.random.normal(ks[1], (N_EXPERTS, D_MODEL), dtype=jnp.float32) * sc_d, 'router_bias': jnp.zeros((N_EXPERTS,), dtype=jnp.float32), 'sw1': jax.random.normal(ks[2], (D_MODEL, H_SHARED), dtype=jnp.float32) * sc_d, 'sw3': jax.random.normal(ks[3], (D_MODEL, H_SHARED), dtype=jnp.float32) * sc_d, 'sw2': jax.random.normal(ks[4], (H_SHARED, D_MODEL), dtype=jnp.float32) * sc_hs, 'ew1': jax.random.normal(ks[5], (N_EXPERTS, D_MODEL, H_ROUTED), dtype=jnp.float32) * sc_d, 'ew2': jax.random.normal(ks[6], (N_EXPERTS, H_ROUTED, D_MODEL), dtype=jnp.float32) * sc_hr}
    _L0_ffn_in = _L0_ffn_setup()
    _d = {'L0_attn_x': _L0_attn_in['x'], 'L0_attn_W_q': _L0_attn_in['W_q'], 'L0_attn_b_q': _L0_attn_in['b_q'], 'L0_attn_W_k': _L0_attn_in['W_k'], 'L0_attn_b_k': _L0_attn_in['b_k'], 'L0_attn_W_v': _L0_attn_in['W_v'], 'L0_attn_b_v': _L0_attn_in['b_v'], 'L0_attn_W_o': _L0_attn_in['W_o'], 'L0_attn_b_o': _L0_attn_in['b_o'], 'L0_attn_rel_k_table': _L0_attn_in['rel_k_table'], 'L0_attn_rel_v_table': _L0_attn_in['rel_v_table'], 'L0_ffn_router_w': _L0_ffn_in['router_w'], 'L0_ffn_router_bias': _L0_ffn_in['router_bias'], 'L0_ffn_sw1': _L0_ffn_in['sw1'], 'L0_ffn_sw3': _L0_ffn_in['sw3'], 'L0_ffn_sw2': _L0_ffn_in['sw2'], 'L0_ffn_ew1': _L0_ffn_in['ew1'], 'L0_ffn_ew2': _L0_ffn_in['ew2']}
    _x0 = _d['L0_attn_x']
    _d['L0_attn_x'] = jax.random.normal(jax.random.fold_in(jax.random.key(seed), 1), (16, 512, 128), dtype=_x0.dtype)
    del _x0
    return _d

def reference(L0_attn_x, L0_attn_W_q, L0_attn_b_q, L0_attn_W_k, L0_attn_b_k, L0_attn_W_v, L0_attn_b_v, L0_attn_W_o, L0_attn_b_o, L0_attn_rel_k_table, L0_attn_rel_v_table, L0_ffn_router_w, L0_ffn_router_bias, L0_ffn_sw1, L0_ffn_sw3, L0_ffn_sw2, L0_ffn_ew1, L0_ffn_ew2):

    def _L0_attn_ref(x, W_q, b_q, W_k, b_k, W_v, b_v, W_o, b_o, rel_k_table, rel_v_table):
        import jax, jax.numpy as jnp
        import numpy as np
        EMBED_DIM = 128
        NUM_HEADS = 16
        HEAD_DIM = EMBED_DIM // NUM_HEADS
        SEQ_LEN = 128
        BATCH = 4
        MAX_REL_POS = 2

        def _rel_index(length_q, length_k):
            q = jnp.arange(length_q)[:, None]
            k = jnp.arange(length_k)[None, :]
            return jnp.clip(k - q, -MAX_REL_POS, MAX_REL_POS) + MAX_REL_POS
        B, S, E = x.shape
        H, D = (NUM_HEADS, HEAD_DIM)
        scale = jnp.sqrt(jnp.asarray(D, x.dtype))
        Q = x @ W_q + b_q
        K = x @ W_k + b_k
        V = x @ W_v + b_v
        Qh = Q.reshape(B, S, H, D).transpose(0, 2, 1, 3)
        Kh = K.reshape(B, S, H, D).transpose(0, 2, 1, 3)
        Vh = V.reshape(B, S, H, D).transpose(0, 2, 1, 3)
        scores = jnp.einsum('bhqd,bhkd->bhqk', Qh, Kh)
        idx = _rel_index(S, S)
        rel_k = rel_k_table[idx]
        scores = (scores + jnp.einsum('bhqd,qkd->bhqk', Qh, rel_k)) / scale
        causal = jnp.tril(jnp.ones((S, S), dtype=bool))
        scores = jnp.where(causal[None, None], scores, jnp.asarray(-1000000000.0, scores.dtype))
        attn = jax.nn.softmax(scores, axis=-1)
        out = jnp.einsum('bhqk,bhkd->bhqd', attn, Vh)
        rel_v = rel_v_table[idx]
        out = out + jnp.einsum('bhqk,qkd->bhqd', attn, rel_v)
        out = out.transpose(0, 2, 1, 3).reshape(B, S, E)
        return out @ W_o + b_o

    def _L0_ffn_ref(x, router_w, router_bias, sw1, sw3, sw2, ew1, ew2):
        import jax, jax.numpy as jnp
        import numpy as np
        D_MODEL = 128
        H_SHARED = 256
        H_ROUTED = 128
        N_EXPERTS = 8
        TOP_K = 2
        B, T, C = x.shape
        xf = x.reshape(-1, C)
        shared_out = jax.nn.silu(xf @ sw1) * (xf @ sw3) @ sw2
        s = jax.nn.sigmoid((xf @ router_w.T).astype(jnp.float32))
        sel_scores = s + router_bias.astype(jnp.float32)
        _, topk_idx = jax.lax.top_k(sel_scores, TOP_K)
        s_sel = jnp.take_along_axis(s, topk_idx, axis=1)
        denom = s_sel.sum(axis=1, keepdims=True)
        gates = jnp.where(denom > 1e-09, s_sel / (denom + 1e-09), 1.0 / TOP_K).astype(x.dtype)
        one_hot = jax.nn.one_hot(topk_idx, N_EXPERTS, dtype=x.dtype)
        comb = jnp.einsum('nke,nk->ne', one_hot, gates)
        h = jax.nn.gelu(jnp.einsum('nd,edh->neh', xf, ew1), approximate=False)
        y = jnp.einsum('neh,ehd->ned', h, ew2)
        routed_out = jnp.einsum('ned,ne->nd', y, comb)
        return (shared_out + routed_out).reshape(B, T, C)
    x = L0_attn_x
    x = x + _layernorm(_L0_attn_ref(_layernorm(x, axis=-1), L0_attn_W_q, L0_attn_b_q, L0_attn_W_k, L0_attn_b_k, L0_attn_W_v, L0_attn_b_v, L0_attn_W_o, L0_attn_b_o, L0_attn_rel_k_table, L0_attn_rel_v_table), axis=-1)
    x = x + _layernorm(_L0_ffn_ref(_layernorm(x, axis=-1), L0_ffn_router_w, L0_ffn_router_bias, L0_ffn_sw1, L0_ffn_sw3, L0_ffn_sw2, L0_ffn_ew1, L0_ffn_ew2), axis=-1)
    return x

_drawn_inputs = setup_inputs


def setup_inputs(seed=0):
    import zlib

    import numpy as np

    out = dict(_drawn_inputs(seed))
    spreads = {'L0_attn_b_q': (0.0, 0.1),
     'L0_attn_b_k': (0.0, 0.1),
     'L0_attn_b_v': (0.0, 0.1),
     'L0_attn_b_o': (0.0, 0.1),
     'L0_ffn_router_bias': (0.0, 0.1)}
    factors = {}
    for name, (base, spread) in spreads.items():
        noise = np.random.default_rng([zlib.crc32(name.encode()), seed]).standard_normal(out[name].shape)
        drawn = base * np.exp(spread * noise) if base else spread * noise
        out[name] = jnp.asarray(drawn.astype(out[name].dtype))
    for name, factor in factors.items():
        out[name] = (out[name] * factor).astype(out[name].dtype)
    return out
```

```python
from contextlib import ExitStack

import numpy as np
import concourse.bass as bass
from concourse import mybir

F32 = mybir.dt.float32
F16 = mybir.dt.float16
BF16 = mybir.dt.bfloat16
U32 = mybir.dt.uint32
ALU = mybir.AluOpType
ACT = mybir.ActivationFunctionType
AX = mybir.AxisListType

P = 128
NSEQ, SEQ = 16, 512
NT = SEQ // P
H, D = 16, 8
NPAIR, NGRP = H // 2, H // 4
SCALE = float(D) ** -0.5
EPS = 1e-5
M_UNIT = 16.0
MASKED = -1e30
TERMS = 4
STACK = TERMS * D
K_MAX = STACK + 1
K_EXP = STACK + 2
PBUF = 4
NE, HR, HS = 8, 128, 256
NC = HS // P
DIAG = P + 1

WIDTH = [SEQ - P * kt for kt in range(NT)]
START = [sum(WIDTH[:kt]) for kt in range(NT)]
PCOLS = sum(WIDTH)

MISC_ORDER = ["e_sums", "av0", "av1", "s_tok", "xn2", "m0", "av2", "logits", "m1", "av3"]
MISC_OF = {"A": ("e_sums", "s_tok", "m0", "m1"), "B": ("av0", "av1", "av2", "av3"), "C": ("xn2", "logits")}
WIDE_ORDER = ["xT", "oT", "qk", "oproj", "v"] + [f"s{i}" for i in range(NPAIR * NT)]
WIDE_OF = {"A": ("xT", "qk", "v") + tuple(f"s{i}" for i in range(NPAIR * NT)), "C": ("oT", "oproj"), "B": ()}
CHAIN_DVE, CHAIN_POOL = 48, 7


class Step:

    def __init__(self, t0, u=None):
        self.t0, self.u = t0, u
        self.A, self.B, self.C = t0 < NSEQ, 1 <= t0 <= NSEQ, t0 >= 2
        self.a, self.b, self.c = t0, t0 - 1, t0 - 2

    def seq(self, s0):
        return s0 if self.u is None else self.u * 2 + s0

    def at(self, count, rate):
        return count if self.u is None else self.u * (2 * rate) + count

    def _uses(self, order, of, what):
        n = 0
        for t in range(self.t0 + 1):
            on = {"A": t < NSEQ, "B": 1 <= t <= NSEQ, "C": t >= 2}
            for name in order:
                if t == self.t0 and name == what:
                    return n
                n += any(on[k] and name in of[k] for k in of)
        raise KeyError(what)

    def misc(self, what):
        return self.at(self._uses(MISC_ORDER, MISC_OF, what), len(MISC_ORDER))

    def wide(self, what):
        n = self._uses(WIDE_ORDER, WIDE_OF, what)
        return self.at(n, len(WIDE_ORDER)), n % 2

    def wide_before(self, what):
        n = self._uses(WIDE_ORDER, WIDE_OF, what) // 2
        return n if self.u is None else self.u * len(WIDE_ORDER) + n


def steps(eng, body):
    body(Step(0))
    body(Step(1))
    with eng.Fori(0, (NSEQ - 2) // 2) as u:
        body(Step(2, u))
        body(Step(3, u))
    body(Step(NSEQ))
    body(Step(NSEQ + 1))


class Ffn:

    def __init__(self, s0, u=None):
        self.s0, self.u = s0, u

    def seq(self, s0):
        return s0 if self.u is None else self.u * 2 + s0

    def at(self, extra, rate):
        n = rate * self.s0 + extra
        return n if self.u is None else self.u * (2 * rate) + n


def ffn_steps(eng, body):
    body(Ffn(0))
    body(Ffn(1))
    with eng.Fori(0, (NSEQ - 4) // 2) as u:
        body(Ffn(2, u))
        body(Ffn(3, u))
    body(Ffn(NSEQ - 2))
    body(Ffn(NSEQ - 1))


UNITS = [("c", 0), ("e", 0), ("e", 1), ("e", 2), ("c", 1)] + [("e", e) for e in range(3, NE)]
CHAIN_FFN = 38
LAG = 2
EXPERT_POS = [UNITS.index(("e", e)) for e in range(NE)]


def hid(f, i):
    return (f.s0 * len(UNITS) + i) % 4


class Own:

    def __init__(self, eng, sem, per_step):
        self.eng, self.sem, self.per_step, self.n, self.base = eng, sem, per_step, 0, None

    def begin(self, st):
        if st.u is not None and st.t0 == 2:
            self.loop0 = self.n
        if st.t0 == NSEQ and self.per_step:
            self.n = self.loop0 + self.per_step * (NSEQ - 2)
        self.st = st
        self.first = self.n

    def end_ffn(self, f):
        if 0 < f.s0 < NSEQ - 1 and self.per_step != self.n - self.first:
            raise AssertionError((self.n - self.first, self.per_step))

    def begin_ffn(self, f):
        if f.s0 == 2 and f.u is not None:
            self.loop0 = self.n
        if f.s0 == NSEQ - 2:
            self.n = self.loop0 + self.per_step * (NSEQ - 4)
        self.st, self.first = Step(0, f.u), self.n

    def end(self):
        if self.st.A and self.st.B and self.st.C and self.per_step != self.n - self.first:
            raise AssertionError((self.n - self.first, self.per_step))

    def mark(self, ins):
        ins.then_inc(self.sem, 1)
        self.n += 1

    def settle(self, apart=None):
        self.eng.wait_ge(self.sem, self.st.at(self.n, self.per_step))
        if apart is not None:
            self.eng.sem_inc(apart, 1)


def need(eng, sem, value):
    if not isinstance(value, int) or value > 0:
        eng.wait_ge(sem, value)


def wait_apart(eng, sem, value, passed):
    need(eng, sem, value)
    eng.sem_inc(passed, 1)


def block_kernel(nc, x, W_q, b_q, W_k, b_k, W_v, b_v, W_o, b_o, rel_k, rel_v,
                 router_w, router_bias, sw1, sw3, sw2, ew1, ew2, out):
    ctx = ExitStack()
    with ctx:
        def sb(name, shape, dt=F32):
            return ctx.enter_context(nc.sbuf_tensor(name, shape, dt))

        def sem(name):
            return ctx.enter_context(nc.semaphore(name))

        ident = sb("ident", [P, P])
        ident16 = sb("ident16", [P, P], F16)
        identb = sb("identb", [P, P], BF16)
        maskb = sb("maskb", [P, DIAG], BF16)
        head_sel = sb("head_sel", [P, D, NPAIR, 2])
        head_sum = sb("head_sum", [P, 32])
        wq_in = sb("wq_in", [P, P])
        wk_in = sb("wk_in", [P, P])
        wq = sb("wq", [P, P])
        wk = sb("wk", [P, P])
        wv = sb("wv", [P, P])
        wo = sb("wo", [P, P])
        rwT = sb("rwT", [P, NE])
        bq = sb("bq", [P, 1])
        bk_in = sb("bk_in", [P, 1])
        rk = sb("rk", [P, 3])
        bk = sb("bk", [P, 1])
        dk = sb("dk", [P, 2])
        bv_in = sb("bv_in", [P, P])
        rv = sb("rv", [P, 3, D])
        bv = sb("bv", [P, 3, P])
        bo = sb("bo", [P, P])
        rb = sb("rb", [P, NE])
        neg_half = sb("neg_half", [P, NT])
        xr = sb("xr", [P, NSEQ, SEQ])
        xnT_dram = nc.dram_tensor("xnT_dram", [NSEQ, P, SEQ], F32, kind="Internal").ap()
        logit = sb("logit", [P, NSEQ, NT * NE])
        st1 = sb("st1", [P, NT, 6])
        mv1 = sb("mv1", [P, NT, 2])
        var1 = sb("var1", [P, NT])
        rs1 = sb("rs1", [P, NT])
        xn = sb("xn", [P, NT, P])
        xnT = sb("xnT", [P, 1 + SEQ])
        qf = sb("qf", [P, SEQ])
        kf = sb("kf", [P, SEQ])
        qh = sb("qh", [P, SEQ], F16)
        ql = sb("ql", [P, SEQ], F16)
        kh = sb("kh", [P, SEQ], F16)
        kl = sb("kl", [P, SEQ], F16)
        e0 = sb("e0", [P, SEQ])
        e1 = sb("e1", [P, SEQ])
        s_rows = sb("s_rows", [64, SEQ])
        s_tok = sb("s_tok", [P, 2, NT, H])
        mx = sb("mx", [P, NT, H])
        mxa = sb("mxa", [P, NT, H])
        m16 = sb("m16", [P, NT, H], F16)
        d01 = sb("d01", [P, 2, NT, H])
        p01 = sb("p01", [P, 2, NT, H])
        mT = [sb(f"mT{i}", [H // 2, SEQ], F16) for i in range(2)]
        v_near = sb("v_near", [P, 2, NT, P])
        pv_near = sb("pv_near", [P, 2, NT, P])
        qs = [sb(f"qs{i}", [P, NPAIR, SEQ], F16) for i in range(2)]
        ks = [sb(f"ks{i}", [P, NPAIR, SEQ], F16) for i in range(2)]
        vp = [sb(f"vp{i}", [P, NT, H, 32]) for i in range(2)]
        near = [sb(f"near{i}", [P, NT, P]) for i in range(2)]
        p_near = [sb(f"p_near{i}", [P, NT, H]) for i in range(2)]
        prob = [sb(f"prob{i}", [P, 2, PCOLS]) for i in range(PBUF)]
        av_s = [sb(f"av_s{i}", [P, SEQ]) for i in range(2)]
        den = sb("den", [P, NT, 4])
        rden = sb("rden", [P, NT, 4])
        num = sb("num", [P, NT, 4, D])
        o_tok = sb("o_tok", [P, NT, P])
        oT = sb("oT", [P, SEQ])
        y = sb("y", [P, NT, P])
        st2 = sb("st2", [P, NT, 6])
        mv2 = sb("mv2", [P, NT, 2])
        var2 = sb("var2", [P, NT])
        rs2 = sb("rs2", [P, NT])
        z = sb("z", [P, NT, P])
        st3 = sb("st3", [P, NT, 6])
        mv3 = sb("mv3", [P, NT, 2])
        var3 = sb("var3", [P, NT])
        rs3 = sb("rs3", [P, NT])
        xn2 = sb("xn2", [P, NT, P])
        xn2T = sb("xn2T", [P, SEQ])

        sw1_s = sb("sw1_s", [P, HS])
        sw3_s = sb("sw3_s", [P, HS])
        sw2_s = sb("sw2_s", [P, NC, P])
        ew1_s = sb("ew1_s", [P, NE, HR])
        ew2_s = sb("ew2_s", [P, NE, P])
        sel_e = sb("sel_e", [64, NE, P], BF16)
        iota_i = sb("iota_i", [P, NE], mybir.dt.int32)
        iota_f = sb("iota_f", [P, NE])
        sel = sb("sel", [P, NT, NE])
        top = sb("top", [P, NT, 8])
        top_i = sb("top_i", [P, NT, 8], U32)
        top_f = sb("top_f", [P, NT, 2])
        is_top = sb("is_top", [P, 2, NT, NE])
        in_two = sb("in_two", [P, NT, NE])
        chosen = sb("chosen", [P, NT, NE])
        total = sb("total", [P, NT])
        total_e = sb("total_e", [P, NT])
        normal = sb("normal", [P, NT])
        even = sb("even", [P, NT])
        gate = sb("gate", [P, NT, NE])
        gate_n = sb("gate_n", [P, NT, NE])
        gate_r = sb("gate_r", [P, NT, NE])
        gate3 = sb("gate3", [P, NT, 64], BF16)
        gateT = sb("gateT", [64, SEQ], BF16)
        xeT = [prob[0][:, 0, i * SEQ:(i + 1) * SEQ] for i in range(2)]
        act_out = [prob[1][:, 0, i * SEQ:(i + 1) * SEQ] for i in range(2)]
        tanh_u = prob[2][:, 0, 0:SEQ]
        silu2 = prob[2][:, 0, SEQ:2 * SEQ]
        hidden = [prob[3][:, i // 2, (i % 2) * SEQ:(i % 2 + 1) * SEQ] for i in range(4)]
        fT = prob[1][:, 1, 0:SEQ]
        f_tok = prob[2][:, 1, 0:SEQ]
        result = prob[0][:, 1, 0:SEQ]

        ps_exp = [ctx.enter_context(nc.psum_tensor(f"ps_exp{i}", [P, SEQ], F32)) for i in range(2)]
        ps_wide = [ctx.enter_context(nc.psum_tensor(f"ps_wide{i}", [P, 2, SEQ], F32)) for i in range(2)]
        ps_av = ctx.enter_context(nc.psum_tensor("ps_av", [P, SEQ], F32))
        ps_misc = ctx.enter_context(nc.psum_tensor("ps_misc", [P, SEQ], F32))

        names = """attn_loaded const_made const_ready x_loaded0 x_loaded1 x_loaded2 dve_own pool_own wide_full wide_free0 wide_free1
            misc_full misc_free stats1 rstd1 xn_ready qk_ready qk_split e_ready
            stacks0 stacks1 v_ready near_ready k_rows q_rows m16_ready mrow0 mrow1 d_ready p_ready
            exp_full exp_done p_masked av_full av_copied o_ready stats2 rstd2 z_ready
            x1_ready stats3 rstd3 xn2_ready xnT_stored
            ffn_loaded ffn_const attn_over xe_loaded0 xe_loaded1 logits_exp chosen_ready gateT_full gateT_ready front_full
            uv_full tanh_ready act_ready hidden_ready uv_free gates_full second_done fT_ready f_tok_full f_tok_ready
            passed_sp passed_pool passed_dve passed_pe stats4 rstd4 z4_ready out_ready stored dve_own2 pool_own2""".split()
        S = {n: sem(n) for n in names}
        x_loaded = [S["x_loaded0"], S["x_loaded1"], S["x_loaded2"]]
        stacks = [S["stacks0"], S["stacks1"]]
        mrow = [S["mrow0"], S["mrow1"]]

        wide_free = [S["wide_free0"], S["wide_free1"]]

        N_ATTN_LOADS = 4 + 1 + 4 + 6 + 4
        N_CONST_MADE, N_CONST = 9, 7 + 10
        x_v = x.rearrange("b (i p) d -> p b i d", p=P)
        out_v = out.rearrange("b (i p) d -> p b i d", p=P)

        def split_heads(v):
            return v.rearrange("(pr b d) -> b d pr", b=2, d=D)

        passed = {n: S["passed_" + n] for n in ("sp", "pool", "dve", "pe")}

        block = ctx.enter_context(nc.Block())

        @block.sync
        def _(sp):
            late = []

            def load(dst, src):
                sp.dma_start(dst, src, allow_slow_non_contiguous=True).then_inc(S["attn_loaded"], 16)

            sp.dma_start(xr[:, 0, :].rearrange("p (i d) -> p i d", i=NT), x_v[:, 0]).then_inc(x_loaded[0], 16)
            for dst, src in ((wq_in, W_q), (wk_in, W_k), (wv, W_v), (wo, W_o)):
                load(dst[:, :], src)
            load(rwT[:, :], router_w.rearrange("e d -> d e"))
            for dst, src in ((bq, b_q), (bk_in, b_k)):
                for b in range(2):
                    load(dst[64 * b:64 * b + 64, :], split_heads(src)[b])
            for r in range(3):
                for b in range(2):
                    load(rk[64 * b:64 * b + 64, r:r + 1],
                         rel_k[r, :].rearrange("(d o) -> d o", o=1).to_broadcast([D, NPAIR]))
            load(bv_in[:, :], b_v.partition_broadcast(P))
            load(bo[:, :], b_o.partition_broadcast(P))
            load(rv[:, :, :], rel_v[0:3, :].partition_broadcast(P))
            load(rb[:, :], router_bias.partition_broadcast(P))
            for dst, src in ((sw1_s[:, :], sw1), (sw3_s[:, :], sw3), (sw2_s[:, :, :], sw2.rearrange("(c p) d -> p c d", p=P)),
                             (ew1_s[:, :, :], ew1.rearrange("e d h -> d e h")),
                             (ew2_s[:, :, :], ew2.rearrange("e h d -> h e d"))):
                late.append((dst, src))

            sp.dma_start(xr[:, 1, :].rearrange("p (i d) -> p i d", i=NT), x_v[:, 1]).then_inc(x_loaded[1], 16)

            def step(st):
                if st.t0 == 1:
                    sp.dma_start(xr[:, 2:, :].rearrange("p b (i d) -> p b i d", i=NT),
                                 x_v[:, 2:]).then_inc(x_loaded[2], 16)
                    for dst, src in late:
                        sp.dma_start(dst, src).then_inc(S["ffn_loaded"], 16)
                if st.A:
                    par = st.t0 % 2
                    wait_apart(sp, S["qk_split"], st.at(2 * (st.a + 1), 2), passed["sp"])
                    wait_apart(sp, S["exp_full"], st.at(2 * NPAIR * NT * (st.a - 1), 2 * NPAIR * NT), passed["sp"])
                    for stk, parts in ((qs[par], (qh, qh, ql, ql)), (ks[par], (kh, kl, kh, kl))):
                        for b in range(2):
                            for r, part in enumerate(parts):
                                lo = 64 * b + D * r
                                sp.dma_start(stk[lo:lo + D, :, :], part[64 * b:64 * b + 64, :]).then_inc(stacks[par], 16)
                if st.C:
                    wait_apart(sp, S["misc_free"], st.misc("xn2") + 1, passed["sp"])
                    sp.dma_start(xnT_dram[st.seq(st.c)], xn2T[:, :]).then_inc(S["xnT_stored"], 16)
                if st.A:
                    for half in range(2):
                        wait_apart(sp, S["misc_free"], st.misc(f"m{half}") + 1, passed["sp"])
                        for b in range(2):
                            row = 64 * b + STACK + 1
                            sp.dma_start(qs[par][row:row + 1, 4 * half:4 * half + 4, :],
                                         mT[half][b:H // 2:2, :]).then_inc(mrow[half], 16)

            steps(sp, step)

            xe_loaded = [S["xe_loaded0"], S["xe_loaded1"]]

            def load_xe(s, s0, par):
                sp.dma_start(xeT[par], xnT_dram[s]).then_inc(xe_loaded[par], 16)

            sp.wait_ge(S["av_full"], NGRP * NSEQ)
            sp.wait_ge(S["xnT_stored"], 16 * NSEQ)
            load_xe(0, 0, 0)
            load_xe(1, 1, 1)

            def ffn(f):
                if f.s0 + 2 < NSEQ:
                    wait_apart(sp, S["front_full"], f.at(NE + NC, NE + NC), passed["sp"])
                    load_xe(f.seq(f.s0 + 2), 0, f.s0 % 2)
                wait_apart(sp, S["out_ready"], f.at(1, 1), passed["sp"])
                sp.dma_start(out_v[:, f.seq(f.s0)], result.rearrange("p (i d) -> p i d", i=NT)).then_inc(S["stored"], 16)

            ffn_steps(sp, ffn)
            sp.wait_ge(S["stored"], 16 * NSEQ)

        @block.gpsimd
        def _(pool):
            def zeros(ins):
                ins.then_inc(S["const_made"], 1)

            zeros(pool.memset(ident[:, :], 0.0))
            zeros(pool.memset(ident16[:, :], 0.0))
            zeros(pool.memset(identb[:, :], 0.0))
            zeros(pool.memset(maskb[:, :], 0.0))
            zeros(pool.memset(head_sel[:, :, :, :], 0.0))
            zeros(pool.memset(neg_half[:, :], -0.5))
            zeros(pool.memset(e1[:, 0:1], MASKED / D))
            zeros(pool.memset(xnT[:, 0:1], 0.0))
            zeros(pool.memset(head_sum[:, :], 0.0))
            pool.wait_ge(S["const_made"], N_CONST_MADE)
            for m in (ident, ident16, identb):
                pool.affine_select(out=m[:, :], in_=m[:, :], compare_op=ALU.not_equal, fill=1.0, base=0,
                                   pattern=[[-1, P]], channel_multiplier=1).then_inc(S["const_ready"], 1)
            pool.affine_select(out=maskb[:, :], in_=maskb[:, :], compare_op=ALU.is_ge, fill=MASKED, base=-1,
                               pattern=[[-1, DIAG]], channel_multiplier=1).then_inc(S["const_ready"], 1)
            pool.affine_select(out=head_sel[:, :, :, :], in_=head_sel[:, :, :, :], compare_op=ALU.not_equal,
                               fill=1.0, base=0, pattern=[[-D, D], [-1, NPAIR], [-64, 2]],
                               channel_multiplier=1).then_inc(S["const_ready"], 1)
            for i in range(2):
                pool.memset(vp[i][:, :, :, :], 0.0).then_inc(S["pool_own"], 1)
            pool.wait_ge(S["pool_own"], 2)
            for i in range(2):
                pool.memset(vp[i][:, :, :, D:D + 1], 1.0).then_inc(S["const_ready"], 1)

            pool.wait_ge(S["const_ready"], 7)
            for i in range(2):
                for b in range(2):
                    lo = 64 * b + STACK
                    pool.memset(ks[i][lo:lo + 32, :, :], -M_UNIT).then_inc(S["k_rows"], 1)
                    pool.wait_ge(S["k_rows"], 2 * i + b + 1)

            pool.memset(sel_e[:, :, :], 0.0).then_inc(S["ffn_const"], 1)
            pool.iota(iota_i[:, :], pattern=[[1, NE]], base=0, channel_multiplier=0).then_inc(S["ffn_const"], 1)
            pool.memset(gate3[:, :, :], 0.0).then_inc(S["ffn_const"], 1)
            for r in range(3):
                pool.wait_ge(S["ffn_const"], 3 + r)
                pool.affine_select(out=sel_e[:, :, :], in_=sel_e[:, :, :], compare_op=ALU.not_equal, fill=1.0,
                                   base=-NE * r, pattern=[[-1, NE], [0, P]],
                                   channel_multiplier=1).then_inc(S["ffn_const"], 1)
            pool.wait_ge(S["ffn_const"], 6)
            pool.tensor_copy(iota_f[:, :], iota_i[:, :]).then_inc(S["ffn_const"], 1)

            own = Own(pool, S["pool_own"], CHAIN_POOL)
            own.n = 2

            def rstd(st, seq, mv, var, rs, got, done):
                wait_apart(pool, S[got], st.at(seq + 1, 1), passed["pool"])
                own.mark(pool.tensor_scalar(var[:, :], mv[:, :, 1], 1.0, EPS, ALU.mult, ALU.add))
                own.settle()
                pool.tensor_tensor(rs[:, :], var[:, :], neg_half[:, :], ALU.pow).then_inc(S[done], 1)

            def mask_pair(st, pr):
                for kt in range(NT):
                    wait_apart(pool, S["exp_done"],
                               st.at(2 * NPAIR * NT * st.b + 2 * NT * pr + 2 * kt + 2, 2 * NPAIR * NT), passed["pool"])
                    w = min(DIAG, WIDTH[kt])
                    v = prob[pr % PBUF][:, :, START[kt]:START[kt] + w]
                    pool.affine_select(out=v, in_=v, compare_op=ALU.is_ge, fill=0.0, base=-2,
                                       pattern=[[0, 2], [1, w]], channel_multiplier=-1).then_inc(S["p_masked"], 1)

            def near_half(st, half):
                pool.wait_ge(S["p_ready"], st.at(2 * st.a + half + 1, 2))
                if half == 0:
                    pool.wait_ge(S["v_ready"], st.at(2 * (st.a + 1), 2))
                    pool.wait_ge(wide_free[st.wide("v")[1]], st.wide_before("v") + 1)
                    need(pool, S["o_ready"], st.at(NGRP * (st.a - 1), NGRP))
                hs = slice(half * 8, half * 8 + 8)
                cols = slice(half * 64, half * 64 + 64)
                for n in range(2):
                    a = v_near[:, n, :, cols].rearrange("p t (h d) -> p t h d", d=D)
                    o = pv_near[:, n, :, cols].rearrange("p t (h d) -> p t h d", d=D)
                    pb = p01[:, n, :, hs].unsqueeze(3).to_broadcast([P, NT, 8, D])
                    own.mark(pool.tensor_tensor(o, a, pb, ALU.mult))
                pool.tensor_tensor(p_near[st.a % 2][:, :, hs], p01[:, 0, :, hs], p01[:, 1, :, hs],
                                   ALU.add).then_inc(S["near_ready"], 1)
                own.settle()
                pool.tensor_tensor(near[st.a % 2][:, :, cols], pv_near[:, 0, :, cols], pv_near[:, 1, :, cols],
                                   ALU.add).then_inc(S["near_ready"], 1)

            def step(st):
                own.begin(st)
                if st.A:
                    rstd(st, st.a, mv1, var1, rs1, "stats1", "rstd1")
                if st.B:
                    mask_pair(st, 0)
                    mask_pair(st, 1)
                if st.C:
                    rstd(st, st.c, mv2, var2, rs2, "stats2", "rstd2")
                if st.B:
                    mask_pair(st, 2)
                if st.C:
                    pool.wait_ge(S["z_ready"], st.at(st.c + 1, 1))
                    xv = xr[:, st.seq(st.c), :]
                    pool.tensor_tensor(xv, xv, z[:, :, :].rearrange("p i d -> p (i d)"),
                                       ALU.add).then_inc(S["x1_ready"], 1)
                if st.B:
                    mask_pair(st, 3)
                if st.C:
                    rstd(st, st.c, mv3, var3, rs3, "stats3", "rstd3")
                if st.B:
                    for pr in (4, 5):
                        mask_pair(st, pr)
                if st.B:
                    mask_pair(st, 6)
                if st.A:
                    near_half(st, 0)
                if st.B:
                    mask_pair(st, 7)
                if st.A:
                    near_half(st, 1)
                own.end()

            steps(pool, step)

            own2 = Own(pool, S["pool_own2"], 1)

            def end_of(f, seq, st0):
                wait_apart(pool, S["stats4"], f.at(st0 + 1, 1), passed["pool"])
                own2.mark(pool.tensor_scalar(var2[:, :], mv2[:, :, 1], 1.0, EPS, ALU.mult, ALU.add))
                own2.settle()
                pool.tensor_tensor(rs2[:, :], var2[:, :], neg_half[:, :], ALU.pow).then_inc(S["rstd4"], 1)
                pool.wait_ge(S["z4_ready"], f.at(st0 + 1, 1))
                need(pool, S["stored"], f.at(16 * st0, 16))
                pool.tensor_tensor(result, xr[:, seq, :], z[:, :, :].rearrange("p i d -> p (i d)"),
                                   ALU.add).then_inc(S["out_ready"], 1)

            def ffn(f):
                own2.begin_ffn(f)
                if f.s0 > 0:
                    end_of(f, f.seq(f.s0 - 1), -1)
                own2.end_ffn(f)

            ffn_steps(pool, ffn)
            end_of(Ffn(NSEQ - 1), NSEQ - 1, 0)

        @block.scalar
        def _(act):
            def exp_unit(st, pr, n):
                i = 2 * NT * pr + n
                kt, b = n // 2, n % 2
                act.wait_ge(S["exp_full"], st.at(2 * NPAIR * NT * st.b + i + 1, 2 * NPAIR * NT))
                if n == 0 and pr % 2 == 0:
                    need(act, S["av_full"], st.at(NGRP * st.b + pr // 2 - 1, NGRP))
                w = WIDTH[kt]
                act.activation(prob[pr % PBUF][:, b, START[kt]:START[kt] + w], ps_exp[b][:, 0:w], ACT.Exp,
                               scale=SCALE).then_inc(S["exp_done"], 1)

            def xT_out(st):
                n, unit = st.wide("xT")
                act.wait_ge(S["wide_full"], n + 1)
                act.copy(xnT[:, 1:1 + SEQ], ps_wide[unit][:, 0, :]).then_inc(wide_free[unit], 1)

            def qk_out(st):
                n, unit = st.wide("qk")
                act.wait_ge(S["wide_full"], n + 1)
                if st.t0 == 0:
                    act.wait_ge(S["const_ready"], N_CONST)
                if st.a > 0:
                    act.wait_ge(stacks[(st.a - 1) % 2], st.at(256 * ((st.a - 1) // 2 + 1), 128))
                    act.wait_ge(S["e_ready"], st.at(2 * st.a, 2))
                for i, (f, hi, bias) in enumerate(((qf, qh, bq), (kf, kh, bk))):
                    act.activation(f[:, :], ps_wide[unit][:, i, :], ACT.Identity, bias=bias[:, :]).then_inc(S["qk_ready"], 1)
                    last = act.activation(hi[:, :], ps_wide[unit][:, i, :], ACT.Identity, bias=bias[:, :])
                    last.then_inc(S["qk_ready"] if i == 0 else wide_free[unit], 1)

            def oT_out(st):
                n, unit = st.wide("oT")
                act.wait_ge(S["wide_full"], n + 1)
                act.copy(oT[:, :], ps_wide[unit][:, 0, :]).then_inc(wide_free[unit], 1)

            def s_rows_out(st):
                act.wait_ge(S["misc_full"], st.misc("e_sums") + 1)
                act.copy(s_rows[:, :], ps_misc[0:64, :]).then_inc(S["misc_free"], 1)

            def av_out(st, g):
                act.wait_ge(S["av_full"], st.at(NGRP * st.b + g + 1, NGRP))
                act.copy(av_s[g % 2][:, :], ps_av[:, :]).then_inc(S["av_copied"], 1)

            def xn2T_out(st):
                act.wait_ge(S["misc_full"], st.misc("xn2") + 1)
                need(act, S["xnT_stored"], st.at(16 * st.c, 16))
                act.copy(xn2T[:, :], ps_misc[:, :]).then_inc(S["misc_free"], 1)

            def mT_out(st, half):
                act.wait_ge(S["misc_full"], st.misc(f"m{half}") + 1)
                if st.a > 0:
                    act.wait_ge(mrow[half], st.at(32 * st.a, 32))
                act.copy(mT[half][:, :], ps_misc[:, :].bitcast(F16)[0:H // 2, 0:SEQ]).then_inc(S["misc_free"], 1)

            def p_near_exp(st, half):
                act.wait_ge(S["d_ready"], st.at(2 * st.a + half + 1, 2))
                need(act, S["near_ready"], st.at(4 * (st.a - 1) + 2 * half + 2, 4))
                hs = slice(half * 8, half * 8 + 8)
                act.activation(p01[:, :, :, hs].rearrange("p n t h -> p (n t) h"),
                               d01[:, :, :, hs].rearrange("p n t h -> p (n t) h"), ACT.Exp,
                               scale=SCALE).then_inc(S["p_ready"], 1)

            def step(st):
                def exps(pr, units=range(2 * NT)):
                    if st.B:
                        for n in units:
                            exp_unit(st, pr, n)

                exps(0)
                if st.A:
                    xT_out(st)
                if st.C:
                    oT_out(st)
                exps(1)
                if st.A:
                    qk_out(st)
                exps(2)
                if st.A:
                    s_rows_out(st)
                exps(3)
                if st.B:
                    av_out(st, 0)
                exps(4)
                exps(5)
                if st.B:
                    av_out(st, 1)
                exps(6, range(3))
                if st.C:
                    xn2T_out(st)
                exps(6, range(3, 2 * NT))
                exps(7, range(3))
                if st.A:
                    mT_out(st, 0)
                    p_near_exp(st, 0)
                exps(7, range(3, 2 * NT))
                if st.B:
                    av_out(st, 2)
                if st.A:
                    mT_out(st, 1)
                    p_near_exp(st, 1)
                if st.B:
                    av_out(st, 3)

            steps(act, step)

            act.wait_ge(S["misc_free"], Step(NSEQ + 1).misc("logits") + 1)
            act.activation(logit[:, :, :], logit[:, :, :], ACT.Exp, scale=-1.0).then_inc(S["logits_exp"], 1)

            def gateT_out(f, ahead):
                act.wait_ge(S["gateT_full"], f.at(ahead + 1, 1))
                act.copy(gateT[:, :], ps_misc[:, :].bitcast(BF16)[0:64, 0:SEQ]).then_inc(S["gateT_ready"], 1)

            def end_out(f, s):
                act.wait_ge(S["second_done"], f.at(len(UNITS) * (s + 1), len(UNITS)))
                act.copy(fT, ps_av[:, :]).then_inc(S["fT_ready"], 1)

            def ffn(f):
                if f.s0 == 0:
                    act.wait_ge(S["av_full"], NGRP * NSEQ)
                    gateT_out(f, 0)
                for i, (kind, k) in enumerate(UNITS):
                    if kind == "c":
                        act.wait_ge(S["front_full"], f.at(i + 1, len(UNITS)))
                        before = UNITS.index(("c", 1 - k)) + 1 - (0 if k else len(UNITS))
                        need(act, S["hidden_ready"], f.at(before, len(UNITS)))
                        act.activation(tanh_u, ps_wide[1][:, 0, :], ACT.Tanh, scale=0.5).then_inc(S["act_ready"], 1)
                    else:
                        act.wait_ge(S["front_full"], f.at(i + 1, len(UNITS)))
                        before = EXPERT_POS[k - 2] + 1 if k >= 2 else EXPERT_POS[k - 2] + 1 - len(UNITS)
                        need(act, S["hidden_ready"], f.at(before, len(UNITS)))
                        act.activation(act_out[k % 2], ps_exp[k % 2][:, :], ACT.Gelu).then_inc(S["act_ready"], 1)
                    if i == 1 and f.s0 > 0:
                        end_out(f, -1)
                if f.s0 < NSEQ - 1:
                    gateT_out(f, 1)

            ffn_steps(act, ffn)
            end_out(Ffn(NSEQ - 1), 0)

        @block.vector
        def _(dve):
            own = Own(dve, S["dve_own"], CHAIN_DVE)

            def ready(ins):
                ins.then_inc(S["const_ready"], 1)

            for i in range(2):
                for b in range(2):
                    lo = 64 * b + STACK
                    dve.memset(qs[i][lo:lo + 32, :, :].bitcast(F32), 0.0).then_inc(S["q_rows"], 1)
            dve.wait_ge(S["attn_loaded"], 16 * N_ATTN_LOADS)
            dve.wait_ge(S["const_ready"], 7)
            for dst, src in ((wq, wq_in), (wk, wk_in)):
                for b in range(2):
                    ready(dve.tensor_copy(dst[:, 64 * b:64 * b + 64].rearrange("p (d pr) -> p d pr", d=D),
                                          src[:, :].rearrange("p (pr b d) -> p b d pr", b=2, d=D)[:, b]))
            ready(dve.tensor_reduce(head_sum[:, 0:H], head_sel[:, :, :, :].rearrange("p d pr b -> p (pr b) d"),
                                    AX.X, ALU.add))
            ready(dve.tensor_tensor(bk[:, :], bk_in[:, :], rk[:, 0:1], ALU.add))
            ready(dve.tensor_scalar(dk[:, :], rk[:, 1:3], rk[:, 0:1], None, ALU.subtract))
            for i in range(3):
                ready(dve.tensor_tensor(bv[:, i, :].rearrange("p (h d) -> p h d", d=D),
                                          bv_in[:, :].rearrange("p (h d) -> p h d", d=D),
                                          rv[:, i, :].unsqueeze(1).to_broadcast([P, H, D]), ALU.add))
            dve.wait_ge(S["const_ready"], N_CONST)

            def stats(src, st_, mv):
                for i in range(NT):
                    own.mark(dve.bn_stats(st_[:, i, :], src[:, i * P:i * P + P]))
                own.settle(passed["dve"])
                for i in range(NT):
                    last = dve.bn_aggr(mv[:, i, :], st_[:, i, :])
                    if i < NT - 1:
                        own.mark(last)
                return last

            def normalise(dst, src, mv, rs):
                for i in range(NT):
                    last = dve.tensor_scalar(dst[:, i, :], src[:, i * P:i * P + P], mv[:, i, 0:1], rs[:, i:i + 1],
                                             ALU.subtract, ALU.mult)
                    if i < NT - 1:
                        own.mark(last)
                return last

            def ln1(st):
                xv = xr[:, st.seq(st.a), :]
                dve.wait_ge(x_loaded[min(st.t0, 2)], 16)
                stats(xv, st1, mv1).then_inc(S["stats1"], 1)
                dve.wait_ge(S["rstd1"], st.at(st.a + 1, 1))
                normalise(xn, xv, mv1, rs1).then_inc(S["xn_ready"], 1)

            def split_and_near(st):
                dve.wait_ge(S["qk_ready"], st.at(3 * (st.a + 1), 3))
                dve.wait_ge(wide_free[st.wide("qk")[1]], st.wide_before("qk") + 1)
                if st.a > 0:
                    dve.wait_ge(stacks[(st.a - 1) % 2], st.at(256 * ((st.a - 1) // 2 + 1), 128))
                dve.tensor_tensor(ql[:, :], qf[:, :], qh[:, :], ALU.subtract).then_inc(S["qk_split"], 1)
                dve.tensor_tensor(kl[:, :], kf[:, :], kh[:, :], ALU.subtract).then_inc(S["qk_split"], 1)
                dve.scalar_tensor_tensor(e0[:, :], kf[:, :], dk[:, 1:2], qf[:, :], ALU.add,
                                         ALU.mult).then_inc(S["e_ready"], 1)
                dve.scalar_tensor_tensor(e1[:, 1:SEQ], kf[:, 0:SEQ - 1], dk[:, 0:1], qf[:, 1:SEQ], ALU.add,
                                         ALU.mult).then_inc(S["e_ready"], 1)

            def values_out(st):
                n, unit = st.wide("v")
                dve.wait_ge(S["wide_full"], n + 1)
                need(dve, S["av_full"], st.at(NGRP * (st.a - 1), NGRP))
                need(dve, S["near_ready"], st.at(4 * st.a, 4))
                pv = ps_wide[unit][:, 0, :].rearrange("p (t c) -> p t c", t=NT)
                ph = ps_wide[unit][:, 0, :].rearrange("p (t h d) -> p t h d", t=NT, d=D)
                for t in range(NT):
                    last = dve.tensor_tensor(vp[st.a % 2][:, t, :, 0:D], ph[:, t], bv[:, 0, :].rearrange(
                        "p (h d) -> p h d", d=D), ALU.add)
                    if t < NT - 1:
                        own.mark(last)
                last.then_inc(S["v_ready"], 1)
                bc = [bv[:, i, :].unsqueeze(1).to_broadcast([P, NT, P]) for i in range(3)]
                dve.tensor_tensor(v_near[:, 0], pv, bc[2], ALU.add).then_inc(S["v_ready"], 1)
                dve.tensor_tensor(v_near[:, 1], ps_wide[unit][:, 1, :].rearrange("p (t c) -> p t c", t=NT), bc[1],
                                  ALU.add).then_inc(wide_free[unit], 1)

            def s_max(st, i):
                pr, qt = i // NT, i % NT
                n, unit = st.wide(f"s{i}")
                dve.wait_ge(S["wide_full"], n + 1)
                dve.tensor_reduce(mx[:, qt, 2 * pr:2 * pr + 2], ps_wide[unit][:, :, 0:P * (qt + 1)], AX.X,
                                  ALU.max).then_inc(wide_free[unit], 1)

            def s_tok_out(st):
                dve.wait_ge(S["misc_full"], st.misc("s_tok") + 1)
                src = ps_misc[:, 0:NT * 64].rearrange("p (t n r) -> p n t r", t=NT, n=2)[:, :, :, 0:H]
                for n in range(2):
                    last = dve.tensor_copy(s_tok[:, n], src[:, n])
                    if n == 0:
                        own.mark(last)
                last.then_inc(S["misc_free"], 1)
                dve.wait_ge(S["misc_free"], st.misc("s_tok") + 1)

            def max_half(st, half):
                hs = slice(half * 8, half * 8 + 8)
                for i in (1, 2):
                    what = f"s{NPAIR * NT // 2 * (half + 1) - i}"
                    dve.wait_ge(wide_free[st.wide(what)[1]], st.wide_before(what) + 1)
                own.mark(dve.tensor_tensor(mxa[:, :, hs], mx[:, :, hs], s_tok[:, 0, :, hs], ALU.max))
                own.settle()
                own.mark(dve.tensor_tensor(mx[:, :, hs], mxa[:, :, hs], s_tok[:, 1, :, hs], ALU.max))
                own.settle()
                need(dve, S["p_ready"], st.at(2 * (st.a - 1) + half + 1, 2))
                dve.tensor_scalar(m16[:, :, hs], mx[:, :, hs], 1.0 / M_UNIT, None, ALU.mult).then_inc(S["m16_ready"], 1)
                dve.wait_ge(S["m16_ready"], st.at(2 * st.a + half + 1, 2))
                for k in range(2):
                    last = dve.scalar_tensor_tensor(d01[:, k, :, hs], m16[:, :, hs], -M_UNIT, s_tok[:, k, :, hs],
                                                    ALU.mult, ALU.add)
                    if k == 0:
                        own.mark(last)
                last.then_inc(S["d_ready"], 1)

            def av_tok_out(st, g):
                dve.wait_ge(S["misc_full"], st.misc(f"av{g}") + 1)
                if g == 0:
                    dve.wait_ge(S["near_ready"], st.at(4 * st.b + 2, 4))
                if g == 2:
                    dve.wait_ge(S["near_ready"], st.at(4 * st.b + 4, 4))
                need(dve, S["o_ready"], st.at(NGRP * st.b + g, NGRP))
                v = ps_misc[:, :].rearrange("p (t j c) -> p t j c", t=NT, j=4)
                par = st.b % 2
                own.mark(dve.tensor_tensor(den[:, :, :], v[:, :, :, D], p_near[par][:, :, 4 * g:4 * g + 4], ALU.add))
                cols = slice(4 * g * D, 4 * g * D + 4 * D)
                dve.tensor_tensor(num[:, :, :, :], v[:, :, :, 0:D], near[par][:, :, cols].rearrange(
                    "p t (j d) -> p t j d", d=D), ALU.add).then_inc(S["misc_free"], 1)
                own.settle()
                own.mark(dve.reciprocal(rden[:, :, :], den[:, :, :]))
                own.settle()
                dve.wait_ge(S["misc_free"], st.misc(f"av{g}") + 1)
                dve.tensor_tensor(o_tok[:, :, cols].rearrange("p t (j d) -> p t j d", d=D), num[:, :, :, :],
                                  rden[:, :, :].unsqueeze(3).to_broadcast([P, NT, 4, D]),
                                  ALU.mult).then_inc(S["o_ready"], 1)

            def y_out(st):
                n, unit = st.wide("oproj")
                dve.wait_ge(S["wide_full"], n + 1)
                dve.tensor_tensor(y[:, :, :], ps_wide[unit][:, 0, :].rearrange("p (t c) -> p t c", t=NT),
                                  bo[:, :].unsqueeze(1).to_broadcast([P, NT, P]), ALU.add).then_inc(wide_free[unit], 1)
                dve.wait_ge(wide_free[unit], st.wide_before("oproj") + 1)
                stats(y[:, :, :].rearrange("p t c -> p (t c)"), st2, mv2).then_inc(S["stats2"], 1)

            def z_out(st):
                dve.wait_ge(S["rstd2"], st.at(st.c + 1, 1))
                need(dve, S["x1_ready"], st.at(st.c, 1))
                normalise(z, y[:, :, :].rearrange("p t c -> p (t c)"), mv2, rs2).then_inc(S["z_ready"], 1)

            def x1_stats(st):
                dve.wait_ge(S["x1_ready"], st.at(st.c + 1, 1))
                stats(xr[:, st.seq(st.c), :], st3, mv3).then_inc(S["stats3"], 1)

            def xn2_out(st):
                dve.wait_ge(S["rstd3"], st.at(st.c + 1, 1))
                normalise(xn2, xr[:, st.seq(st.c), :], mv3, rs3).then_inc(S["xn2_ready"], 1)

            def logits_out(st):
                dve.wait_ge(S["misc_full"], st.misc("logits") + 1)
                dve.tensor_copy(logit[:, st.seq(st.c), :], ps_misc[:, 0:NT * NE]).then_inc(S["misc_free"], 1)

            def step(st):
                own.begin(st)

                def maxima(lo, hi):
                    if st.A:
                        for i in range(lo, hi):
                            s_max(st, i)

                if st.A:
                    ln1(st)
                    split_and_near(st)
                if st.C:
                    y_out(st)
                if st.A:
                    values_out(st)
                maxima(0, 2)
                if st.C:
                    z_out(st)
                maxima(2, 9)
                if st.B:
                    av_tok_out(st, 0)
                if st.C:
                    x1_stats(st)
                maxima(9, 14)
                if st.C:
                    xn2_out(st)
                maxima(14, 22)
                if st.B:
                    av_tok_out(st, 1)
                maxima(22, 23)
                if st.A:
                    s_tok_out(st)
                    max_half(st, 0)
                maxima(23, 32)
                if st.A:
                    max_half(st, 1)
                if st.B:
                    av_tok_out(st, 2)
                if st.C:
                    logits_out(st)
                if st.B:
                    av_tok_out(st, 3)
                own.end()

            steps(dve, step)

            own2 = Own(dve, S["dve_own2"], CHAIN_FFN)
            own2.st = Step(0)
            dve.wait_ge(S["logits_exp"], 1)
            own2.mark(dve.tensor_scalar(logit[:, :, :], logit[:, :, :], 1.0, None, ALU.add))
            own2.settle()
            own2.mark(dve.reciprocal(logit[:, :, :], logit[:, :, :]))
            own2.settle()
            dve.wait_ge(S["ffn_const"], 7)

            def do(ins):
                own2.mark(ins)
                own2.settle()

            def gates(f, ahead):
                score = logit[:, f.seq(f.s0 + ahead), :].rearrange("p (t e) -> p t e", e=NE)
                own2.mark(dve.tensor_tensor(sel[:, :, :], score, rb[:, :].unsqueeze(1).to_broadcast([P, NT, NE]), ALU.add))
                own2.settle(passed["dve"])
                for t in range(NT):
                    own2.mark(dve.max(top[:, t, :], sel[:, t, :]))
                own2.settle(passed["dve"])
                for t in range(NT):
                    own2.mark(dve.max_index(top_i[:, t, :], top[:, t, :], sel[:, t, :]))
                own2.settle()
                do(dve.tensor_copy(top_f[:, :, :], top_i[:, :, 0:2]))
                it = iota_f[:, :].unsqueeze(1).to_broadcast([P, NT, NE])
                for k in range(2):
                    own2.mark(dve.tensor_tensor(is_top[:, k], it, top_f[:, :, k:k + 1].to_broadcast([P, NT, NE]),
                                                ALU.is_equal))
                own2.settle()
                do(dve.tensor_tensor(in_two[:, :, :], is_top[:, 0], is_top[:, 1], ALU.add))
                do(dve.tensor_tensor(chosen[:, :, :], in_two[:, :, :], score, ALU.mult))
                do(dve.tensor_reduce(total[:, :], chosen[:, :, :], AX.X, ALU.add))
                own2.mark(dve.tensor_scalar(normal[:, :], total[:, :], 1e-9, None, ALU.is_gt))
                do(dve.tensor_scalar(total_e[:, :], total[:, :], 1e-9, None, ALU.add))
                own2.mark(dve.tensor_scalar(even[:, :], normal[:, :], -0.5, 0.5, ALU.mult, ALU.add))
                do(dve.reciprocal(total[:, :], total_e[:, :]))
                do(dve.tensor_tensor(total[:, :], total[:, :], normal[:, :], ALU.mult))
                own2.mark(dve.tensor_tensor(gate_n[:, :, :], chosen[:, :, :],
                                            total[:, :].unsqueeze(2).to_broadcast([P, NT, NE]), ALU.mult))
                do(dve.tensor_tensor(gate_r[:, :, :], in_two[:, :, :],
                                     even[:, :].unsqueeze(2).to_broadcast([P, NT, NE]), ALU.mult))
                do(dve.tensor_tensor(gate[:, :, :], gate_n[:, :, :], gate_r[:, :, :], ALU.add))
                need(dve, S["gateT_full"], f.at(ahead, 1))
                do(dve.tensor_copy(gate3[:, :, 0:NE], gate[:, :, :]))
                do(dve.tensor_tensor(gate_r[:, :, :], gate[:, :, :], gate3[:, :, 0:NE], ALU.subtract))
                do(dve.tensor_copy(gate3[:, :, NE:2 * NE], gate_r[:, :, :]))
                dve.tensor_tensor(gate3[:, :, 2 * NE:3 * NE], gate_r[:, :, :], gate3[:, :, NE:2 * NE],
                                  ALU.subtract).then_inc(S["chosen_ready"], 1)

            def end_stats(f, s):
                dve.wait_ge(S["f_tok_full"], f.at(s + 1, 1))
                need(dve, S["z4_ready"], f.at(s, 1))
                dve.tensor_copy(f_tok, ps_misc[:, :]).then_inc(S["f_tok_ready"], 1)
                dve.wait_ge(S["f_tok_ready"], f.at(s + 1, 1))
                for i in range(NT):
                    own2.mark(dve.bn_stats(st2[:, i, :], f_tok[:, i * P:i * P + P]))
                own2.settle(passed["dve"])
                for i in range(NT):
                    last = dve.bn_aggr(mv2[:, i, :], st2[:, i, :])
                    if i < NT - 1:
                        own2.mark(last)
                last.then_inc(S["stats4"], 1)

            def end_z(f, s):
                dve.wait_ge(S["rstd4"], f.at(s + 1, 1))
                need(dve, S["out_ready"], f.at(s, 1))
                for i in range(NT):
                    last = dve.tensor_scalar(z[:, i, :], f_tok[:, i * P:i * P + P], mv2[:, i, 0:1], rs2[:, i:i + 1],
                                             ALU.subtract, ALU.mult)
                    if i < NT - 1:
                        own2.mark(last)
                last.then_inc(S["z4_ready"], 1)

            def back_needed(f, i, kind):
                need(dve, S["second_done"], f.at(i - 3, len(UNITS)))

            def ffn(f):
                own2.begin_ffn(f)
                if f.s0 == 0:
                    dve.wait_ge(S["av_full"], NGRP * NSEQ)
                for i, (kind, k) in enumerate(UNITS):
                    dve.wait_ge(S["act_ready"], f.at(i + 1, len(UNITS)))
                    back_needed(f, i, kind)
                    if kind == "c":
                        need(dve, S["hidden_ready"], f.at(i, len(UNITS)))
                        do(dve.scalar_tensor_tensor(silu2, tanh_u, 1.0, ps_wide[1][:, 0, :], ALU.add, ALU.mult))
                        dve.scalar_tensor_tensor(hidden[hid(f, i)], silu2, 0.5, ps_wide[1][:, 1, :], ALU.mult,
                                                 ALU.mult).then_inc(S["hidden_ready"], 1)
                    else:
                        dve.tensor_tensor(hidden[hid(f, i)], act_out[k % 2], ps_wide[0][:, k % 2, :],
                                          ALU.mult).then_inc(S["hidden_ready"], 1)
                    if i == 3 and f.s0 > 0:
                        end_stats(f, -1)
                    if i == 6 and f.s0 > 0:
                        end_z(f, -1)
                    if i == 7 and f.s0 < NSEQ - 1:
                        gates(f, 1)
                own2.end_ffn(f)

            gates(Ffn(0), 0)
            ffn_steps(dve, ffn)
            end_stats(Ffn(NSEQ - 1), 0)
            end_z(Ffn(NSEQ - 1), 0)

        @block.tensor
        def _(pe):
            def wide(st, what):
                _, unit = st.wide(what)
                need(pe, wide_free[unit], st.wide_before(what))
                return ps_wide[unit]

            def misc(st, what):
                need(pe, S["misc_free"], st.misc(what))
                return ps_misc

            def exp_unit(st, pr, n):
                i = 2 * NT * pr + n
                kt, b = n // 2, n % 2
                par = st.b % 2
                need(pe, S["exp_done"], st.at(2 * NPAIR * NT * st.b + i - 1, 2 * NPAIR * NT))
                if n == 0 and pr % 4 == 0:
                    pe.wait_ge(mrow[pr // 4], st.at(32 * (st.b + 1), 32))
                w = WIDTH[kt]
                r = slice(64 * b, 64 * b + K_EXP)
                pe.matmul(ps_exp[b][:, 0:w], ks[par][r, pr, P * kt:P * kt + P], qs[par][r, pr, P * kt:SEQ],
                          start=True, stop=True).then_inc(S["exp_full"], 1)

            def s_unit(st, i):
                pr, qt = i // NT, i % NT
                par = st.a % 2
                if i == 0:
                    pe.wait_ge(stacks[par], st.at(256 * (st.a // 2 + 1), 128))
                    if st.t0 < 2:
                        pe.wait_ge(S["k_rows"], 2 * st.t0 + 2)
                        pe.wait_ge(S["q_rows"], 2 * st.t0 + 2)
                u = wide(st, f"s{i}")
                w = P * (qt + 1)
                lo = max(w - DIAG, 0)
                for b in range(2):
                    r = slice(64 * b, 64 * b + K_MAX)
                    pe.matmul(u[:, b, 0:w], qs[par][r, pr, P * qt:P * qt + P], ks[par][r, pr, 0:w],
                              start=True, stop=False)
                for b in range(2):
                    last = pe.matmul(u[:, b, lo:w], identb[:, :], maskb[:, DIAG - (w - lo):DIAG],
                                     start=False, stop=True)
                last.then_inc(S["wide_full"], 1)

            def av_part(st, g, kt):
                par = st.b % 2
                n = NPAIR * NT * st.b
                pe.wait_ge(S["p_masked"], st.at(n + NT * (2 * g + 1) + kt + 1, NPAIR * NT))
                if kt == 0:
                    need(pe, S["av_copied"], st.at(NGRP * st.b + g, NGRP))
                    if g == 0:
                        pe.wait_ge(S["v_ready"], st.at(2 * st.b + 1, 2))
                w = WIDTH[kt]
                for j in range(4):
                    pr, b = 2 * g + j // 2, j % 2
                    last = pe.matmul(ps_av[32 * j:32 * j + 32, P * kt:SEQ], vp[par][:, kt, 4 * g + j, :],
                                     prob[pr % PBUF][:, b, START[kt]:START[kt] + w],
                                     start=(kt == 0), stop=(kt == NT - 1))
                if kt == NT - 1:
                    last.then_inc(S["av_full"], 1)

            def transposes(dst, src, unit, done):
                for i in range(NT):
                    last = pe.transpose(dst(i), src(i), unit)
                last.then_inc(done, 1)

            def x_transpose(st):
                u = wide(st, "xT")
                pe.wait_ge(S["xn_ready"], st.at(st.a + 1, 1))
                transposes(lambda i: u[:, 0, i * P:i * P + P], lambda i: xn[:, i, :], ident[:, :], S["wide_full"])

            def qk(st):
                u = wide(st, "qk")
                pe.wait_ge(wide_free[st.wide("xT")[1]], st.wide_before("xT") + 1)
                pe.matmul(u[:, 0, :], wq[:, :], xnT[:, 1:1 + SEQ], start=True, stop=True)
                pe.matmul(u[:, 1, :], wk[:, :], xnT[:, 1:1 + SEQ], start=True, stop=True).then_inc(S["wide_full"], 1)

            def values(st):
                u = wide(st, "v")
                for n in range(2):
                    for i in range(NT):
                        last = pe.matmul(u[:, n, i * P:i * P + P], xnT[:, 1 - n + i * P:1 - n + i * P + P], wv[:, :],
                                         start=True, stop=True)
                last.then_inc(S["wide_full"], 1)

            def o_transpose(st):
                u = wide(st, "oT")
                pe.wait_ge(S["o_ready"], st.at(NGRP * (st.c + 1), NGRP))
                transposes(lambda i: u[:, 0, i * P:i * P + P], lambda i: o_tok[:, i, :], ident[:, :], S["wide_full"])

            def o_proj(st):
                u = wide(st, "oproj")
                pe.wait_ge(wide_free[st.wide("oT")[1]], st.wide_before("oT") + 1)
                for i in range(NT):
                    last = pe.matmul(u[:, 0, i * P:i * P + P], oT[:, i * P:i * P + P], wo[:, :], start=True, stop=True)
                last.then_inc(S["wide_full"], 1)

            def e_sums(st):
                m = misc(st, "e_sums")
                pe.wait_ge(S["e_ready"], st.at(2 * (st.a + 1), 2))
                pe.matmul(m[0:32, :], head_sum[:, :], e0[:, :], start=True, stop=True)
                pe.matmul(m[32:64, :], head_sum[:, :], e1[:, :], start=True, stop=True).then_inc(S["misc_full"], 1)

            def s_tok_transpose(st):
                m = misc(st, "s_tok")
                pe.sem_inc(passed["pe"], 1)
                transposes(lambda i: m[:, i * 64:i * 64 + 64], lambda i: s_rows[:, i * P:i * P + P],
                           ident[0:64, 0:64], S["misc_full"])

            def m_transpose(st, half):
                m = misc(st, f"m{half}")[:, :].bitcast(F16)
                pe.wait_ge(S["m16_ready"], st.at(2 * st.a + half + 1, 2))
                transposes(lambda i: m[0:H // 2, i * P:i * P + P], lambda i: m16[:, i, half * 8:half * 8 + 8],
                           ident16[:, :], S["misc_full"])

            def av_transpose(st, g):
                m = misc(st, f"av{g}")
                pe.wait_ge(S["av_copied"], st.at(NGRP * st.b + g + 1, NGRP))
                transposes(lambda i: m[:, i * P:i * P + P], lambda i: av_s[g % 2][:, i * P:i * P + P],
                           ident[:, :], S["misc_full"])

            def xn2_transpose(st):
                m = misc(st, "xn2")
                pe.wait_ge(S["xn2_ready"], st.at(st.c + 1, 1))
                transposes(lambda i: m[:, i * P:i * P + P], lambda i: xn2[:, i, :], ident[:, :], S["misc_full"])

            def logits(st):
                m = misc(st, "logits")
                for i in range(NT):
                    last = pe.matmul(m[:, i * NE:i * NE + NE], xn2T[:, i * P:i * P + P], rwT[:, :],
                                     start=True, stop=True)
                last.then_inc(S["misc_full"], 1)

            def step(st):
                s_next = 0
                for pr in range(NPAIR):
                    for n in range(2 * NT):
                        if st.B:
                            exp_unit(st, pr, n)
                        if st.A and (pr, n) == (0, 3):
                            x_transpose(st)
                        if st.C and (pr, n) == (0, 6):
                            o_transpose(st)
                        if st.A and (pr, n) == (1, 0):
                            qk(st)
                        if st.C and (pr, n) == (1, 3):
                            o_proj(st)
                        if st.A and (pr, n) == (1, 7):
                            values(st)
                        if st.A and (pr, n) == (2, 4):
                            e_sums(st)
                        if st.B and pr >= 2 and n % 2 == 1:
                            g, part = (pr - 2) // 2, (pr % 2) * 4 + n // 2
                            if part % 2 == 0:
                                av_part(st, g, part // 2)
                        if st.A and pr >= 3 and (8 * (pr - 3) + n) % 5 != 4:
                            s_unit(st, s_next)
                            s_next += 1
                        if st.B and (pr, n) == (4, 2):
                            av_transpose(st, 0)
                        if st.B and (pr, n) == (6, 2):
                            av_transpose(st, 1)
                        if st.A and (pr, n) == (6, 3):
                            s_tok_transpose(st)
                        if st.C and (pr, n) == (6, 4):
                            xn2_transpose(st)
                        if st.A and (pr, n) == (7, 2):
                            m_transpose(st, 0)
                if st.B:
                    av_transpose(st, 2)
                if st.C:
                    logits(st)
                if st.A:
                    m_transpose(st, 1)
                if st.B:
                    for kt in range(NT):
                        av_part(st, 3, kt)
                    av_transpose(st, 3)

            pe.wait_ge(S["const_ready"], N_CONST)
            steps(pe, step)

            def gate_transpose(f, ahead):
                pe.wait_ge(S["chosen_ready"], f.at(ahead + 1, 1))
                need(pe, S["f_tok_ready"], f.at(ahead - 1, 1))
                pe.sem_inc(passed["pe"], 1)
                m = ps_misc[:, :].bitcast(BF16)
                for i in range(NT):
                    last = pe.transpose(m[0:64, i * P:i * P + P], gate3[:, i, :], identb[:, :])
                last.then_inc(S["gateT_full"], 1)

            def first(f, i):
                kind, k = UNITS[i]
                xe = xeT[f.s0 % 2]
                n = len(UNITS)
                if i == 0:
                    pe.wait_ge([S["xe_loaded0"], S["xe_loaded1"]][f.s0 % 2],
                               16 * (f.s0 // 2 + 1) if f.u is None else f.u * 16 + 16 * (f.s0 // 2 + 1))
                if kind == "c":
                    other = UNITS.index(("c", 1 - k)) + 1
                    need(pe, S["hidden_ready"], f.at(other if k else other - n, n))
                    cols = slice(k * P, k * P + P)
                    pe.matmul(ps_wide[1][:, 0, :], sw1_s[:, cols], xe, start=True, stop=True)
                    pe.matmul(ps_wide[1][:, 1, :], sw3_s[:, cols], xe, start=True, stop=True).then_inc(S["front_full"], 1)
                else:
                    before = EXPERT_POS[k - 2] + 1
                    need(pe, S["hidden_ready"], f.at(before if k >= 2 else before - n, n))
                    if k == 0:
                        pe.wait_ge(S["gateT_ready"], f.at(1, 1))
                    pe.matmul(ps_wide[0][:, k % 2, :], sel_e[:, k, :], gateT[:, :], start=True, stop=True)
                    pe.matmul(ps_exp[k % 2][:, :], ew1_s[:, k, :], xe, start=True, stop=True).then_inc(S["front_full"], 1)

            def second(f, i):
                kind, k = UNITS[i]
                n = len(UNITS)
                pe.wait_ge(S["hidden_ready"], f.at(i + 1, n))
                if i == 0:
                    need(pe, S["fT_ready"], f.at(0, 1))
                w = sw2_s[:, k, :] if kind == "c" else ew2_s[:, k, :]
                last = pe.matmul(ps_av[:, :], w, hidden[hid(f, i)], start=(i == 0), stop=(i == n - 1))
                last.then_inc(S["second_done"], 1)

            def end_transpose(f, s):
                pe.wait_ge(S["fT_ready"], f.at(s + 1, 1))
                pe.wait_ge(S["gateT_ready"], f.at(min(s + 2, 1), 1))
                for i in range(NT):
                    last = pe.transpose(ps_misc[:, i * P:i * P + P], fT[:, i * P:i * P + P], ident[:, :])
                last.then_inc(S["f_tok_full"], 1)

            def ffn(f):
                n = len(UNITS)
                if f.s0 == 0:
                    pe.wait_ge(S["ffn_loaded"], 16 * 5)
                    pe.wait_ge(S["ffn_const"], 7)
                    gate_transpose(f, 0)
                for i in range(n):
                    first(f, i)
                    if i == 2 and f.s0 > 0:
                        end_transpose(f, -1)
                    if i == n - 1 and f.s0 < NSEQ - 1:
                        gate_transpose(f, 1)
                    if i >= LAG:
                        second(f, i - LAG)
                for i in range(n - LAG, n):
                    second(f, i)

            ffn_steps(pe, ffn)
            end_transpose(Ffn(NSEQ - 1), 0)


_INS = ["L0_attn_x", "L0_attn_W_q", "L0_attn_b_q", "L0_attn_W_k", "L0_attn_b_k", "L0_attn_W_v", "L0_attn_b_v",
        "L0_attn_W_o", "L0_attn_b_o", "L0_attn_rel_k_table", "L0_attn_rel_v_table", "L0_ffn_router_w",
        "L0_ffn_router_bias", "L0_ffn_sw1", "L0_ffn_sw3", "L0_ffn_sw2", "L0_ffn_ew1", "L0_ffn_ew2"]


def kernel(**inputs):
    import concourse.bacc as bacc
    from concourse.bass_utils import run_bass_kernel_spmd

    nc = bacc.Bacc("TRN2", target_bir_lowering=False, num_devices=1)
    arrays, args = {}, []
    for name in _INS:
        a = np.ascontiguousarray(inputs[name])
        arrays[name] = a
        args.append(nc.dram_tensor(name, a.shape, mybir.dt.from_np(a.dtype), kind="ExternalInput").ap())
    args.append(nc.dram_tensor("out", (NSEQ, SEQ, P), F32, kind="ExternalOutput").ap())
    block_kernel(nc, *args)
    r = run_bass_kernel_spmd(nc, [arrays], core_ids=[0])
    return r.results[0]["out"]
```

```python
from contextlib import ExitStack

import numpy as np
import concourse.bass as bass
from concourse import mybir

F32 = mybir.dt.float32
F16 = mybir.dt.float16
BF16 = mybir.dt.bfloat16
U32 = mybir.dt.uint32
ALU = mybir.AluOpType
ACT = mybir.ActivationFunctionType
AX = mybir.AxisListType

P = 128
NSEQ, SEQ = 16, 512
NT = SEQ // P
H, D = 16, 8
NPAIR, NGRP = H // 2, H // 4
SCALE = float(D) ** -0.5
EPS = 1e-5
M_UNIT = 16.0
MASKED = -1e30
TERMS = 4
STACK = TERMS * D
M_ROW = P - 2
PBUF = 4
NE, HR, HS = 8, 128, 256
NC = HS // P
DIAG = P + 1

WIDTH = [SEQ - P * kt for kt in range(NT)]
START = [sum(WIDTH[:kt]) for kt in range(NT)]
PCOLS = sum(WIDTH)

SLOTS = NPAIR * NT * 2
AT = {"av2": 2, "e_sums": 4, "m1": 6, "s_tok": 14, "av3": 18, "v": 22, "oT": 24, "xT": 26, "oproj": 29,
      "qk": 32, "av0": 34, "m0": 42, "av1": 50, "xn2": 54, "logits": 60}
STAGE = {"av2": "C", "e_sums": "A", "m1": "B", "s_tok": "A", "av3": "C", "v": "A", "oT": "C", "xT": "F",
         "oproj": "C", "qk": "F", "av0": "B", "m0": "A", "av1": "B", "xn2": "C", "logits": "C"}
STAGE.update({f"s{i}": "A" for i in range(NPAIR * NT)})
WIDE_ORDER = [what for _, what in sorted([(AT[w], w) for w in ("v", "oT", "xT", "oproj", "qk")]
                                         + [(2 * i + 1.5, f"s{i}") for i in range(NPAIR * NT)])]
MISC_ORDER = sorted((w for w in AT if w not in WIDE_ORDER), key=AT.get)
LOOP0, LOOP_STEPS = 3, NSEQ - 4 - (NSEQ - 4) % 2
CHAIN_DVE, CHAIN_POOL = 48, 7


class Step:

    def __init__(self, t0, u=None):
        self.t0, self.u = t0, u
        self.F, self.A, self.B, self.C = self._on(t0).values()
        self.f, self.a, self.b, self.c = t0, t0 - 1, t0 - 2, t0 - 3

    @staticmethod
    def _on(t):
        return {stage: 0 <= t - lag < NSEQ for lag, stage in enumerate("FABC")}

    def seq(self, s0):
        return s0 if self.u is None else self.u * 2 + s0

    def at(self, count, rate):
        return count if self.u is None else self.u * (2 * rate) + count

    def _uses(self, order, what):
        before = sum(self._on(t)[STAGE[w]] for t in range(self.t0) for w in order)
        return before + sum(self._on(self.t0)[STAGE[w]] for w in order[:order.index(what)])

    def misc(self, what):
        return self.at(self._uses(MISC_ORDER, what), len(MISC_ORDER))

    def wide(self, what):
        n = self._uses(WIDE_ORDER, what)
        return self.at(n, len(WIDE_ORDER)), n % 2

    def wide_before(self, what):
        n = self._uses(WIDE_ORDER, what) // 2
        return n if self.u is None else self.u * len(WIDE_ORDER) + n


def steps(eng, body):
    for t in range(LOOP0):
        body(Step(t))
    with eng.Fori(0, LOOP_STEPS // 2) as u:
        body(Step(LOOP0, u))
        body(Step(LOOP0 + 1, u))
    for t in range(LOOP0 + LOOP_STEPS, NSEQ + 3):
        body(Step(t))


class Ffn:

    def __init__(self, s0, u=None):
        self.s0, self.u = s0, u

    def seq(self, s0):
        return s0 if self.u is None else self.u * 2 + s0

    def at(self, extra, rate):
        n = rate * self.s0 + extra
        return n if self.u is None else self.u * (2 * rate) + n


def ffn_steps(eng, body):
    body(Ffn(0))
    body(Ffn(1))
    with eng.Fori(0, (NSEQ - 4) // 2) as u:
        body(Ffn(2, u))
        body(Ffn(3, u))
    body(Ffn(NSEQ - 2))
    body(Ffn(NSEQ - 1))


UNITS = [("c", 0), ("e", 0), ("e", 1), ("e", 2), ("c", 1)] + [("e", e) for e in range(3, NE)]
CHAIN_FFN = 38
LAG = 2
EXPERT_POS = [UNITS.index(("e", e)) for e in range(NE)]


def hid(f, i):
    return (f.s0 * len(UNITS) + i) % 4


class Own:

    def __init__(self, eng, sem, per_step):
        self.eng, self.sem, self.per_step, self.n, self.base = eng, sem, per_step, 0, None

    def begin(self, st):
        if st.t0 == LOOP0:
            self.loop0 = self.n
        if st.t0 == LOOP0 + LOOP_STEPS:
            self.n = self.loop0 + self.per_step * LOOP_STEPS
        self.st = st
        self.first = self.n

    def end_ffn(self, f):
        if 0 < f.s0 < NSEQ - 1 and self.per_step != self.n - self.first:
            raise AssertionError((self.n - self.first, self.per_step))

    def begin_ffn(self, f):
        if f.s0 == 2 and f.u is not None:
            self.loop0 = self.n
        if f.s0 == NSEQ - 2:
            self.n = self.loop0 + self.per_step * (NSEQ - 4)
        self.st, self.first = Step(0, f.u), self.n

    def end(self):
        if LOOP0 <= self.st.t0 < NSEQ and self.per_step != self.n - self.first:
            raise AssertionError((self.n - self.first, self.per_step))

    def mark(self, ins):
        ins.then_inc(self.sem, 1)
        self.n += 1

    def settle(self, apart=None):
        self.eng.wait_ge(self.sem, self.st.at(self.n, self.per_step))
        if apart is not None:
            self.eng.sem_inc(apart, 1)


def need(eng, sem, value):
    if not isinstance(value, int) or value > 0:
        eng.wait_ge(sem, value)


def wait_apart(eng, sem, value, passed):
    need(eng, sem, value)
    eng.sem_inc(passed, 1)


def block_kernel(nc, x, W_q, b_q, W_k, b_k, W_v, b_v, W_o, b_o, rel_k, rel_v,
                 router_w, router_bias, sw1, sw3, sw2, ew1, ew2, out):
    ctx = ExitStack()
    with ctx:
        def sb(name, shape, dt=F32):
            return ctx.enter_context(nc.sbuf_tensor(name, shape, dt))

        def sem(name):
            return ctx.enter_context(nc.semaphore(name))

        ident = sb("ident", [P, P])
        ident16 = sb("ident16", [P, P], F16)
        identb = sb("identb", [P, P], BF16)
        maskb = sb("maskb", [P, DIAG], BF16)
        head_sel = sb("head_sel", [P, D, NPAIR, 2])
        head_sum = sb("head_sum", [P, 32])
        wq_in = sb("wq_in", [P, P])
        wk_in = sb("wk_in", [P, P])
        wq = sb("wq", [P, P])
        wk = sb("wk", [P, P])
        wv = sb("wv", [P, P])
        wo = sb("wo", [P, P])
        rwT = sb("rwT", [P, NE])
        bq = sb("bq", [P, 1])
        bk_in = sb("bk_in", [P, 1])
        rk = sb("rk", [P, 3])
        bk = sb("bk", [P, 1])
        dk = sb("dk", [P, 2])
        bv_in = sb("bv_in", [P, P])
        rv = sb("rv", [P, 3, D])
        bv = sb("bv", [P, 3, P])
        bo = sb("bo", [P, P])
        rb = sb("rb", [P, NE])
        neg_half = sb("neg_half", [P, NT])
        xr = sb("xr", [P, NSEQ, SEQ])
        xnT_dram = nc.dram_tensor("xnT_dram", [NSEQ, P, SEQ], F32, kind="Internal").ap()
        logit = sb("logit", [P, NSEQ, NT * NE])
        st1 = sb("st1", [P, NT, 6])
        mv1 = sb("mv1", [P, NT, 2])
        var1 = sb("var1", [P, NT])
        rs1 = sb("rs1", [P, NT])
        xn = sb("xn", [P, NT, P])
        xnT = sb("xnT", [P, 1 + SEQ])
        qf = sb("qf", [P, SEQ])
        kf = sb("kf", [P, SEQ])
        qh = sb("qh", [P, SEQ], F16)
        ql = sb("ql", [P, SEQ], F16)
        kh = sb("kh", [P, SEQ], F16)
        kl = sb("kl", [P, SEQ], F16)
        e0 = sb("e0", [P, SEQ])
        e1 = sb("e1", [P, SEQ])
        s_rows = sb("s_rows", [64, SEQ])
        s_tok = sb("s_tok", [P, 2, NT, H])
        mx = sb("mx", [P, NT, H])
        mxa = sb("mxa", [P, NT, H])
        m16 = sb("m16", [P, NT, H], F16)
        d01 = sb("d01", [P, 2, NT, H])
        p01 = sb("p01", [P, 2, NT, H])
        mT = [sb(f"mT{i}", [H // 2, SEQ], F16) for i in range(2)]
        v_near = sb("v_near", [P, 2, NT, P])
        pv_near = v_near
        qs = [sb(f"qs{i}", [P, NPAIR, SEQ], F16) for i in range(2)]
        ks = [[sb(f"ks{i}{b}", [P, NPAIR, SEQ], F16) for b in range(2)] for i in range(2)]
        vp = [sb(f"vp{i}", [P, NT, H, 32]) for i in range(2)]
        near = [sb(f"near{i}", [P, NT, P]) for i in range(2)]
        p_near = [sb(f"p_near{i}", [P, NT, H]) for i in range(2)]
        prob = [sb(f"prob{i}", [P, 2, PCOLS]) for i in range(PBUF)]
        av_s = [sb(f"av_s{i}", [P, SEQ]) for i in range(2)]
        den = sb("den", [P, NT, 4])
        rden = sb("rden", [P, NT, 4])
        num = sb("num", [P, NT, 4, D])
        o_tok = sb("o_tok", [P, NT, P])
        oT = sb("oT", [P, SEQ])
        y = sb("y", [P, NT, P])
        st2 = sb("st2", [P, NT, 6])
        mv2 = sb("mv2", [P, NT, 2])
        var2 = sb("var2", [P, NT])
        rs2 = sb("rs2", [P, NT])
        z = y
        st3 = sb("st3", [P, NT, 6])
        mv3 = sb("mv3", [P, NT, 2])
        var3 = sb("var3", [P, NT])
        rs3 = sb("rs3", [P, NT])
        xn2 = y
        xn2T = oT

        spare = [t[:, :, :].bitcast(F32) for t in (ks[0][0], ks[0][1])]
        sw1_s, sw3_s = spare[0][:, 0, :], spare[0][:, 1, :]
        sw2_s = spare[0][:, 2, :].rearrange("p (c d) -> p c d", c=NC)
        ew1_s = spare[0][:, 3:7, :].rearrange("p a (e d) -> p (a e) d", e=2)
        ew2_s = spare[1][:, 0:4, :].rearrange("p a (e d) -> p (a e) d", e=2)
        sel_e = sb("sel_e", [64, NE, P], BF16)
        iota_i = sb("iota_i", [P, NE], mybir.dt.int32)
        iota_f = sb("iota_f", [P, NE])
        sel = sb("sel", [P, NT, NE])
        top = sb("top", [P, NT, 8])
        top_i = sb("top_i", [P, NT, 8], U32)
        top_f = sb("top_f", [P, NT, 2])
        is_top = sb("is_top", [P, 2, NT, NE])
        in_two = sb("in_two", [P, NT, NE])
        chosen = sb("chosen", [P, NT, NE])
        total = sb("total", [P, NT])
        total_e = sb("total_e", [P, NT])
        normal = sb("normal", [P, NT])
        even = sb("even", [P, NT])
        gate = sb("gate", [P, NT, NE])
        gate_n = sb("gate_n", [P, NT, NE])
        gate_r = sb("gate_r", [P, NT, NE])
        gate3 = sb("gate3", [P, NT, 64], BF16)
        gateT = sb("gateT", [64, SEQ], BF16)
        xeT = [prob[0][:, 0, i * SEQ:(i + 1) * SEQ] for i in range(2)]
        act_out = [prob[1][:, 0, i * SEQ:(i + 1) * SEQ] for i in range(2)]
        tanh_u = prob[2][:, 0, 0:SEQ]
        silu2 = prob[2][:, 0, SEQ:2 * SEQ]
        hidden = [prob[3][:, i // 2, (i % 2) * SEQ:(i % 2 + 1) * SEQ] for i in range(4)]
        fT = prob[1][:, 1, 0:SEQ]
        f_tok = prob[2][:, 1, 0:SEQ]
        result = prob[0][:, 1, 0:SEQ]

        ps_exp = [ctx.enter_context(nc.psum_tensor(f"ps_exp{i}", [P, SEQ], F32)) for i in range(2)]
        ps_wide = [ctx.enter_context(nc.psum_tensor(f"ps_wide{i}", [P, 2, SEQ], F32)) for i in range(2)]
        ps_av = ctx.enter_context(nc.psum_tensor("ps_av", [P, SEQ], F32))
        ps_misc = ctx.enter_context(nc.psum_tensor("ps_misc", [P, SEQ], F32))

        names = """attn_loaded const_made const_ready x_loaded0 x_loaded1 x_loaded2 dve_own pool_own wide_full wide_free0 wide_free1
            misc_full misc_free stats1 rstd1 xn_ready qk_ready qk_split e_ready
            stacks00 stacks01 stacks10 stacks11 v_ready near_ready k_rows q_rows m16_ready mrow0 mrow1 d_ready p_ready
            exp_full exp_done p_masked av_full av_copied o_ready stats2 rstd2 z_ready
            x1_ready stats3 rstd3 xn2_ready xnT_stored
            ffn_loaded ffn_const attn_over xe_loaded0 xe_loaded1 logits_exp chosen_ready gateT_full gateT_ready front_full
            uv_full tanh_ready act_ready hidden_ready uv_free gates_full second_done fT_ready f_tok_full f_tok_ready
            passed_sp passed_pool passed_dve passed_pe stats4 rstd4 z4_ready out_ready stored dve_own2 pool_own2""".split()
        S = {n: sem(n) for n in names}
        x_loaded = [S["x_loaded0"], S["x_loaded1"], S["x_loaded2"]]
        stacks = [[S[f"stacks{par}{half}"] for half in range(2)] for par in range(2)]
        mrow = [S["mrow0"], S["mrow1"]]

        wide_free = [S["wide_free0"], S["wide_free1"]]

        N_ATTN_LOADS = 4 + 1 + 8 + 12 + 4
        N_CONST_MADE, N_POOL_CONST, N_CONST = 9, 8, 8 + 10
        x_v = x.rearrange("b (i p) d -> p b i d", p=P)
        out_v = out.rearrange("b (i p) d -> p b i d", p=P)

        def split_heads(v):
            return v.rearrange("(hf p4 b d) -> b hf d p4", hf=2, b=2, d=D)

        passed = {n: S["passed_" + n] for n in ("sp", "pool", "dve", "pe")}

        block = ctx.enter_context(nc.Block())

        @block.sync
        def _(sp):
            def load(dst, src):
                sp.dma_start(dst, src, allow_slow_non_contiguous=True).then_inc(S["attn_loaded"], 16)

            sp.dma_start(xr[:, 0, :].rearrange("p (i d) -> p i d", i=NT), x_v[:, 0]).then_inc(x_loaded[0], 16)
            for dst, src in ((wq_in, W_q), (wk_in, W_k), (wv, W_v), (wo, W_o)):
                load(dst[:, :], src)
            load(rwT[:, :], router_w.rearrange("e d -> d e"))
            for dst, src in ((bq, b_q), (bk_in, b_k)):
                for c in range(4):
                    load(dst[32 * c:32 * c + 32, :], split_heads(src)[c // 2, c % 2])
            for r in range(3):
                for lo in range(0, P, 32):
                    load(rk[lo:lo + 32, r:r + 1],
                         rel_k[r, :].rearrange("(d o) -> d o", o=1).to_broadcast([D, NPAIR // 2]))
            load(bv_in[:, :], b_v.partition_broadcast(P))
            load(bo[:, :], b_o.partition_broadcast(P))
            load(rv[:, :, :], rel_v[0:3, :].partition_broadcast(P))
            load(rb[:, :], router_bias.partition_broadcast(P))

            sp.dma_start(xr[:, 1, :].rearrange("p (i d) -> p i d", i=NT), x_v[:, 1]).then_inc(x_loaded[1], 16)

            def stacks_out(st, s, half):
                par, prs = s % 2, slice(4 * half, 4 * half + 4)
                if st.u is None and s < 2:
                    sp.wait_ge(S["k_rows"], 4 * s + 4)
                    sp.wait_ge(S["q_rows"], s + 1)
                for stks, parts in (((qs[par], qs[par]), (qh, qh, ql, ql)), (ks[par], (kh, kl, kh, kl))):
                    for b, stk in enumerate(stks):
                        for r, part in enumerate(parts):
                            lo = 64 * b + D * r
                            src = 64 * b + 32 * half
                            sp.dma_start(stk[lo:lo + D, prs, :], part[src:src + 32, :]).then_inc(stacks[par][half], 16)

            def maxima_out(st, s, half):
                wait_apart(sp, S["misc_free"], st.misc(f"m{half}") + 1, passed["sp"])
                for b in range(2):
                    row = M_ROW + b
                    sp.dma_start(qs[s % 2][row:row + 1, 4 * half:4 * half + 4, :],
                                 mT[half][b:H // 2:2, :]).then_inc(mrow[half], 16)

            def step(st):
                if st.t0 == 0:
                    sp.dma_start(xr[:, 2:, :].rearrange("p b (i d) -> p b i d", i=NT),
                                 x_v[:, 2:]).then_inc(x_loaded[2], 16)
                if st.A:
                    need(sp, S["exp_full"], st.at(SLOTS * (st.a - 1), SLOTS))
                    stacks_out(st, st.a, 1)
                if st.B:
                    maxima_out(st, st.b, 1)
                if st.t0 == NSEQ + 1:
                    sp.wait_ge(S["exp_full"], SLOTS * (NSEQ - 1))
                    for dst, src in ((sw1_s, sw1), (sw3_s, sw3), (sw2_s, sw2.rearrange("(c p) d -> p c d", p=P)),
                                     (ew1_s, ew1.rearrange("e d h -> d e h")), (ew2_s, ew2.rearrange("e h d -> h e d"))):
                        sp.dma_start(dst, src).then_inc(S["ffn_loaded"], 16)
                if st.F:
                    wait_apart(sp, S["qk_split"], st.at(2 * (st.f + 1), 2), passed["sp"])
                    need(sp, S["exp_full"], st.at(SLOTS * (st.f - 2) + SLOTS // 2, SLOTS))
                    stacks_out(st, st.f, 0)
                if st.A:
                    maxima_out(st, st.a, 0)
                if st.C:
                    wait_apart(sp, S["misc_free"], st.misc("xn2") + 1, passed["sp"])
                    sp.dma_start(xnT_dram[st.seq(st.c)], xn2T[:, :]).then_inc(S["xnT_stored"], 16)

            steps(sp, step)

            xe_loaded = [S["xe_loaded0"], S["xe_loaded1"]]

            def load_xe(s, s0, par):
                sp.dma_start(xeT[par], xnT_dram[s]).then_inc(xe_loaded[par], 16)

            sp.wait_ge(S["av_full"], NGRP * NSEQ)
            sp.wait_ge(S["xnT_stored"], 16 * NSEQ)
            load_xe(0, 0, 0)
            load_xe(1, 1, 1)

            def ffn(f):
                if f.s0 + 2 < NSEQ:
                    wait_apart(sp, S["front_full"], f.at(NE + NC, NE + NC), passed["sp"])
                    load_xe(f.seq(f.s0 + 2), 0, f.s0 % 2)
                wait_apart(sp, S["out_ready"], f.at(1, 1), passed["sp"])
                sp.dma_start(out_v[:, f.seq(f.s0)], result.rearrange("p (i d) -> p i d", i=NT)).then_inc(S["stored"], 16)

            ffn_steps(sp, ffn)
            sp.wait_ge(S["stored"], 16 * NSEQ)

        @block.gpsimd
        def _(pool):
            def zeros(ins):
                ins.then_inc(S["const_made"], 1)

            zeros(pool.memset(ident[:, :], 0.0))
            zeros(pool.memset(ident16[:, :], 0.0))
            zeros(pool.memset(identb[:, :], 0.0))
            zeros(pool.memset(maskb[:, :], 0.0))
            zeros(pool.memset(head_sel[:, :, :, :], 0.0))
            zeros(pool.memset(neg_half[:, :], -0.5))
            zeros(pool.memset(e1[:, 0:1], MASKED / D))
            zeros(pool.memset(xnT[:, 0:1], 0.0))
            zeros(pool.memset(head_sum[:, :], 0.0))
            pool.wait_ge(S["const_made"], N_CONST_MADE)
            for m in (ident, ident16, identb):
                pool.affine_select(out=m[:, :], in_=m[:, :], compare_op=ALU.not_equal, fill=1.0, base=0,
                                   pattern=[[-1, P]], channel_multiplier=1).then_inc(S["const_ready"], 1)
            pool.affine_select(out=maskb[:, :], in_=maskb[:, :], compare_op=ALU.is_ge, fill=MASKED, base=-1,
                               pattern=[[-1, DIAG]], channel_multiplier=1).then_inc(S["const_ready"], 1)
            for half in range(2):
                v = head_sel[:, :, 4 * half:4 * half + 4, :]
                pool.affine_select(out=v, in_=v, compare_op=ALU.not_equal, fill=1.0, base=-32 * half,
                                   pattern=[[-4, D], [-1, NPAIR // 2], [-64, 2]],
                                   channel_multiplier=1).then_inc(S["const_ready"], 1)
            for i in range(2):
                pool.memset(vp[i][:, :, :, :], 0.0).then_inc(S["pool_own"], 1)
            pool.wait_ge(S["pool_own"], 2)
            for i in range(2):
                pool.memset(vp[i][:, :, :, D:D + 1], 1.0).then_inc(S["const_ready"], 1)

            pool.wait_ge(S["const_ready"], N_POOL_CONST)
            for i in range(2):
                for b in range(2):
                    pool.memset(ks[i][b][:, :, :].bitcast(F32), 0.0).then_inc(S["k_rows"], 1)
                for b in range(2):
                    pool.wait_ge(S["k_rows"], 4 * i + 2 + b)
                    v = ks[i][b][96:P, :, :]
                    pool.affine_select(out=v, in_=v, compare_op=ALU.not_equal, fill=-M_UNIT, base=96 - M_ROW - b,
                                       pattern=[[0, NPAIR], [0, SEQ]], channel_multiplier=1).then_inc(S["k_rows"], 1)
                pool.wait_ge(S["k_rows"], 4 * i + 4)

            pool.memset(sel_e[:, :, :], 0.0).then_inc(S["ffn_const"], 1)
            pool.iota(iota_i[:, :], pattern=[[1, NE]], base=0, channel_multiplier=0).then_inc(S["ffn_const"], 1)
            pool.memset(gate3[:, :, :], 0.0).then_inc(S["ffn_const"], 1)
            for r in range(3):
                pool.wait_ge(S["ffn_const"], 3 + r)
                pool.affine_select(out=sel_e[:, :, :], in_=sel_e[:, :, :], compare_op=ALU.not_equal, fill=1.0,
                                   base=-NE * r, pattern=[[-1, NE], [0, P]],
                                   channel_multiplier=1).then_inc(S["ffn_const"], 1)
            pool.wait_ge(S["ffn_const"], 6)
            pool.tensor_copy(iota_f[:, :], iota_i[:, :]).then_inc(S["ffn_const"], 1)

            own = Own(pool, S["pool_own"], CHAIN_POOL)
            own.n = 2

            def rstd(st, seq, mv, var, rs, got, done):
                wait_apart(pool, S[got], st.at(seq + 1, 1), passed["pool"])
                own.mark(pool.tensor_scalar(var[:, :], mv[:, :, 1], 1.0, EPS, ALU.mult, ALU.add))
                own.settle()
                pool.tensor_tensor(rs[:, :], var[:, :], neg_half[:, :], ALU.pow).then_inc(S[done], 1)

            def mask_pair(st, pr):
                for kt in range(NT):
                    wait_apart(pool, S["exp_done"],
                               st.at(2 * NPAIR * NT * st.b + 2 * NT * pr + 2 * kt + 2, 2 * NPAIR * NT), passed["pool"])
                    w = min(DIAG, WIDTH[kt])
                    v = prob[pr % PBUF][:, :, START[kt]:START[kt] + w]
                    pool.affine_select(out=v, in_=v, compare_op=ALU.is_ge, fill=0.0, base=-2,
                                       pattern=[[0, 2], [1, w]], channel_multiplier=-1).then_inc(S["p_masked"], 1)

            def near_half(st, s, half):
                pool.wait_ge(S["p_ready"], st.at(2 * s + half + 1, 2))
                if half == 0:
                    pool.wait_ge(S["v_ready"], st.at(2 * (s + 1), 2))
                    pool.wait_ge(wide_free[st.wide("v")[1]], st.wide_before("v") + 1)
                    need(pool, S["o_ready"], st.at(NGRP * (s - 1), NGRP))
                hs = slice(half * 8, half * 8 + 8)
                cols = slice(half * 64, half * 64 + 64)
                for n in range(2):
                    a = v_near[:, n, :, cols].rearrange("p t (h d) -> p t h d", d=D)
                    o = pv_near[:, n, :, cols].rearrange("p t (h d) -> p t h d", d=D)
                    pb = p01[:, n, :, hs].unsqueeze(3).to_broadcast([P, NT, 8, D])
                    own.mark(pool.tensor_tensor(o, a, pb, ALU.mult))
                pool.tensor_tensor(p_near[s % 2][:, :, hs], p01[:, 0, :, hs], p01[:, 1, :, hs],
                                   ALU.add).then_inc(S["near_ready"], 1)
                own.settle()
                pool.tensor_tensor(near[s % 2][:, :, cols], pv_near[:, 0, :, cols], pv_near[:, 1, :, cols],
                                   ALU.add).then_inc(S["near_ready"], 1)

            def step(st):
                own.begin(st)
                if st.F:
                    rstd(st, st.f, mv1, var1, rs1, "stats1", "rstd1")
                if st.B:
                    near_half(st, st.b, 1)
                    for pr in range(4):
                        mask_pair(st, pr)
                if st.C:
                    rstd(st, st.c, mv2, var2, rs2, "stats2", "rstd2")
                    pool.wait_ge(S["z_ready"], st.at(st.c + 1, 1))
                    xv = xr[:, st.seq(st.c), :]
                    pool.tensor_tensor(xv, xv, z[:, :, :].rearrange("p i d -> p (i d)"),
                                       ALU.add).then_inc(S["x1_ready"], 1)
                if st.B:
                    mask_pair(st, 4)
                if st.C:
                    rstd(st, st.c, mv3, var3, rs3, "stats3", "rstd3")
                if st.A:
                    near_half(st, st.a, 0)
                if st.B:
                    for pr in (5, 6, 7):
                        mask_pair(st, pr)
                own.end()

            steps(pool, step)

            own2 = Own(pool, S["pool_own2"], 1)

            def end_of(f, seq, st0):
                wait_apart(pool, S["stats4"], f.at(st0 + 1, 1), passed["pool"])
                own2.mark(pool.tensor_scalar(var2[:, :], mv2[:, :, 1], 1.0, EPS, ALU.mult, ALU.add))
                own2.settle()
                pool.tensor_tensor(rs2[:, :], var2[:, :], neg_half[:, :], ALU.pow).then_inc(S["rstd4"], 1)
                pool.wait_ge(S["z4_ready"], f.at(st0 + 1, 1))
                need(pool, S["stored"], f.at(16 * st0, 16))
                pool.tensor_tensor(result, xr[:, seq, :], z[:, :, :].rearrange("p i d -> p (i d)"),
                                   ALU.add).then_inc(S["out_ready"], 1)

            def ffn(f):
                own2.begin_ffn(f)
                if f.s0 > 0:
                    end_of(f, f.seq(f.s0 - 1), -1)
                own2.end_ffn(f)

            ffn_steps(pool, ffn)
            end_of(Ffn(NSEQ - 1), NSEQ - 1, 0)

        @block.scalar
        def _(act):
            def exp_unit(st, pr, n):
                i = 2 * NT * pr + n
                kt, b = n // 2, n % 2
                act.wait_ge(S["exp_full"], st.at(2 * NPAIR * NT * st.b + i + 1, 2 * NPAIR * NT))
                if n == 0 and pr % 2 == 0:
                    need(act, S["av_full"], st.at(NGRP * st.b + pr // 2 - 1, NGRP))
                w = WIDTH[kt]
                act.activation(prob[pr % PBUF][:, b, START[kt]:START[kt] + w], ps_exp[b][:, 0:w], ACT.Exp,
                               scale=SCALE).then_inc(S["exp_done"], 1)

            def xT_out(st):
                n, unit = st.wide("xT")
                act.wait_ge(S["wide_full"], n + 1)
                act.copy(xnT[:, 1:1 + SEQ], ps_wide[unit][:, 0, :]).then_inc(wide_free[unit], 1)

            def qk_out(st):
                n, unit = st.wide("qk")
                act.wait_ge(S["wide_full"], n + 1)
                if st.t0 == 0:
                    act.wait_ge(S["const_ready"], N_CONST)
                if st.f > 0:
                    for half in range(2):
                        act.wait_ge(stacks[(st.f - 1) % 2][half], st.at(256 * ((st.f - 1) // 2 + 1), 128))
                    act.wait_ge(S["e_ready"], st.at(2 * st.f, 2))
                for i, (f, hi, bias) in enumerate(((qf, qh, bq), (kf, kh, bk))):
                    act.activation(f[:, :], ps_wide[unit][:, i, :], ACT.Identity, bias=bias[:, :]).then_inc(S["qk_ready"], 1)
                    last = act.activation(hi[:, :], ps_wide[unit][:, i, :], ACT.Identity, bias=bias[:, :])
                    last.then_inc(S["qk_ready"] if i == 0 else wide_free[unit], 1)

            def oT_out(st):
                n, unit = st.wide("oT")
                act.wait_ge(S["wide_full"], n + 1)
                need(act, S["xnT_stored"], st.at(16 * st.c, 16))
                act.copy(oT[:, :], ps_wide[unit][:, 0, :]).then_inc(wide_free[unit], 1)

            def s_rows_out(st):
                act.wait_ge(S["misc_full"], st.misc("e_sums") + 1)
                act.copy(s_rows[:, :], ps_misc[0:64, :]).then_inc(S["misc_free"], 1)

            def av_out(st, s, g):
                act.wait_ge(S["av_full"], st.at(NGRP * s + g + 1, NGRP))
                act.copy(av_s[g % 2][:, :], ps_av[:, :]).then_inc(S["av_copied"], 1)

            def xn2T_out(st):
                act.wait_ge(S["misc_full"], st.misc("xn2") + 1)
                act.copy(xn2T[:, :], ps_misc[:, :]).then_inc(S["misc_free"], 1)

            def mT_out(st, s, half):
                act.wait_ge(S["misc_full"], st.misc(f"m{half}") + 1)
                if s > 0:
                    act.wait_ge(mrow[half], st.at(32 * s, 32))
                act.copy(mT[half][:, :], ps_misc[:, :].bitcast(F16)[0:H // 2, 0:SEQ]).then_inc(S["misc_free"], 1)

            def p_near_exp(st, s, half):
                act.wait_ge(S["d_ready"], st.at(2 * s + half + 1, 2))
                need(act, S["near_ready"], st.at(4 * (s - 1) + 2 * half + 2, 4))
                hs = slice(half * 8, half * 8 + 8)
                act.activation(p01[:, :, :, hs].rearrange("p n t h -> p (n t) h"),
                               d01[:, :, :, hs].rearrange("p n t h -> p (n t) h"), ACT.Exp,
                               scale=SCALE).then_inc(S["p_ready"], 1)

            def step(st):
                def exps(pr, units=range(2 * NT)):
                    if st.B:
                        for n in units:
                            exp_unit(st, pr, n)

                exps(0, range(6))
                if st.A:
                    s_rows_out(st)
                exps(0, range(6, 2 * NT))
                if st.B:
                    mT_out(st, st.b, 1)
                    p_near_exp(st, st.b, 1)
                exps(1)
                if st.C:
                    av_out(st, st.c, 3)
                exps(2)
                exps(3, range(2))
                if st.C:
                    oT_out(st)
                exps(3, range(2, 4))
                if st.F:
                    xT_out(st)
                exps(3, range(4, 2 * NT))
                if st.B:
                    av_out(st, st.b, 0)
                exps(4, range(2))
                if st.F:
                    qk_out(st)
                exps(4, range(2, 2 * NT))
                exps(5, range(4))
                if st.A:
                    mT_out(st, st.a, 0)
                    p_near_exp(st, st.a, 0)
                exps(5, range(4, 2 * NT))
                if st.B:
                    av_out(st, st.b, 1)
                exps(6)
                if st.C:
                    xn2T_out(st)
                exps(7)
                if st.B:
                    av_out(st, st.b, 2)

            steps(act, step)

            act.wait_ge(S["misc_free"], Step(NSEQ + 2).misc("logits") + 1)
            act.activation(logit[:, :, :], logit[:, :, :], ACT.Exp, scale=-1.0).then_inc(S["logits_exp"], 1)

            def gateT_out(f, ahead):
                act.wait_ge(S["gateT_full"], f.at(ahead + 1, 1))
                act.copy(gateT[:, :], ps_misc[:, :].bitcast(BF16)[0:64, 0:SEQ]).then_inc(S["gateT_ready"], 1)

            def end_out(f, s):
                act.wait_ge(S["second_done"], f.at(len(UNITS) * (s + 1), len(UNITS)))
                act.copy(fT, ps_av[:, :]).then_inc(S["fT_ready"], 1)

            def ffn(f):
                if f.s0 == 0:
                    act.wait_ge(S["av_full"], NGRP * NSEQ)
                    gateT_out(f, 0)
                for i, (kind, k) in enumerate(UNITS):
                    if kind == "c":
                        act.wait_ge(S["front_full"], f.at(i + 1, len(UNITS)))
                        before = UNITS.index(("c", 1 - k)) + 1 - (0 if k else len(UNITS))
                        need(act, S["hidden_ready"], f.at(before, len(UNITS)))
                        act.activation(tanh_u, ps_wide[1][:, 0, :], ACT.Tanh, scale=0.5).then_inc(S["act_ready"], 1)
                    else:
                        act.wait_ge(S["front_full"], f.at(i + 1, len(UNITS)))
                        before = EXPERT_POS[k - 2] + 1 if k >= 2 else EXPERT_POS[k - 2] + 1 - len(UNITS)
                        need(act, S["hidden_ready"], f.at(before, len(UNITS)))
                        act.activation(act_out[k % 2], ps_exp[k % 2][:, :], ACT.Gelu).then_inc(S["act_ready"], 1)
                    if i == 1 and f.s0 > 0:
                        end_out(f, -1)
                if f.s0 < NSEQ - 1:
                    gateT_out(f, 1)

            ffn_steps(act, ffn)
            end_out(Ffn(NSEQ - 1), 0)

        @block.vector
        def _(dve):
            own = Own(dve, S["dve_own"], CHAIN_DVE)

            def ready(ins):
                ins.then_inc(S["const_ready"], 1)

            for i in range(2):
                dve.memset(qs[i][:, :, :].bitcast(F32), 0.0).then_inc(S["q_rows"], 1)
            dve.wait_ge(S["attn_loaded"], 16 * N_ATTN_LOADS)
            dve.wait_ge(S["const_ready"], N_POOL_CONST)
            for dst, src in ((wq, wq_in), (wk, wk_in)):
                for b in range(2):
                    ready(dve.tensor_copy(dst[:, 64 * b:64 * b + 64].rearrange("p (hf d p4) -> p hf d p4", hf=2, d=D),
                                          src[:, :].rearrange("p (hf p4 b d) -> p b hf d p4", hf=2, b=2, d=D)[:, b]))
            ready(dve.tensor_reduce(head_sum[:, 0:H], head_sel[:, :, :, :].rearrange("p d pr b -> p (pr b) d"),
                                    AX.X, ALU.add))
            ready(dve.tensor_tensor(bk[:, :], bk_in[:, :], rk[:, 0:1], ALU.add))
            ready(dve.tensor_scalar(dk[:, :], rk[:, 1:3], rk[:, 0:1], None, ALU.subtract))
            for i in range(3):
                ready(dve.tensor_tensor(bv[:, i, :].rearrange("p (h d) -> p h d", d=D),
                                          bv_in[:, :].rearrange("p (h d) -> p h d", d=D),
                                          rv[:, i, :].unsqueeze(1).to_broadcast([P, H, D]), ALU.add))
            dve.wait_ge(S["const_ready"], N_CONST)

            def stats(src, st_, mv):
                for i in range(NT):
                    own.mark(dve.bn_stats(st_[:, i, :], src[:, i * P:i * P + P]))
                own.settle(passed["dve"])
                for i in range(NT):
                    last = dve.bn_aggr(mv[:, i, :], st_[:, i, :])
                    if i < NT - 1:
                        own.mark(last)
                return last

            def normalise(dst, src, mv, rs):
                for i in range(NT):
                    last = dve.tensor_scalar(dst[:, i, :], src[:, i * P:i * P + P], mv[:, i, 0:1], rs[:, i:i + 1],
                                             ALU.subtract, ALU.mult)
                    if i < NT - 1:
                        own.mark(last)
                return last

            def ln1(st):
                xv = xr[:, st.seq(st.f), :]
                dve.wait_ge(x_loaded[min(st.t0, 2)], 16)
                stats(xv, st1, mv1).then_inc(S["stats1"], 1)
                dve.wait_ge(S["rstd1"], st.at(st.f + 1, 1))
                normalise(xn, xv, mv1, rs1).then_inc(S["xn_ready"], 1)

            def split_and_near(st):
                dve.wait_ge(S["qk_ready"], st.at(3 * (st.f + 1), 3))
                dve.wait_ge(wide_free[st.wide("qk")[1]], st.wide_before("qk") + 1)
                if st.f > 0:
                    for half in range(2):
                        dve.wait_ge(stacks[(st.f - 1) % 2][half], st.at(256 * ((st.f - 1) // 2 + 1), 128))
                dve.tensor_tensor(ql[:, :], qf[:, :], qh[:, :], ALU.subtract).then_inc(S["qk_split"], 1)
                dve.tensor_tensor(kl[:, :], kf[:, :], kh[:, :], ALU.subtract).then_inc(S["qk_split"], 1)
                dve.scalar_tensor_tensor(e0[:, :], kf[:, :], dk[:, 1:2], qf[:, :], ALU.add,
                                         ALU.mult).then_inc(S["e_ready"], 1)
                dve.scalar_tensor_tensor(e1[:, 1:SEQ], kf[:, 0:SEQ - 1], dk[:, 0:1], qf[:, 1:SEQ], ALU.add,
                                         ALU.mult).then_inc(S["e_ready"], 1)

            def values_out(st):
                n, unit = st.wide("v")
                dve.wait_ge(S["wide_full"], n + 1)
                need(dve, S["av_full"], st.at(NGRP * (st.a - 1), NGRP))
                need(dve, S["near_ready"], st.at(4 * st.a, 4))
                pv = ps_wide[unit][:, 0, :].rearrange("p (t c) -> p t c", t=NT)
                ph = ps_wide[unit][:, 0, :].rearrange("p (t h d) -> p t h d", t=NT, d=D)
                for t in range(NT):
                    last = dve.tensor_tensor(vp[st.a % 2][:, t, :, 0:D], ph[:, t], bv[:, 0, :].rearrange(
                        "p (h d) -> p h d", d=D), ALU.add)
                    if t < NT - 1:
                        own.mark(last)
                last.then_inc(S["v_ready"], 1)
                bc = [bv[:, i, :].unsqueeze(1).to_broadcast([P, NT, P]) for i in range(3)]
                dve.tensor_tensor(v_near[:, 0], pv, bc[2], ALU.add).then_inc(S["v_ready"], 1)
                dve.tensor_tensor(v_near[:, 1], ps_wide[unit][:, 1, :].rearrange("p (t c) -> p t c", t=NT), bc[1],
                                  ALU.add).then_inc(wide_free[unit], 1)

            def s_max(st, i):
                pr, qt = i // NT, i % NT
                n, unit = st.wide(f"s{i}")
                dve.wait_ge(S["wide_full"], n + 1)
                dve.tensor_reduce(mx[:, qt, 2 * pr:2 * pr + 2], ps_wide[unit][:, :, 0:P * (qt + 1)], AX.X,
                                  ALU.max).then_inc(wide_free[unit], 1)

            def s_tok_out(st):
                dve.wait_ge(S["misc_full"], st.misc("s_tok") + 1)
                src = ps_misc[:, 0:NT * 64].rearrange("p (t n r) -> p n t r", t=NT, n=2)[:, :, :, 0:H]
                for n in range(2):
                    last = dve.tensor_copy(s_tok[:, n], src[:, n])
                    if n == 0:
                        own.mark(last)
                last.then_inc(S["misc_free"], 1)
                dve.wait_ge(S["misc_free"], st.misc("s_tok") + 1)

            def max_half(st, s, half):
                hs = slice(half * 8, half * 8 + 8)
                then = st if half == 0 else Step(st.t0 - 1, st.u)
                for i in (1, 2):
                    what = f"s{NPAIR * NT // 2 * (half + 1) - i}"
                    dve.wait_ge(wide_free[then.wide(what)[1]], then.wide_before(what) + 1)
                own.mark(dve.tensor_tensor(mxa[:, :, hs], mx[:, :, hs], s_tok[:, 0, :, hs], ALU.max))
                own.settle()
                own.mark(dve.tensor_tensor(mx[:, :, hs], mxa[:, :, hs], s_tok[:, 1, :, hs], ALU.max))
                own.settle()
                need(dve, S["p_ready"], st.at(2 * (s - 1) + half + 1, 2))
                dve.tensor_scalar(m16[:, :, hs], mx[:, :, hs], 1.0 / M_UNIT, None, ALU.mult).then_inc(S["m16_ready"], 1)
                dve.wait_ge(S["m16_ready"], st.at(2 * s + half + 1, 2))
                for k in range(2):
                    last = dve.scalar_tensor_tensor(d01[:, k, :, hs], m16[:, :, hs], -M_UNIT, s_tok[:, k, :, hs],
                                                    ALU.mult, ALU.add)
                    if k == 0:
                        own.mark(last)
                last.then_inc(S["d_ready"], 1)

            def av_tok_out(st, s, g):
                dve.wait_ge(S["misc_full"], st.misc(f"av{g}") + 1)
                if g == 0:
                    dve.wait_ge(S["near_ready"], st.at(4 * s + 2, 4))
                if g == 2:
                    dve.wait_ge(S["near_ready"], st.at(4 * s + 4, 4))
                need(dve, S["o_ready"], st.at(NGRP * s + g, NGRP))
                v = ps_misc[:, :].rearrange("p (t j c) -> p t j c", t=NT, j=4)
                par = s % 2
                own.mark(dve.tensor_tensor(den[:, :, :], v[:, :, :, D], p_near[par][:, :, 4 * g:4 * g + 4], ALU.add))
                cols = slice(4 * g * D, 4 * g * D + 4 * D)
                dve.tensor_tensor(num[:, :, :, :], v[:, :, :, 0:D], near[par][:, :, cols].rearrange(
                    "p t (j d) -> p t j d", d=D), ALU.add).then_inc(S["misc_free"], 1)
                own.settle()
                own.mark(dve.reciprocal(rden[:, :, :], den[:, :, :]))
                own.settle()
                dve.wait_ge(S["misc_free"], st.misc(f"av{g}") + 1)
                dve.tensor_tensor(o_tok[:, :, cols].rearrange("p t (j d) -> p t j d", d=D), num[:, :, :, :],
                                  rden[:, :, :].unsqueeze(3).to_broadcast([P, NT, 4, D]),
                                  ALU.mult).then_inc(S["o_ready"], 1)

            def y_out(st):
                n, unit = st.wide("oproj")
                dve.wait_ge(S["wide_full"], n + 1)
                dve.tensor_tensor(y[:, :, :], ps_wide[unit][:, 0, :].rearrange("p (t c) -> p t c", t=NT),
                                  bo[:, :].unsqueeze(1).to_broadcast([P, NT, P]), ALU.add).then_inc(wide_free[unit], 1)
                dve.wait_ge(wide_free[unit], st.wide_before("oproj") + 1)
                stats(y[:, :, :].rearrange("p t c -> p (t c)"), st2, mv2).then_inc(S["stats2"], 1)

            def z_out(st):
                dve.wait_ge(S["rstd2"], st.at(st.c + 1, 1))
                need(dve, S["x1_ready"], st.at(st.c, 1))
                normalise(z, y[:, :, :].rearrange("p t c -> p (t c)"), mv2, rs2).then_inc(S["z_ready"], 1)

            def x1_stats(st):
                dve.wait_ge(S["x1_ready"], st.at(st.c + 1, 1))
                stats(xr[:, st.seq(st.c), :], st3, mv3).then_inc(S["stats3"], 1)

            def xn2_out(st):
                dve.wait_ge(S["rstd3"], st.at(st.c + 1, 1))
                normalise(xn2, xr[:, st.seq(st.c), :], mv3, rs3).then_inc(S["xn2_ready"], 1)

            def logits_out(st):
                dve.wait_ge(S["misc_full"], st.misc("logits") + 1)
                dve.tensor_copy(logit[:, st.seq(st.c), :], ps_misc[:, 0:NT * NE]).then_inc(S["misc_free"], 1)

            def step(st):
                own.begin(st)

                def maxima(lo, hi):
                    if st.A:
                        for i in range(lo, hi):
                            s_max(st, i)

                if st.B:
                    max_half(st, st.b, 1)
                maxima(0, 2)
                if st.C:
                    av_tok_out(st, st.c, 2)
                if st.F:
                    ln1(st)
                maxima(2, 7)
                if st.A:
                    s_tok_out(st)
                maxima(7, 9)
                if st.C:
                    av_tok_out(st, st.c, 3)
                maxima(9, 11)
                if st.A:
                    values_out(st)
                maxima(11, 14)
                if st.C:
                    y_out(st)
                maxima(14, 17)
                if st.A:
                    max_half(st, st.a, 0)
                if st.B:
                    av_tok_out(st, st.b, 0)
                if st.C:
                    z_out(st)
                maxima(17, 18)
                if st.F:
                    split_and_near(st)
                maxima(18, 20)
                if st.C:
                    x1_stats(st)
                maxima(20, 23)
                if st.C:
                    xn2_out(st)
                maxima(23, 25)
                if st.B:
                    av_tok_out(st, st.b, 1)
                maxima(25, 31)
                if st.C:
                    logits_out(st)
                maxima(31, 32)
                own.end()

            steps(dve, step)

            own2 = Own(dve, S["dve_own2"], CHAIN_FFN)
            own2.st = Step(0)
            dve.wait_ge(S["logits_exp"], 1)
            own2.mark(dve.tensor_scalar(logit[:, :, :], logit[:, :, :], 1.0, None, ALU.add))
            own2.settle()
            own2.mark(dve.reciprocal(logit[:, :, :], logit[:, :, :]))
            own2.settle()
            dve.wait_ge(S["ffn_const"], 7)

            def do(ins):
                own2.mark(ins)
                own2.settle()

            def gates(f, ahead):
                score = logit[:, f.seq(f.s0 + ahead), :].rearrange("p (t e) -> p t e", e=NE)
                own2.mark(dve.tensor_tensor(sel[:, :, :], score, rb[:, :].unsqueeze(1).to_broadcast([P, NT, NE]), ALU.add))
                own2.settle(passed["dve"])
                for t in range(NT):
                    own2.mark(dve.max(top[:, t, :], sel[:, t, :]))
                own2.settle(passed["dve"])
                for t in range(NT):
                    own2.mark(dve.max_index(top_i[:, t, :], top[:, t, :], sel[:, t, :]))
                own2.settle()
                do(dve.tensor_copy(top_f[:, :, :], top_i[:, :, 0:2]))
                it = iota_f[:, :].unsqueeze(1).to_broadcast([P, NT, NE])
                for k in range(2):
                    own2.mark(dve.tensor_tensor(is_top[:, k], it, top_f[:, :, k:k + 1].to_broadcast([P, NT, NE]),
                                                ALU.is_equal))
                own2.settle()
                do(dve.tensor_tensor(in_two[:, :, :], is_top[:, 0], is_top[:, 1], ALU.add))
                do(dve.tensor_tensor(chosen[:, :, :], in_two[:, :, :], score, ALU.mult))
                do(dve.tensor_reduce(total[:, :], chosen[:, :, :], AX.X, ALU.add))
                own2.mark(dve.tensor_scalar(normal[:, :], total[:, :], 1e-9, None, ALU.is_gt))
                do(dve.tensor_scalar(total_e[:, :], total[:, :], 1e-9, None, ALU.add))
                own2.mark(dve.tensor_scalar(even[:, :], normal[:, :], -0.5, 0.5, ALU.mult, ALU.add))
                do(dve.reciprocal(total[:, :], total_e[:, :]))
                do(dve.tensor_tensor(total[:, :], total[:, :], normal[:, :], ALU.mult))
                own2.mark(dve.tensor_tensor(gate_n[:, :, :], chosen[:, :, :],
                                            total[:, :].unsqueeze(2).to_broadcast([P, NT, NE]), ALU.mult))
                do(dve.tensor_tensor(gate_r[:, :, :], in_two[:, :, :],
                                     even[:, :].unsqueeze(2).to_broadcast([P, NT, NE]), ALU.mult))
                do(dve.tensor_tensor(gate[:, :, :], gate_n[:, :, :], gate_r[:, :, :], ALU.add))
                need(dve, S["gateT_full"], f.at(ahead, 1))
                do(dve.tensor_copy(gate3[:, :, 0:NE], gate[:, :, :]))
                do(dve.tensor_tensor(gate_r[:, :, :], gate[:, :, :], gate3[:, :, 0:NE], ALU.subtract))
                do(dve.tensor_copy(gate3[:, :, NE:2 * NE], gate_r[:, :, :]))
                dve.tensor_tensor(gate3[:, :, 2 * NE:3 * NE], gate_r[:, :, :], gate3[:, :, NE:2 * NE],
                                  ALU.subtract).then_inc(S["chosen_ready"], 1)

            def end_stats(f, s):
                dve.wait_ge(S["f_tok_full"], f.at(s + 1, 1))
                need(dve, S["z4_ready"], f.at(s, 1))
                dve.tensor_copy(f_tok, ps_misc[:, :]).then_inc(S["f_tok_ready"], 1)
                dve.wait_ge(S["f_tok_ready"], f.at(s + 1, 1))
                for i in range(NT):
                    own2.mark(dve.bn_stats(st2[:, i, :], f_tok[:, i * P:i * P + P]))
                own2.settle(passed["dve"])
                for i in range(NT):
                    last = dve.bn_aggr(mv2[:, i, :], st2[:, i, :])
                    if i < NT - 1:
                        own2.mark(last)
                last.then_inc(S["stats4"], 1)

            def end_z(f, s):
                dve.wait_ge(S["rstd4"], f.at(s + 1, 1))
                need(dve, S["out_ready"], f.at(s, 1))
                for i in range(NT):
                    last = dve.tensor_scalar(z[:, i, :], f_tok[:, i * P:i * P + P], mv2[:, i, 0:1], rs2[:, i:i + 1],
                                             ALU.subtract, ALU.mult)
                    if i < NT - 1:
                        own2.mark(last)
                last.then_inc(S["z4_ready"], 1)

            def back_needed(f, i, kind):
                need(dve, S["second_done"], f.at(i - 3, len(UNITS)))

            def ffn(f):
                own2.begin_ffn(f)
                if f.s0 == 0:
                    dve.wait_ge(S["av_full"], NGRP * NSEQ)
                for i, (kind, k) in enumerate(UNITS):
                    dve.wait_ge(S["act_ready"], f.at(i + 1, len(UNITS)))
                    back_needed(f, i, kind)
                    if kind == "c":
                        need(dve, S["hidden_ready"], f.at(i, len(UNITS)))
                        do(dve.scalar_tensor_tensor(silu2, tanh_u, 1.0, ps_wide[1][:, 0, :], ALU.add, ALU.mult))
                        dve.scalar_tensor_tensor(hidden[hid(f, i)], silu2, 0.5, ps_wide[1][:, 1, :], ALU.mult,
                                                 ALU.mult).then_inc(S["hidden_ready"], 1)
                    else:
                        dve.tensor_tensor(hidden[hid(f, i)], act_out[k % 2], ps_wide[0][:, k % 2, :],
                                          ALU.mult).then_inc(S["hidden_ready"], 1)
                    if i == 3 and f.s0 > 0:
                        end_stats(f, -1)
                    if i == 6 and f.s0 > 0:
                        end_z(f, -1)
                    if i == 7 and f.s0 < NSEQ - 1:
                        gates(f, 1)
                own2.end_ffn(f)

            gates(Ffn(0), 0)
            ffn_steps(dve, ffn)
            end_stats(Ffn(NSEQ - 1), 0)
            end_z(Ffn(NSEQ - 1), 0)

        @block.tensor
        def _(pe):
            def wide(st, what):
                _, unit = st.wide(what)
                need(pe, wide_free[unit], st.wide_before(what))
                return ps_wide[unit]

            def misc(st, what):
                need(pe, S["misc_free"], st.misc(what))
                return ps_misc

            def exp_unit(st, pr, n):
                i = 2 * NT * pr + n
                kt, b = n // 2, n % 2
                par = st.b % 2
                need(pe, S["exp_done"], st.at(2 * NPAIR * NT * st.b + i - 1, 2 * NPAIR * NT))
                if n == 0 and pr % 4 == 0:
                    pe.wait_ge(mrow[pr // 4], st.at(32 * (st.b + 1), 32))
                w = WIDTH[kt]
                pe.matmul(ps_exp[b][:, 0:w], ks[par][b][:, pr, P * kt:P * kt + P], qs[par][:, pr, P * kt:SEQ],
                          start=True, stop=True).then_inc(S["exp_full"], 1)

            def s_unit(st, i):
                pr, qt = i // NT, i % NT
                par = st.a % 2
                if qt == 0 and pr % 4 == 0:
                    pe.wait_ge(stacks[par][pr // 4], st.at(256 * (st.a // 2 + 1), 128))
                if i == 0 and st.a < 2:
                    pe.wait_ge(S["k_rows"], 4 * st.a + 4)
                    pe.wait_ge(S["q_rows"], st.a + 1)
                u = wide(st, f"s{i}")
                w = P * (qt + 1)
                lo = max(w - DIAG, 0)
                for b in range(2):
                    pe.matmul(u[:, b, 0:w], qs[par][0:M_ROW, pr, P * qt:P * qt + P], ks[par][b][0:M_ROW, pr, 0:w],
                              start=True, stop=False)
                for b in range(2):
                    last = pe.matmul(u[:, b, lo:w], identb[:, :], maskb[:, DIAG - (w - lo):DIAG],
                                     start=False, stop=True)
                last.then_inc(S["wide_full"], 1)

            def av_part(st, s, g, kt):
                par = s % 2
                n = NPAIR * NT * s
                pe.wait_ge(S["p_masked"], st.at(n + NT * (2 * g + 1) + kt + 1, NPAIR * NT))
                if kt == 0:
                    need(pe, S["av_copied"], st.at(NGRP * s + g, NGRP))
                    if g == 0:
                        pe.wait_ge(S["v_ready"], st.at(2 * s + 1, 2))
                w = WIDTH[kt]
                for j in range(4):
                    pr, b = 2 * g + j // 2, j % 2
                    last = pe.matmul(ps_av[32 * j:32 * j + 32, P * kt:SEQ], vp[par][:, kt, 4 * g + j, :],
                                     prob[pr % PBUF][:, b, START[kt]:START[kt] + w],
                                     start=(kt == 0), stop=(kt == NT - 1))
                if kt == NT - 1:
                    last.then_inc(S["av_full"], 1)

            def transposes(dst, src, unit, done):
                for i in range(NT):
                    last = pe.transpose(dst(i), src(i), unit)
                last.then_inc(done, 1)

            def x_transpose(st):
                u = wide(st, "xT")
                pe.wait_ge(S["xn_ready"], st.at(st.f + 1, 1))
                transposes(lambda i: u[:, 0, i * P:i * P + P], lambda i: xn[:, i, :], ident[:, :], S["wide_full"])

            def qk(st):
                u = wide(st, "qk")
                pe.wait_ge(wide_free[st.wide("xT")[1]], st.wide_before("xT") + 1)
                pe.matmul(u[:, 0, :], wq[:, :], xnT[:, 1:1 + SEQ], start=True, stop=True)
                pe.matmul(u[:, 1, :], wk[:, :], xnT[:, 1:1 + SEQ], start=True, stop=True).then_inc(S["wide_full"], 1)

            def values(st):
                u = wide(st, "v")
                for n in range(2):
                    for i in range(NT):
                        last = pe.matmul(u[:, n, i * P:i * P + P], xnT[:, 1 - n + i * P:1 - n + i * P + P], wv[:, :],
                                         start=True, stop=True)
                last.then_inc(S["wide_full"], 1)

            def o_transpose(st):
                u = wide(st, "oT")
                pe.wait_ge(S["o_ready"], st.at(NGRP * (st.c + 1), NGRP))
                transposes(lambda i: u[:, 0, i * P:i * P + P], lambda i: o_tok[:, i, :], ident[:, :], S["wide_full"])

            def o_proj(st):
                u = wide(st, "oproj")
                pe.wait_ge(wide_free[st.wide("oT")[1]], st.wide_before("oT") + 1)
                for i in range(NT):
                    last = pe.matmul(u[:, 0, i * P:i * P + P], oT[:, i * P:i * P + P], wo[:, :], start=True, stop=True)
                last.then_inc(S["wide_full"], 1)

            def e_sums(st):
                m = misc(st, "e_sums")
                pe.wait_ge(S["e_ready"], st.at(2 * (st.a + 1), 2))
                pe.matmul(m[0:32, :], head_sum[:, :], e0[:, :], start=True, stop=True)
                pe.matmul(m[32:64, :], head_sum[:, :], e1[:, :], start=True, stop=True).then_inc(S["misc_full"], 1)

            def s_tok_transpose(st):
                m = misc(st, "s_tok")
                pe.sem_inc(passed["pe"], 1)
                transposes(lambda i: m[:, i * 64:i * 64 + 64], lambda i: s_rows[:, i * P:i * P + P],
                           ident[0:64, 0:64], S["misc_full"])

            def m_transpose(st, s, half):
                m = misc(st, f"m{half}")[:, :].bitcast(F16)
                pe.wait_ge(S["m16_ready"], st.at(2 * s + half + 1, 2))
                transposes(lambda i: m[0:H // 2, i * P:i * P + P], lambda i: m16[:, i, half * 8:half * 8 + 8],
                           ident16[:, :], S["misc_full"])

            def av_transpose(st, s, g):
                m = misc(st, f"av{g}")
                pe.wait_ge(S["av_copied"], st.at(NGRP * s + g + 1, NGRP))
                transposes(lambda i: m[:, i * P:i * P + P], lambda i: av_s[g % 2][:, i * P:i * P + P],
                           ident[:, :], S["misc_full"])

            def xn2_transpose(st):
                m = misc(st, "xn2")
                pe.wait_ge(S["xn2_ready"], st.at(st.c + 1, 1))
                transposes(lambda i: m[:, i * P:i * P + P], lambda i: xn2[:, i, :], ident[:, :], S["misc_full"])

            def logits(st):
                m = misc(st, "logits")
                for i in range(NT):
                    last = pe.matmul(m[:, i * NE:i * NE + NE], xn2T[:, i * P:i * P + P], rwT[:, :],
                                     start=True, stop=True)
                last.then_inc(S["misc_full"], 1)

            def step(st):
                uses = {"av2": lambda: av_transpose(st, st.c, 2), "e_sums": lambda: e_sums(st),
                        "m1": lambda: m_transpose(st, st.b, 1), "s_tok": lambda: s_tok_transpose(st),
                        "av3": lambda: av_transpose(st, st.c, 3), "v": lambda: values(st),
                        "oT": lambda: o_transpose(st), "xT": lambda: x_transpose(st), "oproj": lambda: o_proj(st),
                        "qk": lambda: qk(st), "av0": lambda: av_transpose(st, st.b, 0),
                        "m0": lambda: m_transpose(st, st.a, 0), "av1": lambda: av_transpose(st, st.b, 1),
                        "xn2": lambda: xn2_transpose(st), "logits": lambda: logits(st)}
                here = {"F": st.F, "A": st.A, "B": st.B, "C": st.C}
                for slot in range(SLOTS):
                    pr, n = slot // (2 * NT), slot % (2 * NT)
                    if st.B:
                        exp_unit(st, pr, n)
                    for what, use in uses.items():
                        if AT[what] == slot and here[STAGE[what]]:
                            use()
                    if n % 4 == 1:
                        kt = pr % 2 * 2 + n // 4
                        if pr >= 2 and st.B:
                            av_part(st, st.b, pr // 2 - 1, kt)
                        if pr < 2 and st.C:
                            av_part(st, st.c, NGRP - 1, kt)
                    if st.A and n % 2 == 1:
                        s_unit(st, slot // 2)

            pe.wait_ge(S["const_ready"], N_CONST)
            steps(pe, step)

            def gate_transpose(f, ahead):
                pe.wait_ge(S["chosen_ready"], f.at(ahead + 1, 1))
                need(pe, S["f_tok_ready"], f.at(ahead - 1, 1))
                pe.sem_inc(passed["pe"], 1)
                m = ps_misc[:, :].bitcast(BF16)
                for i in range(NT):
                    last = pe.transpose(m[0:64, i * P:i * P + P], gate3[:, i, :], identb[:, :])
                last.then_inc(S["gateT_full"], 1)

            def first(f, i):
                kind, k = UNITS[i]
                xe = xeT[f.s0 % 2]
                n = len(UNITS)
                if i == 0:
                    pe.wait_ge([S["xe_loaded0"], S["xe_loaded1"]][f.s0 % 2],
                               16 * (f.s0 // 2 + 1) if f.u is None else f.u * 16 + 16 * (f.s0 // 2 + 1))
                if kind == "c":
                    other = UNITS.index(("c", 1 - k)) + 1
                    need(pe, S["hidden_ready"], f.at(other if k else other - n, n))
                    cols = slice(k * P, k * P + P)
                    pe.matmul(ps_wide[1][:, 0, :], sw1_s[:, cols], xe, start=True, stop=True)
                    pe.matmul(ps_wide[1][:, 1, :], sw3_s[:, cols], xe, start=True, stop=True).then_inc(S["front_full"], 1)
                else:
                    before = EXPERT_POS[k - 2] + 1
                    need(pe, S["hidden_ready"], f.at(before if k >= 2 else before - n, n))
                    if k == 0:
                        pe.wait_ge(S["gateT_ready"], f.at(1, 1))
                    pe.matmul(ps_wide[0][:, k % 2, :], sel_e[:, k, :], gateT[:, :], start=True, stop=True)
                    pe.matmul(ps_exp[k % 2][:, :], ew1_s[:, k, :], xe, start=True, stop=True).then_inc(S["front_full"], 1)

            def second(f, i):
                kind, k = UNITS[i]
                n = len(UNITS)
                pe.wait_ge(S["hidden_ready"], f.at(i + 1, n))
                if i == 0:
                    need(pe, S["fT_ready"], f.at(0, 1))
                w = sw2_s[:, k, :] if kind == "c" else ew2_s[:, k, :]
                last = pe.matmul(ps_av[:, :], w, hidden[hid(f, i)], start=(i == 0), stop=(i == n - 1))
                last.then_inc(S["second_done"], 1)

            def end_transpose(f, s):
                pe.wait_ge(S["fT_ready"], f.at(s + 1, 1))
                pe.wait_ge(S["gateT_ready"], f.at(min(s + 2, 1), 1))
                for i in range(NT):
                    last = pe.transpose(ps_misc[:, i * P:i * P + P], fT[:, i * P:i * P + P], ident[:, :])
                last.then_inc(S["f_tok_full"], 1)

            def ffn(f):
                n = len(UNITS)
                if f.s0 == 0:
                    pe.wait_ge(S["ffn_loaded"], 16 * 5)
                    pe.wait_ge(S["ffn_const"], 7)
                    gate_transpose(f, 0)
                for i in range(n):
                    first(f, i)
                    if i == 2 and f.s0 > 0:
                        end_transpose(f, -1)
                    if i == n - 1 and f.s0 < NSEQ - 1:
                        gate_transpose(f, 1)
                    if i >= LAG:
                        second(f, i - LAG)
                for i in range(n - LAG, n):
                    second(f, i)

            ffn_steps(pe, ffn)
            end_transpose(Ffn(NSEQ - 1), 0)


_INS = ["L0_attn_x", "L0_attn_W_q", "L0_attn_b_q", "L0_attn_W_k", "L0_attn_b_k", "L0_attn_W_v", "L0_attn_b_v",
        "L0_attn_W_o", "L0_attn_b_o", "L0_attn_rel_k_table", "L0_attn_rel_v_table", "L0_ffn_router_w",
        "L0_ffn_router_bias", "L0_ffn_sw1", "L0_ffn_sw3", "L0_ffn_sw2", "L0_ffn_ew1", "L0_ffn_ew2"]


def kernel(**inputs):
    import concourse.bacc as bacc
    from concourse.bass_utils import run_bass_kernel_spmd

    nc = bacc.Bacc("TRN2", target_bir_lowering=False, num_devices=1)
    arrays, args = {}, []
    for name in _INS:
        a = np.ascontiguousarray(inputs[name])
        arrays[name] = a
        args.append(nc.dram_tensor(name, a.shape, mybir.dt.from_np(a.dtype), kind="ExternalInput").ap())
    args.append(nc.dram_tensor("out", (NSEQ, SEQ, P), F32, kind="ExternalOutput").ap())
    block_kernel(nc, *args)
    r = run_bass_kernel_spmd(nc, [arrays], core_ids=[0])
    return r.results[0]["out"]
```

```python
from contextlib import ExitStack

import numpy as np
import concourse.bass as bass
from concourse import mybir

F32 = mybir.dt.float32
F16 = mybir.dt.float16
BF16 = mybir.dt.bfloat16
U32 = mybir.dt.uint32
F32R = mybir.dt.float32r
ALU = mybir.AluOpType
ACT = mybir.ActivationFunctionType
AX = mybir.AxisListType

P = 128
NSEQ, SEQ = 16, 512
NT = SEQ // P
H, D = 16, 8
NPAIR, NGRP = H // 2, H // 4
SCALE = float(D) ** -0.5
EPS = 1e-5
M_UNIT = 16.0
MASKED = -1e30
M_ROW = P - 2
PBUF = 4
NE, HR, HS = 8, 128, 256
NC = HS // P
DIAG = P + 1

WIDTH = [SEQ - P * kt for kt in range(NT)]
START = [sum(WIDTH[:kt]) for kt in range(NT)]
PCOLS = sum(WIDTH)

SLOTS = NPAIR * NT * 2
AT = {"av2": 3, "e_sums": 6, "m1": 8, "s_tok": 13, "av3": 19, "v": 20, "xT": 24, "oT": 28,
      "oproj": 32, "qk": 36, "av0": 38, "m0": 42, "av1": 54, "xn2": 57, "logits": 59}
STAGE = {"av2": "C", "e_sums": "A", "m1": "B", "s_tok": "A", "av3": "C", "v": "A", "oT": "C", "xT": "F",
         "oproj": "C", "qk": "F", "av0": "B", "m0": "A", "av1": "B", "xn2": "C", "logits": "C"}
STAGE.update({f"s{i}": "A" for i in range(NPAIR * NT)})
WIDE_ORDER = [what for _, what in sorted([(AT[w], w) for w in ("v", "oT", "xT", "oproj", "qk")]
                                         + [(2 * i + 1.5, f"s{i}") for i in range(NPAIR * NT)])]
MISC_ORDER = sorted((w for w in AT if w not in WIDE_ORDER), key=AT.get)
LOOP0, LOOP_STEPS = 3, NSEQ - 4 - (NSEQ - 4) % 2
CHAIN_DVE, CHAIN_POOL = 39, 14


class Step:

    def __init__(self, t0, u=None):
        self.t0, self.u = t0, u
        self.F, self.A, self.B, self.C = self._on(t0).values()
        self.f, self.a, self.b, self.c = t0, t0 - 1, t0 - 2, t0 - 3

    @staticmethod
    def _on(t):
        return {stage: 0 <= t - lag < NSEQ for lag, stage in enumerate("FABC")}

    def seq(self, s0):
        return s0 if self.u is None else self.u * 2 + s0

    def at(self, count, rate):
        return count if self.u is None else self.u * (2 * rate) + count

    def _uses(self, order, what):
        before = sum(self._on(t)[STAGE[w]] for t in range(self.t0) for w in order)
        return before + sum(self._on(self.t0)[STAGE[w]] for w in order[:order.index(what)])

    def misc(self, what):
        return self.at(self._uses(MISC_ORDER, what), len(MISC_ORDER))

    def wide(self, what):
        n = self._uses(WIDE_ORDER, what)
        return self.at(n, len(WIDE_ORDER)), n % 2

    def wide_before(self, what):
        n = self._uses(WIDE_ORDER, what) // 2
        return n if self.u is None else self.u * len(WIDE_ORDER) + n


def steps(eng, body):
    for t in range(LOOP0):
        body(Step(t))
    with eng.Fori(0, LOOP_STEPS // 2) as u:
        body(Step(LOOP0, u))
        body(Step(LOOP0 + 1, u))
    for t in range(LOOP0 + LOOP_STEPS, NSEQ + 3):
        body(Step(t))


class Ffn:

    def __init__(self, s0, u=None):
        self.s0, self.u = s0, u

    def seq(self, s0):
        return s0 if self.u is None else self.u * 2 + s0

    def at(self, extra, rate):
        n = rate * self.s0 + extra
        return n if self.u is None else self.u * (2 * rate) + n


def ffn_steps(eng, body):
    body(Ffn(0))
    body(Ffn(1))
    with eng.Fori(0, (NSEQ - 4) // 2) as u:
        body(Ffn(2, u))
        body(Ffn(3, u))
    body(Ffn(NSEQ - 2))
    body(Ffn(NSEQ - 1))


UNITS = [("c", 0), ("e", 0), ("e", 1), ("e", 2), ("c", 1)] + [("e", e) for e in range(3, NE)]
CHAIN_FFN, CHAIN_FFN_POOL = 38, 3
HIDDEN = 5
LAG = 4
EXPERT_POS = [UNITS.index(("e", e)) for e in range(NE)]


def hid(f, i):
    return (f.s0 * len(UNITS) + i) % HIDDEN


class Own:

    def __init__(self, eng, sem, per_step):
        self.eng, self.sem, self.per_step, self.n, self.base = eng, sem, per_step, 0, None

    def begin(self, st):
        if st.t0 == LOOP0:
            self.loop0 = self.n
        if st.t0 == LOOP0 + LOOP_STEPS:
            self.n = self.loop0 + self.per_step * LOOP_STEPS
        self.st = st
        self.first = self.n

    def end_ffn(self, f):
        if 0 < f.s0 < NSEQ - 1 and self.per_step != self.n - self.first:
            raise AssertionError((self.n - self.first, self.per_step))

    def begin_ffn(self, f):
        if f.s0 == 2 and f.u is not None:
            self.loop0 = self.n
        if f.s0 == NSEQ - 2:
            self.n = self.loop0 + self.per_step * (NSEQ - 4)
        self.st, self.first = Step(0, f.u), self.n

    def end(self):
        if LOOP0 <= self.st.t0 < NSEQ and self.per_step != self.n - self.first:
            raise AssertionError((self.n - self.first, self.per_step))

    def mark(self, ins):
        ins.then_inc(self.sem, 1)
        self.n += 1

    def settle(self, apart=None):
        self.eng.wait_ge(self.sem, self.st.at(self.n, self.per_step))
        if apart is not None:
            self.eng.sem_inc(apart, 1)


def need(eng, sem, value):
    if not isinstance(value, int) or value > 0:
        eng.wait_ge(sem, value)


def wait_apart(eng, sem, value, passed):
    need(eng, sem, value)
    eng.sem_inc(passed, 1)


def block_kernel(nc, x, W_q, b_q, W_k, b_k, W_v, b_v, W_o, b_o, rel_k, rel_v,
                 router_w, router_bias, sw1, sw3, sw2, ew1, ew2, out):
    ctx = ExitStack()
    with ctx:
        def sb(name, shape, dt=F32):
            return ctx.enter_context(nc.sbuf_tensor(name, shape, dt))

        def sem(name):
            return ctx.enter_context(nc.semaphore(name))

        ident = sb("ident", [P, P])
        ident16 = sb("ident16", [P, P], F16)
        identb = sb("identb", [P, P], BF16)
        maskb = sb("maskb", [P, DIAG], BF16)
        head_sel = sb("head_sel", [P, D, NPAIR, 2])
        head_sum = sb("head_sum", [P, 32])
        wq_in = sb("wq_in", [P, P])
        wk_in = sb("wk_in", [P, P])
        wq = sb("wq", [P, P])
        wk = sb("wk", [P, P])
        wv = sb("wv", [P, P])
        wo = sb("wo", [P, P])
        rwT = sb("rwT", [P, NE])
        bq = sb("bq", [P, 1])
        bk_in = sb("bk_in", [P, 1])
        rk = sb("rk", [P, 3])
        rk_all = sb("rk_all", [P, 3, D])
        rk_own = sb("rk_own", [P, 3, D])
        feature = sb("feature", [P, D])
        bk = sb("bk", [P, 1])
        dk = sb("dk", [P, 2])
        bv_col = sb("bv_col", [P, 1])
        rv0_col = sb("rv0_col", [P, 1])
        bias_v = sb("bias_v", [P, P])
        rv = sb("rv", [P, 3, D])
        dv = sb("dv", [P, 2, P])
        bo_in = sb("bo_in", [P, P])
        bo = sb("bo", [P, P])
        rb = sb("rb", [P, NE])
        m_col = sb("m_col", [P, 2], F16)
        neg_half = sb("neg_half", [P, NT])
        xr = sb("xr", [P, NSEQ, SEQ])
        xnT_dram = nc.dram_tensor("xnT_dram", [NSEQ, P, SEQ], F32, kind="Internal").ap()
        logit = sb("logit", [P, NSEQ, NT * NE])
        st1 = sb("st1", [P, NT, 6])
        mv1 = sb("mv1", [P, NT, 2])
        var1 = sb("var1", [P, NT])
        rs1 = sb("rs1", [P, NT])
        xn = sb("xn", [P, NT, P])
        xnT = sb("xnT", [P, 1 + SEQ])
        qf = sb("qf", [P, SEQ])
        kf = sb("kf", [P, SEQ])
        qh = sb("qh", [P, SEQ], F16)
        ql = sb("ql", [P, SEQ], F16)
        kh = sb("kh", [P, SEQ], F16)
        kl = sb("kl", [P, SEQ], F16)
        e0 = sb("e0", [P, SEQ])
        e1 = sb("e1", [P, SEQ])
        s_rows = sb("s_rows", [64, SEQ])
        s_tok = sb("s_tok", [P, 2, NT, H])
        mx = sb("mx", [P, NT, H])
        mxa = sb("mxa", [P, NT, H])
        m16 = sb("m16", [P, NT, H], F16)
        d01 = sb("d01", [P, 2, NT, H])
        p01 = sb("p01", [P, 2, NT, H])
        mT = [sb(f"mT{i}", [H // 2, SEQ], F16) for i in range(2)]
        v_near = sb("v_near", [P, 2, NT, P])
        pv_near = v_near
        vp = [sb(f"vp{i}", [P, NT, H, 32]) for i in range(2)]
        near = [sb(f"near{i}", [P, NT, P]) for i in range(2)]
        p_near = [sb(f"p_near{i}", [P, NT, H]) for i in range(2)]
        av_s = [sb(f"av_s{i}", [P, SEQ]) for i in range(2)]
        den = sb("den", [P, NT, 4])
        rden = sb("rden", [P, NT, 4])
        num = sb("num", [P, NT, 4, D])
        o_tok = sb("o_tok", [P, NT, P])
        oT = sb("oT", [P, SEQ])
        y = sb("y", [P, NT, P])
        st2 = sb("st2", [P, NT, 6])
        mv2 = sb("mv2", [P, NT, 2])
        var2 = sb("var2", [P, NT])
        rs2 = sb("rs2", [P, NT])
        z = y
        st3 = sb("st3", [P, NT, 6])
        mv3 = sb("mv3", [P, NT, 2])
        var3 = sb("var3", [P, NT])
        rs3 = sb("rs3", [P, NT])
        xn2 = y
        xn2T = oT

        sel_e = sb("sel_e", [64, NE, P], BF16)
        iota_i = sb("iota_i", [P, NE], mybir.dt.int32)
        iota_f = sb("iota_f", [P, NE])
        sel = sb("sel", [P, NT, NE])
        top = sb("top", [P, NT, 8])
        top_i = sb("top_i", [P, NT, 8], U32)
        top_f = sb("top_f", [P, NT, 2])
        is_top = sb("is_top", [P, 2, NT, NE])
        in_two = sb("in_two", [P, NT, NE])
        chosen = sb("chosen", [P, NT, NE])
        total = sb("total", [P, NT])
        total_e = sb("total_e", [P, NT])
        normal = sb("normal", [P, NT])
        even = sb("even", [P, NT])
        gate = sb("gate", [P, NT, NE])
        gate_n = sb("gate_n", [P, NT, NE])
        gate_r = sb("gate_r", [P, NT, NE])
        gate3 = sb("gate3", [P, NT, 64], BF16)
        gateT = sb("gateT", [64, SEQ], BF16)
        with ExitStack() as attention:
            def sb_attention(name, shape, dt=F32):
                return attention.enter_context(nc.sbuf_tensor(name, shape, dt))

            qs0 = sb_attention("qs0", [P, NPAIR, SEQ], F16)
            ks0 = [sb_attention(f"ks0{b}", [P, NPAIR, SEQ], F16) for b in range(2)]
            prob = [sb_attention(f"prob{i}", [P, 2, PCOLS]) for i in range(PBUF)]
            qs1 = sb_attention("qs1", [P, NPAIR, SEQ], F16)
            ks1 = [sb_attention(f"ks1{b}", [P, NPAIR, SEQ], F16) for b in range(2)]
            qs, ks = [qs0, qs1], [ks0, ks1]
        w_first = sb("w_first", [P, 12, P])
        w_high = sb("w_high", [P, 12, P])
        w_low = sb("w_low", [P, 12, P])
        w_second = sb("w_second", [P, NC + NE, P])
        sb("rest_of_stacks", [P, 2, P])
        xeT = [sb(f"xeT{i}", [P, SEQ]) for i in range(2)]
        xe_high = [sb(f"xe_high{i}", [P, SEQ]) for i in range(2)]
        xe_low = [sb(f"xe_low{i}", [P, SEQ]) for i in range(2)]
        act_out = [sb(f"act_out{i}", [P, SEQ]) for i in range(2)]
        tanh_u = sb("tanh_u", [P, SEQ])
        silu2 = sb("silu2", [P, SEQ])
        hidden = [sb(f"hidden{i}", [P, SEQ]) for i in range(HIDDEN)]
        hidden_high = [sb(f"hidden_high{i}", [P, SEQ]) for i in range(HIDDEN)]
        hidden_low = [sb(f"hidden_low{i}", [P, SEQ]) for i in range(HIDDEN)]
        w2_high = sb("w2_high", [P, NC + NE, P])
        w2_low = sb("w2_low", [P, NC + NE, P])
        fT = sb("fT", [P, SEQ])
        f_tok = sb("f_tok", [P, SEQ])
        result = sb("result", [P, SEQ])

        ps_exp = [ctx.enter_context(nc.psum_tensor(f"ps_exp{i}", [P, SEQ], F32)) for i in range(2)]
        ps_wide = [ctx.enter_context(nc.psum_tensor(f"ps_wide{i}", [P, 2, SEQ], F32)) for i in range(2)]
        ps_av = ctx.enter_context(nc.psum_tensor("ps_av", [P, SEQ], F32))
        ps_misc = ctx.enter_context(nc.psum_tensor("ps_misc", [P, SEQ], F32))

        names = """
            attn_loaded x_loaded0 x_loaded1 x_loaded2 const_made const_ready bias_full bias_ready
            k_zeros v_rows k_rows q_rows
            dve_own pool_own dve_own2 pool_own2 passed_sp passed_pool passed_dve passed_pe
            wide_full wide_free0 wide_free1 misc_full misc_free
            stats1 xn_ready qk_ready qk_split e_ready stacks00 stacks01 stacks10 stacks11
            v_ready near_ready m16_ready mrow0 mrow1 d_ready p_ready
            exp_full exp_done p_masked av_full av_copied o_ready
            stats2 x1_ready stats3 xn2_ready xnT_stored
            ffn_loaded ffn_const w_split xe_loaded0 xe_loaded1 xe_split
            chosen_ready gateT_full gateT_ready front_full act_ready hidden_ready high_ready low_ready
            second_done fT_ready f_tok_full f_tok_ready stats4 z4_ready out_ready stored""".split()
        S = {n: sem(n) for n in names}
        x_loaded = [S["x_loaded0"], S["x_loaded1"], S["x_loaded2"]]
        stacks = [[S[f"stacks{par}{half}"] for half in range(2)] for par in range(2)]
        mrow = [S["mrow0"], S["mrow1"]]
        wide_free = [S["wide_free0"], S["wide_free1"]]

        N_ATTN_LOADS = 4 + 1 + 8 + 1 + 5
        N_CONST_MADE, N_POOL_CONST, N_CONST = 10, 7, 7 + 10
        x_v = x.rearrange("b (i p) d -> p b i d", p=P)
        out_v = out.rearrange("b (i p) d -> p b i d", p=P)

        def split_heads(v):
            return v.rearrange("(hf p4 b d) -> b hf d p4", hf=2, b=2, d=D)

        passed = {n: S["passed_" + n] for n in ("sp", "pool", "dve", "pe")}

        block = ctx.enter_context(nc.Block())

        @block.sync
        def _(sp):
            def load(dst, src):
                sp.dma_start(dst, src, allow_slow_non_contiguous=True).then_inc(S["attn_loaded"], 16)

            sp.dma_start(xr[:, 0, :].rearrange("p (i d) -> p i d", i=NT), x_v[:, 0]).then_inc(x_loaded[0], 16)
            for dst, src in ((wq_in, W_q), (wk_in, W_k), (wv, W_v), (wo, W_o)):
                load(dst[:, :], src)
            load(rwT[:, :], router_w.rearrange("e d -> d e"))
            for dst, src in ((bq, b_q), (bk_in, b_k)):
                for c in range(4):
                    load(dst[32 * c:32 * c + 32, :], split_heads(src)[c // 2, c % 2])
            load(rk_all[:, :, :], rel_k[0:3, :].partition_broadcast(P))
            load(bv_col[:, :], b_v.rearrange("(d o) -> d o", o=1))
            load(rv0_col[:, :], rel_v[0, :].partition_broadcast(H))
            load(bo_in[:, :], b_o.partition_broadcast(P))
            load(rv[:, :, :], rel_v[0:3, :].partition_broadcast(P))
            load(rb[:, :], router_bias.partition_broadcast(P))

            sp.dma_start(xr[:, 1, :].rearrange("p (i d) -> p i d", i=NT), x_v[:, 1]).then_inc(x_loaded[1], 16)

            xe_loaded = [S["xe_loaded0"], S["xe_loaded1"]]

            def load_xe(s, par):
                sp.dma_start(xeT[par][:, :], xnT_dram[s]).then_inc(xe_loaded[par], 16)

            def stacks_out(st, s, half):
                par, prs = s % 2, slice(4 * half, 4 * half + 4)
                if st.u is None and s < 2:
                    sp.wait_ge(S["k_rows"], 2 * s + 2)
                    sp.wait_ge(S["q_rows"], s + 1)
                for stks, parts in (((qs[par], qs[par]), (qh, qh, ql, ql)), (ks[par], (kh, kl, kh, kl))):
                    for b, stk in enumerate(stks):
                        for r, part in enumerate(parts):
                            lo = 64 * b + D * r
                            src = 64 * b + 32 * half
                            sp.dma_start(stk[lo:lo + D, prs, :], part[src:src + 32, :]).then_inc(stacks[par][half], 16)

            def maxima_out(st, s, half):
                wait_apart(sp, S["misc_free"], st.misc(f"m{half}") + 1, passed["sp"])
                for b in range(2):
                    row = M_ROW + b
                    sp.dma_start(qs[s % 2][row:row + 1, 4 * half:4 * half + 4, :],
                                 mT[half][b:H // 2:2, :]).then_inc(mrow[half], 16)

            def step(st):
                if st.t0 == 0:
                    sp.dma_start(xr[:, 2:, :].rearrange("p b (i d) -> p b i d", i=NT),
                                 x_v[:, 2:]).then_inc(x_loaded[2], 16)
                if st.A:
                    need(sp, S["exp_full"], st.at(SLOTS * (st.a - 1), SLOTS))
                    stacks_out(st, st.a, 1)
                if st.B:
                    maxima_out(st, st.b, 1)
                if st.t0 == NSEQ + 1:
                    sp.wait_ge(S["exp_full"], SLOTS * (NSEQ - 1))
                    for dst, src in ((w_first[:, 0:2, :], sw1.rearrange("d (c h) -> d c h", c=NC)),
                                     (w_first[:, 2:4, :], sw3.rearrange("d (c h) -> d c h", c=NC)),
                                     (w_first[:, 4:, :], ew1.rearrange("e d h -> d e h")),
                                     (w_second[:, 0:NC, :], sw2.rearrange("(c p) d -> p c d", p=P)),
                                     (w_second[:, NC:, :], ew2.rearrange("e h d -> h e d"))):
                        sp.dma_start(dst, src).then_inc(S["ffn_loaded"], 16)
                if st.A:
                    maxima_out(st, st.a, 0)
                if st.F:
                    wait_apart(sp, S["qk_split"], st.at(2 * (st.f + 1), 2), passed["sp"])
                    need(sp, S["exp_full"], st.at(SLOTS * (st.f - 2) + SLOTS // 2, SLOTS))
                    stacks_out(st, st.f, 0)
                if st.t0 == NSEQ + 2:
                    sp.wait_ge(S["av_full"], NGRP * NSEQ)
                    sp.wait_ge(S["xnT_stored"], 16 * (NSEQ - 1))
                    load_xe(0, 0)
                    load_xe(1, 1)
                if st.C:
                    wait_apart(sp, S["misc_free"], st.misc("xn2") + 1, passed["sp"])
                    sp.dma_start(xnT_dram[st.seq(st.c)], xn2T[:, :]).then_inc(S["xnT_stored"], 16)

            steps(sp, step)

            def ffn(f):
                if f.s0 + 2 < NSEQ:
                    wait_apart(sp, S["xe_split"], f.at(1, 1), passed["sp"])
                    load_xe(f.seq(f.s0 + 2), f.s0 % 2)
                if f.s0 > 0:
                    result_out(f, -1)

            def result_out(f, s):
                wait_apart(sp, S["out_ready"], f.at(s + 1, 1), passed["sp"])
                sp.dma_start(out_v[:, f.seq(f.s0 + s)], result[:, :].rearrange("p (i d) -> p i d", i=NT)).then_inc(
                    S["stored"], 16)

            sp.wait_ge(S["xnT_stored"], 16 * NSEQ)
            ffn_steps(sp, ffn)
            result_out(Ffn(NSEQ - 1), 0)
            sp.wait_ge(S["stored"], 16 * NSEQ)

        @block.gpsimd
        def _(pool):
            def zeros(ins):
                ins.then_inc(S["const_made"], 1)

            zeros(pool.memset(ident[:, :], 0.0))
            zeros(pool.memset(ident16[:, :], 0.0))
            zeros(pool.memset(identb[:, :], 0.0))
            zeros(pool.memset(maskb[:, :], 0.0))
            zeros(pool.memset(head_sel[:, :, :, :], 0.0))
            zeros(pool.memset(neg_half[:, :], -0.5))
            zeros(pool.memset(m_col[:, :], 0.0))
            zeros(pool.memset(e1[:, 0:1], MASKED / D))
            zeros(pool.memset(xnT[:, 0:1], 0.0))
            zeros(pool.memset(head_sum[:, :], 0.0))
            pool.wait_ge(S["const_made"], N_CONST_MADE)
            for m in (ident, ident16, identb):
                pool.affine_select(out=m[:, :], in_=m[:, :], compare_op=ALU.not_equal, fill=1.0, base=0,
                                   pattern=[[-1, P]], channel_multiplier=1).then_inc(S["const_ready"], 1)
            pool.affine_select(out=maskb[:, :], in_=maskb[:, :], compare_op=ALU.is_ge, fill=MASKED, base=-1,
                               pattern=[[-1, DIAG]], channel_multiplier=1).then_inc(S["const_ready"], 1)
            for half in range(2):
                v = head_sel[:, :, 4 * half:4 * half + 4, :]
                pool.affine_select(out=v, in_=v, compare_op=ALU.not_equal, fill=1.0, base=-32 * half,
                                   pattern=[[-4, D], [-1, NPAIR // 2], [-64, 2]],
                                   channel_multiplier=1).then_inc(S["const_ready"], 1)
            pool.affine_select(out=m_col[:, :], in_=m_col[:, :], compare_op=ALU.not_equal, fill=-M_UNIT,
                               base=-M_ROW, pattern=[[-1, 2]], channel_multiplier=1).then_inc(S["const_ready"], 1)

            def selectors():
                pool.memset(sel_e[:, :, :], 0.0).then_inc(S["ffn_const"], 1)
                pool.iota(iota_i[:, :], pattern=[[1, NE]], base=0, channel_multiplier=0).then_inc(S["ffn_const"], 1)
                pool.memset(gate3[:, :, :], 0.0).then_inc(S["ffn_const"], 1)
                for r in range(3):
                    pool.wait_ge(S["ffn_const"], 3 + r)
                    pool.affine_select(out=sel_e[:, :, :], in_=sel_e[:, :, :], compare_op=ALU.not_equal, fill=1.0,
                                       base=-NE * r, pattern=[[-1, NE], [0, P]],
                                       channel_multiplier=1).then_inc(S["ffn_const"], 1)
                pool.wait_ge(S["ffn_const"], 6)
                pool.tensor_copy(iota_f[:, :], iota_i[:, :]).then_inc(S["ffn_const"], 1)

            own = Own(pool, S["pool_own"], CHAIN_POOL)

            def normalise(st, seq, dst, src, mv, var, rs, got):
                wait_apart(pool, S[got], st.at(seq + 1, 1), passed["pool"])
                own.mark(pool.tensor_scalar(var[:, :], mv[:, :, 1], 1.0, EPS, ALU.mult, ALU.add))
                own.mark(pool.tensor_tensor(dst, src, mv[:, :, 0:1].to_broadcast([P, NT, P]), ALU.subtract))
                own.settle()
                own.mark(pool.tensor_tensor(rs[:, :], var[:, :], neg_half[:, :], ALU.pow))
                own.settle()
                return pool.tensor_tensor(dst, dst, rs[:, :].unsqueeze(2).to_broadcast([P, NT, P]), ALU.mult)

            def tiles(v):
                return v.rearrange("p (t c) -> p t c", t=NT)

            def mask_tiles(st, lo, hi):
                for pr, kt in ((i // NT, i % NT) for i in range(lo, hi)):
                    wait_apart(pool, S["exp_done"],
                               st.at(2 * NPAIR * NT * st.b + 2 * NT * pr + 2 * kt + 2, 2 * NPAIR * NT), passed["pool"])
                    w = min(DIAG, WIDTH[kt])
                    v = prob[pr % PBUF][:, :, START[kt]:START[kt] + w]
                    pool.affine_select(out=v, in_=v, compare_op=ALU.is_ge, fill=0.0, base=-2,
                                       pattern=[[0, 2], [1, w]], channel_multiplier=-1).then_inc(S["p_masked"], 1)

            def near_half(st, s, half):
                pool.wait_ge(S["p_ready"], st.at(2 * s + half + 1, 2))
                if half == 0:
                    pool.wait_ge(wide_free[st.wide("v")[1]], st.wide_before("v") + 1)
                    need(pool, S["o_ready"], st.at(NGRP * (s - 1), NGRP))
                hs = slice(half * 8, half * 8 + 8)
                cols = slice(half * 64, half * 64 + 64)
                for n in range(2):
                    a = v_near[:, n, :, cols].rearrange("p t (h d) -> p t h d", d=D)
                    o = pv_near[:, n, :, cols].rearrange("p t (h d) -> p t h d", d=D)
                    pb = p01[:, n, :, hs].unsqueeze(3).to_broadcast([P, NT, 8, D])
                    own.mark(pool.tensor_tensor(o, a, pb, ALU.mult))
                pool.tensor_tensor(p_near[s % 2][:, :, hs], p01[:, 0, :, hs], p01[:, 1, :, hs],
                                   ALU.add).then_inc(S["near_ready"], 1)
                own.settle()
                pool.tensor_tensor(near[s % 2][:, :, cols], pv_near[:, 0, :, cols], pv_near[:, 1, :, cols],
                                   ALU.add).then_inc(S["near_ready"], 1)

            def step(st):
                own.begin(st)

                def masks(lo, hi):
                    if st.B:
                        mask_tiles(st, lo, hi)

                if st.B:
                    near_half(st, st.b, 1)
                masks(0, 8)
                if st.F:
                    normalise(st, st.f, xn[:, :, :], tiles(xr[:, st.seq(st.f), :]), mv1, var1, rs1,
                              "stats1").then_inc(S["xn_ready"], 1)
                masks(8, 16)
                if st.C:
                    own.mark(normalise(st, st.c, y[:, :, :], y[:, :, :], mv2, var2, rs2, "stats2"))
                    own.settle()
                    xv = xr[:, st.seq(st.c), :]
                    pool.tensor_tensor(xv, xv, y[:, :, :].rearrange("p i d -> p (i d)"),
                                       ALU.add).then_inc(S["x1_ready"], 1)
                if st.t0 == 1:
                    selectors()
                masks(16, 25)
                if st.C:
                    normalise(st, st.c, xn2[:, :, :], tiles(xr[:, st.seq(st.c), :]), mv3, var3, rs3,
                              "stats3").then_inc(S["xn2_ready"], 1)
                if st.A:
                    near_half(st, st.a, 0)
                masks(25, 32)
                own.end()

            steps(pool, step)

            own2 = Own(pool, S["pool_own2"], CHAIN_FFN_POOL)

            def end_centre(f, seq, st0):
                need(pool, S["out_ready"], f.at(st0, 1))
                wait_apart(pool, S["stats4"], f.at(st0 + 1, 1), passed["pool"])
                own2.mark(pool.tensor_scalar(var2[:, :], mv2[:, :, 1], 1.0, EPS, ALU.mult, ALU.add))
                own2.mark(pool.tensor_tensor(z[:, :, :], tiles(f_tok[:, :]), mv2[:, :, 0:1].to_broadcast([P, NT, P]),
                                             ALU.subtract))

            def end_rstd(f, seq, st0):
                own2.settle()
                own2.mark(pool.tensor_tensor(rs2[:, :], var2[:, :], neg_half[:, :], ALU.pow))

            def end_scale(f, seq, st0):
                own2.settle()
                pool.tensor_tensor(z[:, :, :], z[:, :, :], rs2[:, :].unsqueeze(2).to_broadcast([P, NT, P]),
                                   ALU.mult).then_inc(S["z4_ready"], 1)

            def end_add(f, seq, st0):
                pool.wait_ge(S["z4_ready"], f.at(st0 + 1, 1))
                need(pool, S["stored"], f.at(16 * st0, 16))
                pool.tensor_tensor(result[:, :], xr[:, seq, :], z[:, :, :].rearrange("p i d -> p (i d)"),
                                   ALU.add).then_inc(S["out_ready"], 1)

            def low_half(f, i):
                pool.wait_ge(S["high_ready"], f.at(i + 1, len(UNITS)))
                pool.tensor_tensor(hidden_low[hid(f, i)][:, :].bitcast(F32R), hidden[hid(f, i)][:, :],
                                   hidden_high[hid(f, i)][:, :], ALU.subtract).then_inc(S["low_ready"], 1)

            end_parts = {5: end_centre, 6: end_rstd, 8: end_scale, 9: end_add}

            def ffn(f):
                own2.begin_ffn(f)
                for i in range(len(UNITS)):
                    low_half(f, i)
                    if f.s0 > 0 and i in end_parts:
                        end_parts[i](f, f.seq(f.s0 - 1), -1)
                own2.end_ffn(f)

            ffn_steps(pool, ffn)
            for part in end_parts.values():
                part(Ffn(NSEQ - 1), NSEQ - 1, 0)

        @block.scalar
        def _(act):
            def key_rows(i):
                act.wait_ge(S["const_ready"], N_POOL_CONST)
                act.wait_ge(S["k_zeros"], 2 * i + 2)
                for b in range(2):
                    act.copy(ks[i][b][96:P, :, :], m_col[96:P, b:b + 1].unsqueeze(2).to_broadcast(
                        [32, NPAIR, SEQ])).then_inc(S["k_rows"], 1)

            def exp_unit(st, pr, n):
                i = 2 * NT * pr + n
                kt, b = n // 2, n % 2
                act.wait_ge(S["exp_full"], st.at(2 * NPAIR * NT * st.b + i + 1, 2 * NPAIR * NT))
                if n == 0 and pr % 2 == 0:
                    need(act, S["av_full"], st.at(NGRP * st.b + pr // 2 - 1, NGRP))
                w = WIDTH[kt]
                act.activation(prob[pr % PBUF][:, b, START[kt]:START[kt] + w], ps_exp[b][:, 0:w], ACT.Exp,
                               scale=SCALE).then_inc(S["exp_done"], 1)

            def xT_out(st):
                n, unit = st.wide("xT")
                act.wait_ge(S["wide_full"], n + 1)
                act.copy(xnT[:, 1:1 + SEQ], ps_wide[unit][:, 0, :]).then_inc(wide_free[unit], 1)

            def qk_out(st):
                n, unit = st.wide("qk")
                act.wait_ge(S["wide_full"], n + 1)
                if st.t0 == 0:
                    act.wait_ge(S["const_ready"], N_CONST)
                if st.f > 0:
                    act.wait_ge(S["e_ready"], st.at(2 * st.f, 2))
                    act.wait_ge(S["qk_split"], st.at(2 * st.f, 2))
                act.activation(qf[:, :], ps_wide[unit][:, 0, :], ACT.Identity, bias=bq[:, :]).then_inc(S["qk_ready"], 1)
                act.activation(kf[:, :], ps_wide[unit][:, 1, :], ACT.Identity, bias=bk[:, :]).then_inc(wide_free[unit], 1)

            def v_out(st):
                n, unit = st.wide("v")
                act.wait_ge(S["wide_full"], n + 1)
                need(act, S["av_full"], st.at(NGRP * (st.a - 1), NGRP))
                if st.u is None and st.a < 2:
                    act.wait_ge(S["v_rows"], 2 * st.a + 2)
                act.copy(vp[st.a % 2][:, :, :, 0:D].rearrange("p t h d -> p (t h) d"),
                         ps_wide[unit][:, 0, :].rearrange("p (c d) -> p c d", d=D)).then_inc(S["v_ready"], 1)

            def oT_out(st):
                n, unit = st.wide("oT")
                act.wait_ge(S["wide_full"], n + 1)
                need(act, S["xnT_stored"], st.at(16 * st.c, 16))
                act.copy(oT[:, :], ps_wide[unit][:, 0, :]).then_inc(wide_free[unit], 1)

            def s_rows_out(st):
                act.wait_ge(S["misc_full"], st.misc("e_sums") + 1)
                act.copy(s_rows[:, :], ps_misc[0:64, :]).then_inc(S["misc_free"], 1)

            def av_out(st, s, g):
                act.wait_ge(S["av_full"], st.at(NGRP * s + g + 1, NGRP))
                act.copy(av_s[g % 2][:, :], ps_av[:, :]).then_inc(S["av_copied"], 1)

            def xn2T_out(st):
                act.wait_ge(S["misc_full"], st.misc("xn2") + 1)
                act.copy(xn2T[:, :], ps_misc[:, :]).then_inc(S["misc_free"], 1)

            def logits_out(st):
                act.wait_ge(S["misc_full"], st.misc("logits") + 1)
                act.activation(logit[:, st.seq(st.c), :], ps_misc[:, 0:NT * NE], ACT.Exp,
                               scale=-1.0).then_inc(S["misc_free"], 1)

            def mT_out(st, s, half):
                act.wait_ge(S["misc_full"], st.misc(f"m{half}") + 1)
                if s > 0:
                    act.wait_ge(mrow[half], st.at(32 * s, 32))
                act.copy(mT[half][:, :], ps_misc[:, :].bitcast(F16)[0:H // 2, 0:SEQ]).then_inc(S["misc_free"], 1)

            def p_near_exp(st, s, half):
                act.wait_ge(S["d_ready"], st.at(2 * s + half + 1, 2))
                need(act, S["near_ready"], st.at(4 * (s - 1) + 2 * half + 2, 4))
                hs = slice(half * 8, half * 8 + 8)
                act.activation(p01[:, :, :, hs].rearrange("p n t h -> p (n t) h"),
                               d01[:, :, :, hs].rearrange("p n t h -> p (n t) h"), ACT.Exp,
                               scale=SCALE).then_inc(S["p_ready"], 1)

            key_rows(0)

            def step(st):
                def exps(lo, hi):
                    if st.B:
                        for i in range(lo, hi):
                            exp_unit(st, i // (2 * NT), i % (2 * NT))

                exps(0, 7)
                if st.A:
                    s_rows_out(st)
                exps(7, 8)
                if st.B:
                    p_near_exp(st, st.b, 1)
                exps(8, 9)
                if st.B:
                    mT_out(st, st.b, 1)
                exps(9, 16)
                if st.C:
                    av_out(st, st.c, 3)
                exps(16, 21)
                if st.A:
                    v_out(st)
                exps(21, 25)
                if st.F:
                    xT_out(st)
                exps(25, 29)
                if st.C:
                    oT_out(st)
                exps(29, 32)
                if st.B:
                    av_out(st, st.b, 0)
                exps(32, 37)
                if st.F:
                    qk_out(st)
                exps(37, 40)
                if st.t0 == 0:
                    key_rows(1)
                exps(40, 43)
                if st.A:
                    mT_out(st, st.a, 0)
                exps(43, 44)
                if st.A:
                    p_near_exp(st, st.a, 0)
                exps(44, 48)
                if st.B:
                    av_out(st, st.b, 1)
                exps(48, 58)
                if st.C:
                    xn2T_out(st)
                exps(58, 62)
                if st.C:
                    logits_out(st)
                exps(62, 64)
                if st.B:
                    av_out(st, st.b, 2)

            steps(act, step)

            def gateT_out(f, ahead):
                act.wait_ge(S["gateT_full"], f.at(ahead + 1, 1))
                act.copy(gateT[:, :], ps_misc[:, :].bitcast(BF16)[0:64, 0:SEQ]).then_inc(S["gateT_ready"], 1)

            def end_out(f, s):
                act.wait_ge(S["second_done"], f.at(len(UNITS) * (s + 1), len(UNITS)))
                act.copy(fT[:, :], ps_av[:, :]).then_inc(S["fT_ready"], 1)

            def f_tok_out(f, s):
                act.wait_ge(S["f_tok_full"], f.at(s + 1, 1))
                need(act, S["z4_ready"], f.at(s, 1))
                act.copy(f_tok[:, :], ps_misc[:, :]).then_inc(S["f_tok_ready"], 1)

            def high_half(f, i):
                act.wait_ge(S["hidden_ready"], f.at(i + 1, len(UNITS)))
                need(act, S["second_done"], f.at(i + 1 - HIDDEN, len(UNITS)))
                act.copy(hidden_high[hid(f, i)][:, :].bitcast(F32R), hidden[hid(f, i)][:, :]).then_inc(S["high_ready"], 1)

            def ffn(f):
                if f.s0 == 0:
                    act.wait_ge(S["av_full"], NGRP * NSEQ)
                    gateT_out(f, 0)
                for i, (kind, k) in enumerate(UNITS):
                    if kind == "c":
                        act.wait_ge(S["front_full"], f.at(i + 1, len(UNITS)))
                        before = UNITS.index(("c", 1 - k)) + 1 - (0 if k else len(UNITS))
                        need(act, S["hidden_ready"], f.at(before, len(UNITS)))
                        act.activation(tanh_u[:, :], ps_wide[1][:, 0, :], ACT.Tanh, scale=0.5).then_inc(S["act_ready"], 1)
                    else:
                        act.wait_ge(S["front_full"], f.at(i + 1, len(UNITS)))
                        before = EXPERT_POS[k - 2] + 1 if k >= 2 else EXPERT_POS[k - 2] + 1 - len(UNITS)
                        need(act, S["hidden_ready"], f.at(before, len(UNITS)))
                        act.activation(act_out[k % 2][:, :], ps_exp[k % 2][:, :], ACT.Gelu).then_inc(S["act_ready"], 1)
                    if i == 0 and f.s0 > 0:
                        gateT_out(f, 0)
                    if i > 0 or f.s0 > 0:
                        high_half(f, i - 1)
                    if i == LAG - 1 and f.s0 > 0:
                        end_out(f, -1)
                    if i == LAG + 1 and f.s0 > 0:
                        f_tok_out(f, -1)

            ffn_steps(act, ffn)
            high_half(Ffn(NSEQ - 1), len(UNITS) - 1)
            end_out(Ffn(NSEQ - 1), 0)
            f_tok_out(Ffn(NSEQ - 1), 0)

        @block.vector
        def _(dve):
            own = Own(dve, S["dve_own"], CHAIN_DVE)

            def ready(ins):
                ins.then_inc(S["const_ready"], 1)

            def buffers(i):
                for b in range(2):
                    dve.memset(ks[i][b][:, :, :].bitcast(F32), 0.0).then_inc(S["k_zeros"], 1)
                dve.memset(qs[i][:, :, :].bitcast(F32), 0.0).then_inc(S["q_rows"], 1)
                dve.memset(vp[i][:, :, :, :], 0.0).then_inc(S["v_rows"], 1)
                dve.wait_ge(S["v_rows"], 2 * i + 1)
                dve.memset(vp[i][:, :, :, D:D + 1], 1.0).then_inc(S["v_rows"], 1)

            buffers(0)
            dve.wait_ge(S["attn_loaded"], 16 * N_ATTN_LOADS)
            dve.wait_ge(S["const_ready"], N_POOL_CONST)
            for dst, src in ((wq, wq_in), (wk, wk_in)):
                for b in range(2):
                    ready(dve.tensor_copy(dst[:, 64 * b:64 * b + 64].rearrange("p (hf d p4) -> p hf d p4", hf=2, d=D),
                                          src[:, :].rearrange("p (hf p4 b d) -> p b hf d p4", hf=2, b=2, d=D)[:, b]))
            ready(dve.tensor_reduce(head_sum[:, 0:H], head_sel[:, :, :, :].rearrange("p d pr b -> p (pr b) d"),
                                    AX.X, ALU.add))
            own.mark(dve.tensor_reduce(feature[:, :], head_sel[:, :, :, :].rearrange("p d pr b -> p d (pr b)"),
                                       AX.X, ALU.add))
            dve.wait_ge(S["dve_own"], 1)
            own.mark(dve.tensor_tensor(rk_own[:, :, :], rk_all[:, :, :],
                                       feature[:, :].unsqueeze(1).to_broadcast([P, 3, D]), ALU.mult))
            dve.wait_ge(S["dve_own"], 2)
            own.mark(dve.tensor_reduce(rk[:, :], rk_own[:, :, :], AX.X, ALU.add))
            dve.wait_ge(S["dve_own"], 3)
            ready(dve.tensor_tensor(bk[:, :], bk_in[:, :], rk[:, 0:1], ALU.add))
            ready(dve.tensor_scalar(dk[:, :], rk[:, 1:3], rk[:, 0:1], None, ALU.subtract))
            for i in range(2):
                ready(dve.tensor_tensor(dv[:, i, :].rearrange("p (h d) -> p h d", d=D),
                                        rv[:, i + 1, :].unsqueeze(1).to_broadcast([P, H, D]),
                                        rv[:, 0, :].unsqueeze(1).to_broadcast([P, H, D]), ALU.subtract))
            ready(dve.tensor_tensor(bias_v[:, :], bv_col[:, :].to_broadcast([P, P]),
                                    rv0_col[:, :].to_broadcast([P, P]), ALU.add))
            dve.wait_ge(S["const_ready"], N_CONST)
            dve.wait_ge(S["bias_full"], 1)
            dve.tensor_tensor(bo[:, :], ps_av[:, 0:P], bo_in[:, :], ALU.add).then_inc(S["bias_ready"], 1)
            dve.wait_ge(S["bias_ready"], 1)

            def bn(src, st_):
                for i in range(NT):
                    own.mark(dve.bn_stats(st_[:, i, :], src[:, i * P:i * P + P]))

            def aggregate(st_, mv, done):
                own.settle(passed["dve"])
                for i in range(NT):
                    last = dve.bn_aggr(mv[:, i, :], st_[:, i, :])
                    if i < NT - 1:
                        own.mark(last)
                last.then_inc(S[done], 1)

            def ln1_bn(st):
                dve.wait_ge(x_loaded[min(st.t0, 2)], 16)
                need(dve, S["xn_ready"], st.at(st.f, 1))
                bn(xr[:, st.seq(st.f), :], st1)

            def near_products(st):
                dve.wait_ge(S["qk_ready"], st.at(st.f + 1, 1))
                dve.wait_ge(wide_free[st.wide("qk")[1]], st.wide_before("qk") + 1)
                dve.scalar_tensor_tensor(e0[:, :], kf[:, :], dk[:, 1:2], qf[:, :], ALU.add,
                                         ALU.mult).then_inc(S["e_ready"], 1)
                dve.scalar_tensor_tensor(e1[:, 1:SEQ], kf[:, 0:SEQ - 1], dk[:, 0:1], qf[:, 1:SEQ], ALU.add,
                                         ALU.mult).then_inc(S["e_ready"], 1)

            def split(st):
                dve.wait_ge(S["qk_ready"], st.at(st.f + 1, 1))
                dve.wait_ge(wide_free[st.wide("qk")[1]], st.wide_before("qk") + 1)
                if st.f > 0:
                    for half in range(2):
                        dve.wait_ge(stacks[(st.f - 1) % 2][half], st.at(256 * ((st.f - 1) // 2 + 1), 128))
                own.mark(dve.tensor_copy(qh[:, :], qf[:, :]))
                own.mark(dve.tensor_copy(kh[:, :], kf[:, :]))
                own.settle()
                dve.tensor_tensor(ql[:, :], qf[:, :], qh[:, :], ALU.subtract).then_inc(S["qk_split"], 1)
                dve.tensor_tensor(kl[:, :], kf[:, :], kh[:, :], ALU.subtract).then_inc(S["qk_split"], 1)

            def values_out(st):
                n, unit = st.wide("v")
                dve.wait_ge(S["wide_full"], n + 1)
                need(dve, S["near_ready"], st.at(4 * st.a, 4))
                for i in (1, 0):
                    if i == 0:
                        dve.wait_ge(S["v_ready"], st.at(st.a + 1, 1))
                    last = dve.tensor_tensor(v_near[:, i], ps_wide[unit][:, i, :].rearrange("p (t c) -> p t c", t=NT),
                                             dv[:, 1 - i, :].unsqueeze(1).to_broadcast([P, NT, P]), ALU.add)
                    if i == 1:
                        own.mark(last)
                last.then_inc(wide_free[unit], 1)

            def s_max(st, i):
                pr, qt = i // NT, i % NT
                n, unit = st.wide(f"s{i}")
                dve.wait_ge(S["wide_full"], n + 1)
                dve.tensor_reduce(mx[:, qt, 2 * pr:2 * pr + 2], ps_wide[unit][:, :, 0:P * (qt + 1)], AX.X,
                                  ALU.max).then_inc(wide_free[unit], 1)

            def s_tok_out(st):
                dve.wait_ge(S["misc_full"], st.misc("s_tok") + 1)
                src = ps_misc[:, 0:NT * 64].rearrange("p (t n r) -> p n t r", t=NT, n=2)[:, :, :, 0:H]
                for n in range(2):
                    last = dve.tensor_copy(s_tok[:, n], src[:, n])
                    if n == 0:
                        own.mark(last)
                last.then_inc(S["misc_free"], 1)
                dve.wait_ge(S["misc_free"], st.misc("s_tok") + 1)

            def max_half(st, s, half):
                hs = slice(half * 8, half * 8 + 8)
                then = st if half == 0 else Step(st.t0 - 1, st.u)
                for i in (1, 2):
                    what = f"s{NPAIR * NT // 2 * (half + 1) - i}"
                    dve.wait_ge(wide_free[then.wide(what)[1]], then.wide_before(what) + 1)
                own.mark(dve.tensor_tensor(mxa[:, :, hs], mx[:, :, hs], s_tok[:, 0, :, hs], ALU.max))
                own.settle()
                own.mark(dve.tensor_tensor(mx[:, :, hs], mxa[:, :, hs], s_tok[:, 1, :, hs], ALU.max))
                own.settle()
                need(dve, S["p_ready"], st.at(2 * (s - 1) + half + 1, 2))
                dve.tensor_scalar(m16[:, :, hs], mx[:, :, hs], 1.0 / M_UNIT, None, ALU.mult).then_inc(S["m16_ready"], 1)
                dve.wait_ge(S["m16_ready"], st.at(2 * s + half + 1, 2))
                for k in range(2):
                    last = dve.scalar_tensor_tensor(d01[:, k, :, hs], m16[:, :, hs], -M_UNIT, s_tok[:, k, :, hs],
                                                    ALU.mult, ALU.add)
                    if k == 0:
                        own.mark(last)
                last.then_inc(S["d_ready"], 1)

            def av_tok_out(st, s, g):
                dve.wait_ge(S["misc_full"], st.misc(f"av{g}") + 1)
                if g == 0:
                    dve.wait_ge(S["near_ready"], st.at(4 * s + 2, 4))
                if g == 2:
                    dve.wait_ge(S["near_ready"], st.at(4 * s + 4, 4))
                need(dve, S["o_ready"], st.at(NGRP * s + g, NGRP))
                v = ps_misc[:, :].rearrange("p (t j c) -> p t j c", t=NT, j=4)
                par = s % 2
                own.mark(dve.tensor_tensor(den[:, :, :], v[:, :, :, D], p_near[par][:, :, 4 * g:4 * g + 4], ALU.add))
                cols = slice(4 * g * D, 4 * g * D + 4 * D)
                dve.tensor_tensor(num[:, :, :, :], v[:, :, :, 0:D], near[par][:, :, cols].rearrange(
                    "p t (j d) -> p t j d", d=D), ALU.add).then_inc(S["misc_free"], 1)
                own.settle()
                own.mark(dve.reciprocal(rden[:, :, :], den[:, :, :]))
                own.settle()
                dve.wait_ge(S["misc_free"], st.misc(f"av{g}") + 1)
                dve.tensor_tensor(o_tok[:, :, cols].rearrange("p t (j d) -> p t j d", d=D), num[:, :, :, :],
                                  rden[:, :, :].unsqueeze(3).to_broadcast([P, NT, 4, D]),
                                  ALU.mult).then_inc(S["o_ready"], 1)

            def y_out(st):
                n, unit = st.wide("oproj")
                dve.wait_ge(S["wide_full"], n + 1)
                dve.tensor_tensor(y[:, :, :], ps_wide[unit][:, 0, :].rearrange("p (t c) -> p t c", t=NT),
                                  bo[:, :].unsqueeze(1).to_broadcast([P, NT, P]), ALU.add).then_inc(wide_free[unit], 1)

            def y_bn(st):
                _, unit = st.wide("oproj")
                dve.wait_ge(wide_free[unit], st.wide_before("oproj") + 1)
                bn(y[:, :, :].rearrange("p t c -> p (t c)"), st2)

            def x1_bn(st):
                dve.wait_ge(S["x1_ready"], st.at(st.c + 1, 1))
                bn(xr[:, st.seq(st.c), :], st3)

            own2 = Own(dve, S["dve_own2"], CHAIN_FFN)
            own2.st = Step(0)

            def do(ins):
                own2.mark(ins)
                own2.settle()

            def gates_scores(f, ahead):
                score = logit[:, f.seq(f.s0 + ahead), :].rearrange("p (t e) -> p t e", e=NE)
                do(dve.tensor_scalar(score, score, 1.0, None, ALU.add))
                dve.sem_inc(passed["dve"], 1)
                do(dve.reciprocal(score, score))
                own2.mark(dve.tensor_tensor(sel[:, :, :], score, rb[:, :].unsqueeze(1).to_broadcast([P, NT, NE]),
                                            ALU.add))

            def gates_top(f, ahead):
                own2.settle(passed["dve"])
                for t in range(NT):
                    own2.mark(dve.max(top[:, t, :], sel[:, t, :]))
                own2.settle(passed["dve"])
                for t in range(NT):
                    own2.mark(dve.max_index(top_i[:, t, :], top[:, t, :], sel[:, t, :]))

            def gates_found(f, ahead):
                own2.settle()
                do(dve.tensor_copy(top_f[:, :, :], top_i[:, :, 0:2]))
                it = iota_f[:, :].unsqueeze(1).to_broadcast([P, NT, NE])
                for k in range(2):
                    own2.mark(dve.tensor_tensor(is_top[:, k], it, top_f[:, :, k:k + 1].to_broadcast([P, NT, NE]),
                                                ALU.is_equal))
                own2.settle()
                own2.mark(dve.tensor_tensor(in_two[:, :, :], is_top[:, 0], is_top[:, 1], ALU.add))

            def gates_chosen(f, ahead):
                score = logit[:, f.seq(f.s0 + ahead), :].rearrange("p (t e) -> p t e", e=NE)
                own2.settle()
                do(dve.tensor_tensor(chosen[:, :, :], in_two[:, :, :], score, ALU.mult))
                do(dve.tensor_reduce(total[:, :], chosen[:, :, :], AX.X, ALU.add))
                own2.mark(dve.tensor_scalar(normal[:, :], total[:, :], 1e-9, None, ALU.is_gt))
                own2.mark(dve.tensor_scalar(total_e[:, :], total[:, :], 1e-9, None, ALU.add))

            def gates_shares(f, ahead):
                own2.settle()
                own2.mark(dve.tensor_scalar(even[:, :], normal[:, :], -0.5, 0.5, ALU.mult, ALU.add))
                do(dve.reciprocal(total[:, :], total_e[:, :]))
                do(dve.tensor_tensor(total[:, :], total[:, :], normal[:, :], ALU.mult))
                own2.mark(dve.tensor_tensor(gate_n[:, :, :], chosen[:, :, :],
                                            total[:, :].unsqueeze(2).to_broadcast([P, NT, NE]), ALU.mult))
                do(dve.tensor_tensor(gate_r[:, :, :], in_two[:, :, :],
                                     even[:, :].unsqueeze(2).to_broadcast([P, NT, NE]), ALU.mult))
                own2.mark(dve.tensor_tensor(gate[:, :, :], gate_n[:, :, :], gate_r[:, :, :], ALU.add))

            def gates_parts(f, ahead):
                own2.settle()
                need(dve, S["gateT_full"], f.at(ahead, 1))
                do(dve.tensor_copy(gate3[:, :, 0:NE], gate[:, :, :]))
                do(dve.tensor_tensor(gate_r[:, :, :], gate[:, :, :], gate3[:, :, 0:NE], ALU.subtract))
                do(dve.tensor_copy(gate3[:, :, NE:2 * NE], gate_r[:, :, :]))
                dve.tensor_tensor(gate3[:, :, 2 * NE:3 * NE], gate_r[:, :, :], gate3[:, :, NE:2 * NE],
                                  ALU.subtract).then_inc(S["chosen_ready"], 1)

            def first_gates():
                dve.wait_ge(S["misc_free"], Step(3).misc("logits") + 1)
                dve.wait_ge(S["ffn_const"], 7)
                for part in (gates_scores, gates_top, gates_found, gates_chosen, gates_shares, gates_parts):
                    part(Ffn(0), 0)

            def step(st):
                own.begin(st)

                def maxima(lo, hi):
                    if st.A:
                        for i in range(lo, hi):
                            s_max(st, i)

                if st.B:
                    max_half(st, st.b, 1)
                maxima(0, 1)
                if st.C:
                    av_tok_out(st, st.c, 2)
                maxima(1, 3)
                if st.F:
                    ln1_bn(st)
                maxima(3, 4)
                if st.F:
                    aggregate(st1, mv1, "stats1")
                maxima(4, 8)
                if st.A:
                    s_tok_out(st)
                maxima(8, 10)
                if st.A:
                    values_out(st)
                maxima(10, 12)
                if st.C:
                    av_tok_out(st, st.c, 3)
                maxima(12, 16)
                if st.C:
                    y_out(st)
                maxima(16, 17)
                if st.C:
                    y_bn(st)
                maxima(17, 18)
                if st.C:
                    aggregate(st2, mv2, "stats2")
                if st.A:
                    max_half(st, st.a, 0)
                maxima(18, 19)
                if st.B:
                    av_tok_out(st, st.b, 0)
                maxima(19, 21)
                if st.F:
                    split(st)
                maxima(21, 22)
                if st.C:
                    x1_bn(st)
                maxima(22, 24)
                if st.C:
                    aggregate(st3, mv3, "stats3")
                maxima(24, 25)
                if st.F:
                    near_products(st)
                if st.t0 == 0:
                    buffers(1)
                maxima(25, 27)
                if st.B:
                    av_tok_out(st, st.b, 1)
                maxima(27, 32)
                if st.t0 == NSEQ + 1:
                    first_gates()
                own.end()

            steps(dve, step)

            def end_stats(f, s):
                need(dve, S["z4_ready"], f.at(s, 1))
                dve.wait_ge(S["f_tok_ready"], f.at(s + 1, 1))
                for i in range(NT):
                    own2.mark(dve.bn_stats(st2[:, i, :], f_tok[:, i * P:i * P + P]))
                own2.settle(passed["dve"])
                for i in range(NT):
                    last = dve.bn_aggr(mv2[:, i, :], st2[:, i, :])
                    if i < NT - 1:
                        own2.mark(last)
                last.then_inc(S["stats4"], 1)

            def split_rows_high(f, ahead):
                par = (f.s0 + ahead) % 2
                n = f.s0 + ahead
                dve.wait_ge([S["xe_loaded0"], S["xe_loaded1"]][par],
                            16 * (n // 2 + 1) if f.u is None else f.u * 16 + 16 * (n // 2 + 1))
                need(dve, S["front_full"], f.at(len(UNITS) * (ahead - 1), len(UNITS)))
                own2.mark(dve.tensor_copy(xe_high[par][:, :].bitcast(F32R), xeT[par][:, :]))

            def split_rows_low(f, ahead):
                par = (f.s0 + ahead) % 2
                own2.settle()
                dve.tensor_tensor(xe_low[par][:, :].bitcast(F32R), xeT[par][:, :], xe_high[par][:, :],
                                  ALU.subtract).then_inc(S["xe_split"], 1)

            def split_weights():
                dve.wait_ge(S["ffn_loaded"], 16 * 5)
                do(dve.tensor_copy(w_high[:, :, :].bitcast(F32R), w_first[:, :, :]))
                dve.tensor_tensor(w_low[:, :, :].bitcast(F32R), w_first[:, :, :], w_high[:, :, :],
                                  ALU.subtract).then_inc(S["w_split"], 1)

            def split_second_weights():
                do(dve.tensor_copy(w2_high[:, :, :].bitcast(F32R), w_second[:, :, :]))
                dve.tensor_tensor(w2_low[:, :, :].bitcast(F32R), w_second[:, :, :], w2_high[:, :, :],
                                  ALU.subtract).then_inc(S["w_split"], 1)

            ahead_parts = {0: split_rows_high, 1: gates_scores, 2: gates_top, 3: split_rows_low, 4: gates_found,
                           6: gates_chosen, 7: gates_shares, 8: gates_parts}

            def ffn(f):
                own2.begin_ffn(f)
                if f.s0 == 0:
                    dve.wait_ge(S["av_full"], NGRP * NSEQ)
                for i, (kind, k) in enumerate(UNITS):
                    dve.wait_ge(S["act_ready"], f.at(i + 1, len(UNITS)))
                    need(dve, S["low_ready"], f.at(i + 1 - HIDDEN, len(UNITS)))
                    if kind == "c":
                        need(dve, S["hidden_ready"], f.at(i, len(UNITS)))
                        do(dve.scalar_tensor_tensor(silu2[:, :], tanh_u[:, :], 1.0, ps_wide[1][:, 0, :], ALU.add, ALU.mult))
                        dve.scalar_tensor_tensor(hidden[hid(f, i)][:, :], silu2[:, :], 0.5, ps_wide[1][:, 1, :], ALU.mult,
                                                 ALU.mult).then_inc(S["hidden_ready"], 1)
                    else:
                        dve.tensor_tensor(hidden[hid(f, i)][:, :], act_out[k % 2][:, :], ps_wide[0][:, k % 2, :],
                                          ALU.mult).then_inc(S["hidden_ready"], 1)
                    if i in ahead_parts and f.s0 < NSEQ - 1:
                        ahead_parts[i](f, 1)
                    if i == LAG + 1 and f.s0 > 0:
                        end_stats(f, -1)
                own2.end_ffn(f)

            split_weights()
            split_rows_high(Ffn(0), 0)
            split_rows_low(Ffn(0), 0)
            dve.wait_ge(S["av_full"], NGRP * NSEQ)
            split_second_weights()
            dve.wait_ge(S["misc_free"], Step(NSEQ + 2).misc("logits") + 1)
            ffn_steps(dve, ffn)
            end_stats(Ffn(NSEQ - 1), 0)

        @block.tensor
        def _(pe):
            def wide(st, what):
                _, unit = st.wide(what)
                need(pe, wide_free[unit], st.wide_before(what))
                return ps_wide[unit]

            def misc(st, what):
                need(pe, S["misc_free"], st.misc(what))
                return ps_misc

            def exp_unit(st, pr, n):
                i = 2 * NT * pr + n
                kt, b = n // 2, n % 2
                par = st.b % 2
                need(pe, S["exp_done"], st.at(2 * NPAIR * NT * st.b + i - 1, 2 * NPAIR * NT))
                if n == 0 and pr % 4 == 0:
                    pe.wait_ge(mrow[pr // 4], st.at(32 * (st.b + 1), 32))
                w = WIDTH[kt]
                pe.matmul(ps_exp[b][:, 0:w], ks[par][b][:, pr, P * kt:P * kt + P], qs[par][:, pr, P * kt:SEQ],
                          start=True, stop=True).then_inc(S["exp_full"], 1)

            def s_unit(st, i):
                pr, qt = i // NT, i % NT
                par = st.a % 2
                if qt == 0 and pr % 4 == 0:
                    pe.wait_ge(stacks[par][pr // 4], st.at(256 * (st.a // 2 + 1), 128))
                if i == 0 and st.a < 2:
                    pe.wait_ge(S["k_rows"], 2 * st.a + 2)
                    pe.wait_ge(S["q_rows"], st.a + 1)
                u = wide(st, f"s{i}")
                w = P * (qt + 1)
                lo = max(w - DIAG, 0)
                for b in range(2):
                    pe.matmul(u[:, b, 0:w], qs[par][0:M_ROW, pr, P * qt:P * qt + P], ks[par][b][0:M_ROW, pr, 0:w],
                              start=True, stop=False)
                for b in range(2):
                    last = pe.matmul(u[:, b, lo:w], identb[:, :], maskb[:, DIAG - (w - lo):DIAG],
                                     start=False, stop=True)
                last.then_inc(S["wide_full"], 1)

            def av_part(st, s, g, kt):
                par = s % 2
                n = NPAIR * NT * s
                pe.wait_ge(S["p_masked"], st.at(n + NT * (2 * g + 1) + kt + 1, NPAIR * NT))
                if kt == 0:
                    need(pe, S["av_copied"], st.at(NGRP * s + g, NGRP))
                    if g == 0:
                        pe.wait_ge(S["v_ready"], st.at(s + 1, 1))
                w = WIDTH[kt]
                for j in range(4):
                    pr, b = 2 * g + j // 2, j % 2
                    last = pe.matmul(ps_av[32 * j:32 * j + 32, P * kt:SEQ], vp[par][:, kt, 4 * g + j, :],
                                     prob[pr % PBUF][:, b, START[kt]:START[kt] + w],
                                     start=(kt == 0), stop=(kt == NT - 1))
                if kt == NT - 1:
                    last.then_inc(S["av_full"], 1)

            def transposes(dst, src, unit, done):
                for i in range(NT):
                    last = pe.transpose(dst(i), src(i), unit)
                last.then_inc(done, 1)

            def x_transpose(st):
                u = wide(st, "xT")
                pe.wait_ge(S["xn_ready"], st.at(st.f + 1, 1))
                transposes(lambda i: u[:, 0, i * P:i * P + P], lambda i: xn[:, i, :], ident[:, :], S["wide_full"])

            def qk(st):
                u = wide(st, "qk")
                pe.wait_ge(wide_free[st.wide("xT")[1]], st.wide_before("xT") + 1)
                pe.matmul(u[:, 0, :], wq[:, :], xnT[:, 1:1 + SEQ], start=True, stop=True)
                pe.matmul(u[:, 1, :], wk[:, :], xnT[:, 1:1 + SEQ], start=True, stop=True).then_inc(S["wide_full"], 1)

            def values(st):
                u = wide(st, "v")
                for n in range(2):
                    for i in range(NT):
                        last = pe.matmul(u[:, n, i * P:i * P + P], xnT[:, 1 - n + i * P:1 - n + i * P + P], wv[:, :],
                                         start=True, stop=True)
                last.then_inc(S["wide_full"], 1)

            def o_transpose(st):
                u = wide(st, "oT")
                pe.wait_ge(S["o_ready"], st.at(NGRP * (st.c + 1), NGRP))
                transposes(lambda i: u[:, 0, i * P:i * P + P], lambda i: o_tok[:, i, :], ident[:, :], S["wide_full"])

            def o_proj(st):
                u = wide(st, "oproj")
                pe.wait_ge(wide_free[st.wide("oT")[1]], st.wide_before("oT") + 1)
                for i in range(NT):
                    last = pe.matmul(u[:, 0, i * P:i * P + P], oT[:, i * P:i * P + P], wo[:, :], start=True, stop=True)
                last.then_inc(S["wide_full"], 1)

            def e_sums(st):
                m = misc(st, "e_sums")
                pe.wait_ge(S["e_ready"], st.at(2 * (st.a + 1), 2))
                pe.matmul(m[0:32, :], head_sum[:, :], e0[:, :], start=True, stop=True)
                pe.matmul(m[32:64, :], head_sum[:, :], e1[:, :], start=True, stop=True).then_inc(S["misc_full"], 1)

            def s_tok_transpose(st):
                m = misc(st, "s_tok")
                pe.sem_inc(passed["pe"], 1)
                transposes(lambda i: m[:, i * 64:i * 64 + 64], lambda i: s_rows[:, i * P:i * P + P],
                           ident[0:64, 0:64], S["misc_full"])

            def m_transpose(st, s, half):
                m = misc(st, f"m{half}")[:, :].bitcast(F16)
                pe.wait_ge(S["m16_ready"], st.at(2 * s + half + 1, 2))
                transposes(lambda i: m[0:H // 2, i * P:i * P + P], lambda i: m16[:, i, half * 8:half * 8 + 8],
                           ident16[:, :], S["misc_full"])

            def av_transpose(st, s, g):
                m = misc(st, f"av{g}")
                pe.wait_ge(S["av_copied"], st.at(NGRP * s + g + 1, NGRP))
                transposes(lambda i: m[:, i * P:i * P + P], lambda i: av_s[g % 2][:, i * P:i * P + P],
                           ident[:, :], S["misc_full"])

            def xn2_transpose(st):
                m = misc(st, "xn2")
                pe.wait_ge(S["xn2_ready"], st.at(st.c + 1, 1))
                transposes(lambda i: m[:, i * P:i * P + P], lambda i: xn2[:, i, :], ident[:, :], S["misc_full"])

            def logits(st):
                m = misc(st, "logits")
                for i in range(NT):
                    last = pe.matmul(m[:, i * NE:i * NE + NE], xn2T[:, i * P:i * P + P], rwT[:, :],
                                     start=True, stop=True)
                last.then_inc(S["misc_full"], 1)

            def step(st):
                uses = {"av2": lambda: av_transpose(st, st.c, 2), "e_sums": lambda: e_sums(st),
                        "m1": lambda: m_transpose(st, st.b, 1), "s_tok": lambda: s_tok_transpose(st),
                        "av3": lambda: av_transpose(st, st.c, 3), "v": lambda: values(st),
                        "oT": lambda: o_transpose(st), "xT": lambda: x_transpose(st), "oproj": lambda: o_proj(st),
                        "qk": lambda: qk(st), "av0": lambda: av_transpose(st, st.b, 0),
                        "m0": lambda: m_transpose(st, st.a, 0), "av1": lambda: av_transpose(st, st.b, 1),
                        "xn2": lambda: xn2_transpose(st), "logits": lambda: logits(st)}
                here = {"F": st.F, "A": st.A, "B": st.B, "C": st.C}
                for slot in range(SLOTS):
                    pr, n = slot // (2 * NT), slot % (2 * NT)
                    if st.B:
                        exp_unit(st, pr, n)
                    for what, use in uses.items():
                        if AT[what] == slot and here[STAGE[what]]:
                            use()
                    if n % 4 == 1:
                        kt = pr % 2 * 2 + n // 4
                        if pr >= 2 and st.B:
                            av_part(st, st.b, pr // 2 - 1, kt)
                        if pr < 2 and st.C:
                            av_part(st, st.c, NGRP - 1, kt)
                    if st.A and n % 2 == 1:
                        s_unit(st, slot // 2)

            pe.wait_ge(S["const_ready"], N_CONST)
            pe.matmul(ps_av[:, 0:P], bias_v[:, :], wo[:, :], start=True, stop=True).then_inc(S["bias_full"], 1)
            pe.wait_ge(S["bias_ready"], 1)
            steps(pe, step)

            def gate_transpose(f, ahead):
                pe.wait_ge(S["chosen_ready"], f.at(ahead + 1, 1))
                need(pe, S["f_tok_ready"], f.at(ahead - 1, 1))
                pe.sem_inc(passed["pe"], 1)
                m = ps_misc[:, :].bitcast(BF16)
                for i in range(NT):
                    last = pe.transpose(m[0:64, i * P:i * P + P], gate3[:, i, :], identb[:, :])
                last.then_inc(S["gateT_full"], 1)

            def first(f, i):
                kind, k = UNITS[i]
                n = len(UNITS)
                if i == 0:
                    pe.wait_ge(S["xe_split"], f.at(1, 1))

                def product(out, w):
                    for j, (ws, xs) in enumerate(((w_high, xe_high), (w_high, xe_low), (w_low, xe_high))):
                        last = pe.matmul(out, ws[:, w, :].bitcast(F32R), xs[f.s0 % 2][:, :].bitcast(F32R),
                                         start=(j == 0), stop=(j == 2))
                    return last

                if kind == "c":
                    other = UNITS.index(("c", 1 - k)) + 1
                    need(pe, S["hidden_ready"], f.at(other if k else other - n, n))
                    product(ps_wide[1][:, 0, :], k)
                    product(ps_wide[1][:, 1, :], NC + k).then_inc(S["front_full"], 1)
                else:
                    before = EXPERT_POS[k - 2] + 1
                    need(pe, S["hidden_ready"], f.at(before if k >= 2 else before - n, n))
                    if k == 0:
                        pe.wait_ge(S["gateT_ready"], f.at(1, 1))
                    pe.matmul(ps_wide[0][:, k % 2, :], sel_e[:, k, :], gateT[:, :], start=True, stop=True)
                    product(ps_exp[k % 2][:, :], 2 * NC + k).then_inc(S["front_full"], 1)

            def second(f, i):
                kind, k = UNITS[i]
                n = len(UNITS)
                pe.wait_ge(S["low_ready"], f.at(i + 1, n))
                if i == 0 and f.s0 == 0:
                    pe.wait_ge(S["w_split"], 2)
                if i == 0:
                    need(pe, S["fT_ready"], f.at(0, 1))
                w, hd = k if kind == "c" else NC + k, hid(f, i)
                for j, (ws, hs) in enumerate(((w2_high, hidden_high), (w2_low, hidden_high), (w2_high, hidden_low))):
                    last = pe.matmul(ps_av[:, :], ws[:, w, :].bitcast(F32R), hs[hd][:, :].bitcast(F32R),
                                     start=(i % n == 0 and j == 0), stop=(i % n == n - 1 and j == 2))
                last.then_inc(S["second_done"], 1)

            def end_transpose(f, s):
                pe.wait_ge(S["fT_ready"], f.at(s + 1, 1))
                pe.wait_ge(S["gateT_ready"], f.at(min(s + 2, 1), 1))
                for i in range(NT):
                    last = pe.transpose(ps_misc[:, i * P:i * P + P], fT[:, i * P:i * P + P], ident[:, :])
                last.then_inc(S["f_tok_full"], 1)

            def ffn(f):
                n = len(UNITS)
                if f.s0 == 0:
                    pe.wait_ge(S["w_split"], 1)
                    pe.wait_ge(S["ffn_const"], 7)
                    pe.wait_ge(S["misc_free"], Step(NSEQ + 2).misc("logits") + 1)
                    gate_transpose(f, 0)
                for i in range(n):
                    first(f, i)
                    if i == LAG and f.s0 > 0:
                        end_transpose(f, -1)
                    if i == 0 and f.s0 > 0:
                        gate_transpose(f, 0)
                    if i >= LAG or f.s0 > 0:
                        second(f, i - LAG)

            ffn_steps(pe, ffn)
            for i in range(len(UNITS) - LAG, len(UNITS)):
                second(Ffn(NSEQ - 1), i)
            end_transpose(Ffn(NSEQ - 1), 0)


_INS = ["L0_attn_x", "L0_attn_W_q", "L0_attn_b_q", "L0_attn_W_k", "L0_attn_b_k", "L0_attn_W_v", "L0_attn_b_v",
        "L0_attn_W_o", "L0_attn_b_o", "L0_attn_rel_k_table", "L0_attn_rel_v_table", "L0_ffn_router_w",
        "L0_ffn_router_bias", "L0_ffn_sw1", "L0_ffn_sw3", "L0_ffn_sw2", "L0_ffn_ew1", "L0_ffn_ew2"]


def kernel(**inputs):
    import concourse.bacc as bacc
    from concourse.bass_utils import run_bass_kernel_spmd

    nc = bacc.Bacc("TRN2", target_bir_lowering=False, num_devices=1)
    arrays, args = {}, []
    for name in _INS:
        a = np.ascontiguousarray(inputs[name])
        arrays[name] = a
        args.append(nc.dram_tensor(name, a.shape, mybir.dt.from_np(a.dtype), kind="ExternalInput").ap())
    args.append(nc.dram_tensor("out", (NSEQ, SEQ, P), F32, kind="ExternalOutput").ap())
    block_kernel(nc, *args)
    r = run_bass_kernel_spmd(nc, [arrays], core_ids=[0])
    return r.results[0]["out"]
```
